# Optimizing a Trainium2 kernel written in Bass

```python
import numpy as np
import jax
import jax.numpy as jnp

def _softmax(x, axis=-1):
    return jax.nn.softmax(x, axis=axis)

def _gelu(x):
    return jax.nn.gelu(x, approximate=True)

def _silu(x):
    return jax.nn.silu(x)

def _sigmoid(x):
    return jax.nn.sigmoid(x)

def _layernorm(x, axis=-1, eps=1e-05):
    m = jnp.mean(x, axis=axis, keepdims=True)
    v = jnp.var(x, axis=axis, keepdims=True)
    return (x - m) / jnp.sqrt(v + eps)

def _scatter_add(tgt, idx, src, axis=0):
    return tgt.at[idx].add(src)

def _segment_sum(src, seg, n):
    return jax.ops.segment_sum(src, seg, n)
kernel_name = 'mk_audio_tower_d1_tok_audfeat768_r4_543824'

def setup_inputs(seed: int=0):
    np.random.seed(seed)
    _w = jnp.asarray

    def _rec_inputs():
        import jax
        import jax.numpy as jnp
        _rk = jax.random.key(seed)
        x = -0.000183583 + 0.999963 * jax.random.normal(jax.random.fold_in(_rk, 1), (4, 750, 192), jnp.float32)
        return x
    x = _rec_inputs()

    def _L0_tok_setup():
        import jax, jax.numpy as jnp
        import numpy as np
        KEEP_RATIO = 0.7
        key = jax.random.key(seed)
        kx, kw = jax.random.split(key)
        B, N, D = (32, 1024, 192)
        x = jax.random.normal(kx, (B, N, D), dtype=jnp.float32)
        w = jax.random.normal(kw, (D, 1), dtype=jnp.float32) * (1.0 / np.sqrt(D))
        b = jnp.zeros((1,), dtype=jnp.float32)
        return {'x': x, 'w': w, 'b': b}
    _L0_tok_all = _L0_tok_setup()
    _L0_tok_in = {k: v for k, v in _L0_tok_all.items() if k in ('w', 'b')}
    del _L0_tok_all

    def _L0_attn_setup():
        import jax, jax.numpy as jnp
        import numpy as np
        H = 12

        def _alibi_bias(num_heads, n, dtype):
            ratio = 2.0 ** (-8.0 / num_heads)
            slopes = ratio ** jnp.arange(1, num_heads + 1, dtype=jnp.float32)
            pos = jnp.arange(n)
            rel = jnp.abs(pos[None, :] - pos[:, None]).astype(jnp.float32)
            return (-slopes[:, None, None] * rel[None]).astype(dtype)
        key = jax.random.key(seed)
        ks = jax.random.split(key, 5)
        B, N, C = (16, 256, 192)
        s = 0.02
        return {'x': jax.random.normal(ks[0], (B, N, C), jnp.float32), 'w_qkv': jax.random.normal(ks[1], (3 * C, C), jnp.float32) * s, 'b_qkv': jax.random.normal(ks[2], (3 * C,), jnp.float32) * s, 'w_proj': jax.random.normal(ks[3], (C, C), jnp.float32) * s, 'b_proj': jax.random.normal(ks[4], (C,), jnp.float32) * s}
    _L0_attn_all = _L0_attn_setup()
    _L0_attn_in = {k: v for k, v in _L0_attn_all.items() if k in ('w_qkv', 'b_qkv', 'w_proj', 'b_proj')}
    del _L0_attn_all

    def _L0_ffn_setup():
        import jax, jax.numpy as jnp
        import numpy as np
        HID = 192
        NQ = 12
        NKV = 3
        HD = 64
        REP = NQ // NKV
        E = 16
        TOPK = 2
        FF = 384
        EPS = 1e-06
        THETA = 10000.0

        def rms_norm(x, w):
            return x / jnp.sqrt(jnp.mean(x * x, axis=-1, keepdims=True) + EPS) * w

        def rope_tables(seq_len):
            inv = 1.0 / THETA ** (jnp.arange(0, HD, 2, dtype=jnp.float32) / HD)
            f = jnp.arange(seq_len, dtype=jnp.float32)[:, None] * inv[None, :]
            return (jnp.cos(f), jnp.sin(f))

        def apply_rope(t, cos, sin):
            B, S, H, _ = t.shape
            tr = t.reshape(B, S, H, HD // 2, 2)
            c = cos[None, :, None, :]
            s = sin[None, :, None, :]
            r0 = tr[..., 0] * c - tr[..., 1] * s
            r1 = tr[..., 0] * s + tr[..., 1] * c
            return jnp.stack([r0, r1], axis=-1).reshape(B, S, H, HD)

        def attention(x, w_qkv, w_out):
            B, S, _ = x.shape
            qkv = x @ w_qkv
            q, k, v = jnp.split(qkv, [NQ * HD, (NQ + NKV) * HD], axis=-1)
            q = q.reshape(B, S, NQ, HD)
            k = k.reshape(B, S, NKV, HD)
            v = v.reshape(B, S, NKV, HD)
            cos, sin = rope_tables(S)
            q = apply_rope(q, cos, sin)
            k = apply_rope(k, cos, sin)
            k = jnp.repeat(k, REP, axis=2)
            v = jnp.repeat(v, REP, axis=2)
            q = q.transpose(0, 2, 1, 3)
            k = k.transpose(0, 2, 1, 3)
            v = v.transpose(0, 2, 1, 3)
            scores = jnp.einsum('bhqd,bhkd->bhqk', q, k) / jnp.sqrt(jnp.float32(HD))
            causal = jnp.tril(jnp.ones((S, S), dtype=bool))
            scores = jnp.where(causal[None, None], scores, jnp.finfo(scores.dtype).min)
            attn = jax.nn.softmax(scores, axis=-1)
            out = jnp.einsum('bhqk,bhkd->bhqd', attn, v)
            out = out.transpose(0, 2, 1, 3).reshape(B, S, NQ * HD)
            return out @ w_out

        def moe_ffn(x2d, w_router, w_gate_up, w_down):
            logits = x2d @ w_router
            probs = jax.nn.softmax(logits, axis=-1)
            vals, idx = jax.lax.top_k(probs, TOPK)
            vals = vals / jnp.sum(vals, axis=-1, keepdims=True)
            combine = jnp.sum(jax.nn.one_hot(idx, E, dtype=x2d.dtype) * vals[..., None], axis=1)
            out = jnp.zeros_like(x2d)
            for e in range(E):
                gu = x2d @ w_gate_up[e]
                gate, up = jnp.split(gu, 2, axis=-1)
                h = jax.nn.silu(gate) * up
                out = out + combine[:, e:e + 1] * (h @ w_down[e])
            return out
        key = jax.random.key(seed)
        ks = jax.random.split(key, 6)
        B, S = (1, 512)
        return {'x': jax.random.normal(ks[0], (B, S, HID), dtype=jnp.float32), 'norm1_w': jnp.ones((HID,), dtype=jnp.float32), 'w_qkv': jax.random.normal(ks[1], (HID, (NQ + 2 * NKV) * HD), dtype=jnp.float32) * 0.02, 'w_out': jax.random.normal(ks[2], (NQ * HD, HID), dtype=jnp.float32) * 0.02, 'norm2_w': jnp.ones((HID,), dtype=jnp.float32), 'w_router': jax.random.normal(ks[3], (HID, E), dtype=jnp.float32) * 0.02, 'w_gate_up': jax.random.normal(ks[4], (E, HID, 2 * FF), dtype=jnp.float32) * 0.02, 'w_down': jax.random.normal(ks[5], (E, FF, HID), dtype=jnp.float32) * 0.02}
    _L0_ffn_all = _L0_ffn_setup()
    _L0_ffn_in = {k: v for k, v in _L0_ffn_all.items() if k in ('norm1_w', 'w_qkv', 'w_out', 'norm2_w', 'w_router', 'w_gate_up', 'w_down')}
    del _L0_ffn_all
    return {'x': x, 'L0_tok_w': _L0_tok_in['w'], 'L0_tok_b': _L0_tok_in['b'], 'L0_attn_w_qkv': _L0_attn_in['w_qkv'], 'L0_attn_b_qkv': _L0_attn_in['b_qkv'], 'L0_attn_w_proj': _L0_attn_in['w_proj'], 'L0_attn_b_proj': _L0_attn_in['b_proj'], 'L0_ffn_norm1_w': _L0_ffn_in['norm1_w'], 'L0_ffn_w_qkv': _L0_ffn_in['w_qkv'], 'L0_ffn_w_out': _L0_ffn_in['w_out'], 'L0_ffn_norm2_w': _L0_ffn_in['norm2_w'], 'L0_ffn_w_router': _L0_ffn_in['w_router'], 'L0_ffn_w_gate_up': _L0_ffn_in['w_gate_up'], 'L0_ffn_w_down': _L0_ffn_in['w_down']}

def reference(x, L0_tok_w, L0_tok_b, L0_attn_w_qkv, L0_attn_b_qkv, L0_attn_w_proj, L0_attn_b_proj, L0_ffn_norm1_w, L0_ffn_w_qkv, L0_ffn_w_out, L0_ffn_norm2_w, L0_ffn_w_router, L0_ffn_w_gate_up, L0_ffn_w_down):
    import jax
    import jax.numpy as jnp

    def _L0_tok_ref(x, w, b):
        import jax, jax.numpy as jnp
        import numpy as np
        KEEP_RATIO = 0.7
        scores = jnp.einsum('bnd,do->bn', x, w) + b[0]
        N = x.shape[1]
        k = int(round(N * KEEP_RATIO))
        _, idx = jax.lax.top_k(scores, k)
        return jnp.take_along_axis(x, idx[:, :, None], axis=1)

    def _L0_attn_ref(x, w_qkv, b_qkv, w_proj, b_proj):
        import jax, jax.numpy as jnp
        import numpy as np
        H = 12

        def _alibi_bias(num_heads, n, dtype):
            ratio = 2.0 ** (-8.0 / num_heads)
            slopes = ratio ** jnp.arange(1, num_heads + 1, dtype=jnp.float32)
            pos = jnp.arange(n)
            rel = jnp.abs(pos[None, :] - pos[:, None]).astype(jnp.float32)
            return (-slopes[:, None, None] * rel[None]).astype(dtype)
        B, N, C = x.shape
        D = C // H
        scale = D ** (-0.5)
        qkv = x @ w_qkv.T + b_qkv
        qkv = qkv.reshape(B, N, 3, H, D)
        q = qkv[:, :, 0].transpose(0, 2, 1, 3)
        k = qkv[:, :, 1].transpose(0, 2, 1, 3)
        v = qkv[:, :, 2].transpose(0, 2, 1, 3)
        bias = _alibi_bias(H, N, x.dtype)
        scores = jnp.einsum('bhnd,bhmd->bhnm', q, k) * scale + bias[None]
        attn = jax.nn.softmax(scores, axis=-1)
        out = jnp.einsum('bhnm,bhmd->bhnd', attn, v)
        out = out.transpose(0, 2, 1, 3).reshape(B, N, C)
        return out @ w_proj.T + b_proj

    def _L0_ffn_ref(x, norm1_w, w_qkv, w_out, norm2_w, w_router, w_gate_up, w_down):
        import jax, jax.numpy as jnp
        import numpy as np
        HID = 192
        NQ = 12
        NKV = 3
        HD = 64
        REP = NQ // NKV
        E = 16
        TOPK = 2
        FF = 384
        EPS = 1e-06
        THETA = 10000.0

        def rms_norm(x, w):
            return x / jnp.sqrt(jnp.mean(x * x, axis=-1, keepdims=True) + EPS) * w

        def rope_tables(seq_len):
            inv = 1.0 / THETA ** (jnp.arange(0, HD, 2, dtype=jnp.float32) / HD)
            f = jnp.arange(seq_len, dtype=jnp.float32)[:, None] * inv[None, :]
            return (jnp.cos(f), jnp.sin(f))

        def apply_rope(t, cos, sin):
            B, S, H, _ = t.shape
            tr = t.reshape(B, S, H, HD // 2, 2)
            c = cos[None, :, None, :]
            s = sin[None, :, None, :]
            r0 = tr[..., 0] * c - tr[..., 1] * s
            r1 = tr[..., 0] * s + tr[..., 1] * c
            return jnp.stack([r0, r1], axis=-1).reshape(B, S, H, HD)

        def attention(x, w_qkv, w_out):
            B, S, _ = x.shape
            qkv = x @ w_qkv
            q, k, v = jnp.split(qkv, [NQ * HD, (NQ + NKV) * HD], axis=-1)
            q = q.reshape(B, S, NQ, HD)
            k = k.reshape(B, S, NKV, HD)
            v = v.reshape(B, S, NKV, HD)
            cos, sin = rope_tables(S)
            q = apply_rope(q, cos, sin)
            k = apply_rope(k, cos, sin)
            k = jnp.repeat(k, REP, axis=2)
            v = jnp.repeat(v, REP, axis=2)
            q = q.transpose(0, 2, 1, 3)
            k = k.transpose(0, 2, 1, 3)
            v = v.transpose(0, 2, 1, 3)
            scores = jnp.einsum('bhqd,bhkd->bhqk', q, k) / jnp.sqrt(jnp.float32(HD))
            causal = jnp.tril(jnp.ones((S, S), dtype=bool))
            scores = jnp.where(causal[None, None], scores, jnp.finfo(scores.dtype).min)
            attn = jax.nn.softmax(scores, axis=-1)
            out = jnp.einsum('bhqk,bhkd->bhqd', attn, v)
            out = out.transpose(0, 2, 1, 3).reshape(B, S, NQ * HD)
            return out @ w_out

        def moe_ffn(x2d, w_router, w_gate_up, w_down):
            logits = x2d @ w_router
            probs = jax.nn.softmax(logits, axis=-1)
            vals, idx = jax.lax.top_k(probs, TOPK)
            vals = vals / jnp.sum(vals, axis=-1, keepdims=True)
            combine = jnp.sum(jax.nn.one_hot(idx, E, dtype=x2d.dtype) * vals[..., None], axis=1)
            out = jnp.zeros_like(x2d)
            for e in range(E):
                gu = x2d @ w_gate_up[e]
                gate, up = jnp.split(gu, 2, axis=-1)
                h = jax.nn.silu(gate) * up
                out = out + combine[:, e:e + 1] * (h @ w_down[e])
            return out
        B, S, _ = x.shape
        h = x + attention(rms_norm(x, norm1_w), w_qkv, w_out)
        moe_in = rms_norm(h, norm2_w).reshape(B * S, HID)
        out = h + moe_ffn(moe_in, w_router, w_gate_up, w_down).reshape(B, S, HID)
        return out
    h = _L0_tok_ref(x, L0_tok_w, L0_tok_b)
    h = h + _L0_attn_ref(_layernorm(h, axis=-1), L0_attn_w_qkv, L0_attn_b_qkv, L0_attn_w_proj, L0_attn_b_proj)
    h = h + _L0_ffn_ref(_layernorm(h, axis=-1), L0_ffn_norm1_w, L0_ffn_w_qkv, L0_ffn_w_out, L0_ffn_norm2_w, L0_ffn_w_router, L0_ffn_w_gate_up, L0_ffn_w_down)
    return h

_drawn_inputs = setup_inputs


def setup_inputs(seed=0):
    import zlib

    import numpy as np

    out = dict(_drawn_inputs(seed))
    spreads = {'L0_ffn_norm1_w': (1.0, 0.6), 'L0_ffn_norm2_w': (1.0, 0.6)}
    factors = {'L0_attn_w_qkv': 3.668,
     'L0_attn_b_qkv': 8.0,
     'L0_attn_w_proj': 3.423,
     'L0_attn_b_proj': 2.927,
     'L0_ffn_w_qkv': 4.958,
     'L0_ffn_w_out': 4.99,
     'L0_ffn_w_router': 8.0,
     'L0_ffn_w_gate_up': 8.0,
     'L0_ffn_w_down': 8.0}
    for name, (base, spread) in spreads.items():
        noise = np.random.default_rng([zlib.crc32(name.encode()), seed]).standard_normal(out[name].shape)
        drawn = base * np.exp(spread * noise) if base else spread * noise
        out[name] = jnp.asarray(drawn.astype(out[name].dtype))
    for name, factor in factors.items():
        out[name] = (out[name] * factor).astype(out[name].dtype)
    return out
```

```python
from contextlib import ExitStack

import numpy as np
import concourse.bass as bass
from concourse import mybir

ALU = mybir.AluOpType
ACT = mybir.ActivationFunctionType
AX = mybir.AxisListType
F32 = mybir.dt.float32
BF16 = mybir.dt.bfloat16
I32 = mybir.dt.int32
U32 = mybir.dt.uint32

B, NIN, C = 4, 750, 192
KEEP = int(round(NIN * 0.7))
P_IN = 125
T_IN = NIN // P_IN
P = 105
T = KEEP // P
CH = 175
NCH = KEEP // CH
CS = 256
KC = 96
NK = C // KC

H1, D1 = 12, 16
PARTS = 3
HI, MID, LO = range(PARTS)
Q_PART = [HI, HI, HI, MID, MID, LO]
K_PART = [HI, MID, LO, HI, MID, HI]
NPROD = len(Q_PART)
R_PROD = NPROD * D1
R_DIST = 4 * T
R_MAX = R_PROD + R_DIST
R_ALL = R_MAX + PARTS
GH = 4
NG = H1 // GH
VW = 32

H2, HKV, D2 = 12, 3, 64
HALF = D2 // 2
NPAIR = H2 // 2
PK = 128
THETA = 10000.0

E, TOPK, FF = 16, 2, 384
NTOK = B * KEEP
NT = B * T
ST = 128
NST = (NTOK * TOPK + E * (ST - 1)) // ST
NSLOT = NST * ST
MF = FF // ST
WMAX = -(-NTOK // ST)

LN_EPS, RMS_EPS = 1e-5, 1e-6
SLOPES = [float(np.float32(2.0 ** (-8.0 / H1)) ** np.float32(h + 1)) for h in range(H1)]


def constants():
    c = {}
    c["ident"] = np.eye(128, dtype=np.float32)
    n = np.arange(KEEP)
    big, rest, tile = n // 4 * 4, n % 4, n // P
    q, k = np.zeros((R_DIST, KEEP), np.float32), np.zeros((R_DIST, KEEP), np.float32)
    for i in range(T):
        s = np.sign(tile - i)
        q[4 * i:4 * i + 4] = np.stack([big, rest, n >= 0, n >= 0]) * (tile == i)
        k[4 * i:4 * i + 4] = np.stack([s, s, -s * big, -s * rest])
    bf16 = mybir.dt.np(BF16)
    c["dist_q"] = q.astype(bf16)
    c["dist_k"] = np.concatenate([k, np.ones((PARTS, KEEP), np.float32)]).astype(bf16)
    m = np.arange(P)
    c["near"] = -np.abs(m[:, None] - m[None, :]).astype(bf16)
    c["future"] = np.where(m[None, :] > m[:, None], -1e30, 0.0).astype(bf16)
    t = np.arange(P_IN)
    c["earlier"] = (t[None, :] < t[:, None]).astype(np.float32)
    f = np.repeat(np.float32(D1 ** -0.5) / np.asarray(SLOPES, np.float32), D1)
    c["q_factor"] = np.ascontiguousarray(f.reshape(NK, KC).T.astype(np.float32))
    inv = (1.0 / np.float32(THETA) ** (np.arange(0, D2, 2, dtype=np.float32) / np.float32(D2)))
    a = np.arange(KEEP, dtype=np.float32)[None, :] * inv.astype(np.float32)[:, None]
    cos, sin = np.cos(a).astype(np.float32), np.sin(a).astype(np.float32)
    c["rope"] = np.ascontiguousarray(
        np.stack([np.concatenate([cos] * 4), np.concatenate([-sin, sin] * 2)], axis=1))
    c["before"] = (m[:, None] < m[None, :]).astype(np.float32)
    marks = np.ones((E, NT), np.float32)
    marks[:, 0] = 0
    marks1 = np.ones(E, np.float32)
    c["counts"] = np.concatenate([
        np.arange(E), np.arange(WMAX) * ST, np.arange(NST), marks.ravel(), marks1]).astype(np.float32)[None]
    return c


N_CNT = E + WMAX + NST + E * NT + E


def audio_tower(nc, a, out):
    es = ExitStack()
    with es:
        def sb(name, shape, dt=F32):
            return es.enter_context(nc.sbuf_tensor(name, shape, dt))

        def dram(name, shape, dt=F32):
            return nc.dram_tensor(name, shape, dt, kind="Internal").ap()

        score_d = dram("score_d", [B * T_IN, P_IN])
        kept_d = dram("kept_d", [B * NIN, C])
        parts_d = dram("parts_d", [2, 2, PARTS, C, KEEP], BF16)
        moe_in_d = dram("moe_in_d", [NT, P, C])
        res_d = dram("res_d", [NT, P, C])
        logit_d = dram("logit_d", [NT, P, E])
        slot_x_d = dram("slot_x_d", [NSLOT, C])
        slot_y_d = dram("slot_y_d", [NSLOT, C])

        region = [es.enter_context(nc.psum_tensor(f"region{i}", [128, 1024], F32)) for i in range(4)]

        ident = sb("ident", [128, 128])
        identb = sb("identb", [128, 128], BF16)

        sort_tokens(nc, a, region, ident, identb, score_d, kept_d, slot_x_d)
        tower(nc, a, region, ident, identb, kept_d, parts_d, moe_in_d, res_d, logit_d)
        experts(nc, a, region, ident, identb, moe_in_d, res_d, logit_d, slot_x_d, slot_y_d, out)


def chain(eng, sem):
    count = [0]

    def link(ins, wait=True):
        count[0] += 1
        ins.then_inc(sem, 1)
        if wait:
            eng.wait_ge(sem, count[0])
        return count[0]
    return link


def chunks(region, rows=128):
    return region[0:rows, :].rearrange("p (c x) -> p c x", x=CS)[:, 0:NCH, 0:CH]


def sort_tokens(nc, a, region, ident, identb, score_d, kept_d, slot_x_d):
    es = ExitStack()
    with es:
        def sb(name, shape, dt=F32):
            return es.enter_context(nc.sbuf_tensor(name, shape, dt))

        def sem(name):
            return es.enter_context(nc.semaphore(name))

        NB = B * T_IN
        x_in = sb("x_in", [P_IN, NB, C])
        tok_w = sb("tok_w", [P_IN, C])
        tok_b = sb("tok_b", [P_IN, 1])
        earlier = sb("earlier", [P_IN, P_IN])
        prod = sb("prod", [P_IN, C])
        score = sb("score", [P_IN, NB])
        score_t = sb("score_t", [NB, P_IN])
        all_scores = sb("all_scores", [P_IN, B, NIN])
        hit = sb("hit", [P_IN, NIN])
        cnt = sb("cnt", [P_IN, NB, 3])
        rank = sb("rank", [P_IN, NB])
        rank_i = sb("rank_i", [P_IN, NB], I32)
        zeros = sb("zeros", [ST, NST // 4 * C])

        consts_in = sem("so_consts_in")
        x_loaded = [sem(f"so_x_loaded{b}") for b in range(B)]
        dve_self = sem("so_dve_self")
        identb_ready = sem("so_identb_ready")
        scores_ready = sem("so_scores_ready")
        scores_turned = sem("so_scores_turned")
        scores_row = sem("so_scores_row")
        scores_out = sem("so_scores_out")
        scores_back = [sem(f"so_scores_back{b}") for b in range(B)]
        ranks_ready = sem("so_ranks_ready")
        scattered = sem("so_scattered")
        zeros_ready = sem("so_zeros_ready")
        zeroed = sem("so_zeroed")

        with nc.Block() as block:
            @block.sync
            def _(sp):
                for b in range(B):
                    sp.dma_start(x_in[:, b * T_IN:(b + 1) * T_IN, :],
                                 a["x"][b].rearrange("(t p) c -> p t c", p=P_IN)).then_inc(x_loaded[b], 16)
                sp.wait_ge(scores_row, 1)
                sp.dma_start(score_d, score_t[:, :]).then_inc(scores_out, 16)
                sp.wait_ge(scores_out, 16)
                for b in range(B):
                    src = score_d[b * T_IN:(b + 1) * T_IN, :].rearrange("(a t) p -> a (t p)", a=1)
                    sp.dma_start(all_scores[:, b, :], src.broadcast_to([P_IN, NIN])).then_inc(scores_back[b], 16)

            @block.scalar
            def _(act):
                act.dma_start(tok_w[:, :], a["tok_w"].broadcast_to([P_IN, C])).then_inc(consts_in, 16)
                act.dma_start(tok_b[:, :], a["tok_b"].broadcast_to([P_IN, 1])).then_inc(consts_in, 16)
                act.dma_start(ident[:, :], a["ident"]).then_inc(consts_in, 16)
                act.dma_start(earlier[:, :], a["earlier"]).then_inc(consts_in, 16)
                act.wait_ge(zeros_ready, 1)
                v = slot_x_d.rearrange("(n p r) c -> n p (r c)", n=4, p=ST)
                for n in range(4):
                    act.dma_start(v[n], zeros[:, :]).then_inc(zeroed, 16)
                act.wait_ge(zeroed, 64)

            @block.vector
            def _(dve):
                link = chain(dve, dve_self)
                dve.wait_ge(consts_in, 64)
                nc.vector.tensor_copy(identb[:, :], ident[:, :]).then_inc(identb_ready, 1)
                dve.wait_ge(identb_ready, 1)
                for b in range(B):
                    dve.wait_ge(x_loaded[b], 16)
                    for t in range(b * T_IN, (b + 1) * T_IN):
                        link(nc.vector.tensor_tensor_reduce(prod[:, :], x_in[:, t, :], tok_w[:, :], 1.0, 0.0,
                                                            ALU.mult, ALU.add, score[:, t:t + 1]))
                link(nc.vector.tensor_scalar(score[:, :], score[:, :], tok_b[:, 0:1], None, ALU.add))
                nc.vector.engine_nop().then_inc(scores_ready, 1)
                dve.wait_ge(scores_turned, 1)
                nc.vector.tensor_copy(score_t[:, :], region[0][0:NB, 0:P_IN]).then_inc(scores_row, 1)
                for b in range(B):
                    dve.wait_ge(scores_back[b], 16)
                    for t in range(T_IN):
                        n = b * T_IN + t
                        own, lo, hi = score[:, n:n + 1], t * P_IN, (t + 1) * P_IN
                        if t:
                            link(nc.vector.tensor_scalar(hit[:, 0:lo], all_scores[:, b, 0:lo], own, 0.0,
                                                         ALU.is_ge, ALU.add, accum_out=cnt[:, n, 0:1]))
                        else:
                            link(nc.vector.memset(cnt[:, n, 0:1], 0.0))
                        link(nc.vector.tensor_scalar(hit[:, lo:NIN], all_scores[:, b, lo:NIN], own, 0.0,
                                                     ALU.is_gt, ALU.add, accum_out=cnt[:, n, 1:2]))
                        link(nc.vector.scalar_tensor_tensor(
                            out=hit[:, 0:P_IN], in0=all_scores[:, b, lo:hi], scalar=own, in1=earlier[:, :],
                            op0=ALU.is_equal, op1=ALU.mult, accum_out=cnt[:, n, 2:3]))
                    s = slice(b * T_IN, (b + 1) * T_IN)
                    link(nc.vector.tensor_reduce(rank[:, s], cnt[:, s, :], AX.X, ALU.add))
                    link(nc.vector.tensor_scalar(rank[:, s], rank[:, s], float(b * NIN), None, ALU.add))
                    nc.vector.tensor_copy(rank_i[:, s], rank[:, s]).then_inc(ranks_ready, 1)

            @block.tensor
            def _(pe):
                pe.wait_ge(scores_ready, 1)
                nc.tensor.transpose(region[0][0:NB, 0:P_IN], score[:, :], ident[0:P_IN, 0:P_IN])\
                    .then_inc(scores_turned, 1)

            @block.gpsimd
            def _(pool):
                nc.gpsimd.memset(zeros[:, :], 0.0).then_inc(zeros_ready, 1)
                for b in range(B):
                    pool.wait_ge(ranks_ready, b + 1)
                    for n in range(b * T_IN, (b + 1) * T_IN):
                        nc.gpsimd.indirect_dma_start(
                            kept_d, bass.IndirectOffsetOnAxis(ap=rank_i[:, n:n + 1], axis=0),
                            x_in[:, n, :], None).then_inc(scattered, 16)
                pool.wait_ge(scattered, 16 * NB)




def both(*kinds):
    return [(k, j) for k in kinds for j in range(2)]


def merged(x, y):
    out, n = [], 0
    for i, s in enumerate(x):
        out.append(s)
        while n * len(x) < (i + 1) * len(y):
            out.append(y[n])
            n += 1
    return out


def maxima(j):
    return [("row_max", j, h, i) for h in range(H1) for i in range(T)] + [("max_parts", j)]


def weights(j):
    out = []
    for g in range(NG):
        for k in range(T):
            out.append(("exp_sum", j, g, k))
            if g and k == 0:
                out.append(("group_end", j, g - 1))
    return out + [("group_end", j, NG - 1)]


def pairs(j):
    out = []
    for u in range(NPAIR):
        for x in range(2):
            for i in range(T):
                out.append(("causal", j, u, x, i))
                if u and x == 0 and i == 2:
                    out.append(("pair_end", j, u - 1))
    return out + [("pair_end", j, NPAIR - 1)]


ORDER = (
    both("norm1_stats", "norm1", "turn1", "qk_split", "v1") + maxima(0) + merged(weights(0), maxima(1))
    + weights(1) + both("heads_out", "norm2_stats", "norm2", "norm2_rms", "rms2", "turn2", "rotate", "v2")
    + pairs(0) + pairs(1) + both("out2", "rms3_stats", "rms3", "turn3", "route_logits")
)


def step_before(step, n):
    same = [s for s in ORDER if s[0] == step[0]]
    return same[same.index(step) - n]


def numbered(*kinds):
    steps = [s for s in ORDER if s[0] in kinds]
    return {s: n + 1 for n, s in enumerate(steps)}


def uses(order):
    count, place = [0] * 4, {}

    def use(key, r):
        count[r] += 1
        place[key] = (r, count[r])

    turn = 0
    for kind, j, *w in order:
        if kind in ("turn1", "turn2", "turn3", "turn_o"):
            use((kind, j, 0), 0)
            use((kind, j, 1), 1)
        elif kind == "qk_split":
            for m in range(2 * NK):
                use((kind, j, m), m % 4)
        elif kind in ("v1", "v2", "out2"):
            use((kind, j, 0), 2)
            use((kind, j, 1), 3)
        elif kind == "row_max":
            use((kind, j, *w), 0)
        elif kind == "max_parts":
            use((kind, j), 0)
        elif kind == "exp_sum":
            for hl in range(GH):
                use((kind, j, *w, hl), 1 + hl % 2)
            if w[1] == 0:
                use(("sum", j, w[0]), 3)
        elif kind == "heads_out":
            for t in range(T):
                use(("turn_n", j, t), t % 2)
            use(("turn_o", j, 0), 2)
            use(("turn_o", j, 1), 3)
            use(("proj1", j, 0), 0)
            use(("proj1", j, 1), 1)
        elif kind == "rotate":
            for m in range(NPAIR + HKV):
                use((kind, j, m), m % 4)
        elif kind == "causal":
            u, x, i = w
            use((kind, j, u, x, i), turn % 2)
            use(("turn_p", j, u, x, i), 2)
            turn += 1
        elif kind == "pair_end":
            use((kind, j, *w), 3)
        elif kind == "route_logits":
            use((kind, j), 2)
    return place, count


def tower(nc, a, region, ident, identb, kept_d, parts_d, moe_in_d, res_d, logit_d):
    es = ExitStack()
    with es:
        def sb(name, shape, dt=F32):
            return es.enter_context(nc.sbuf_tensor(name, shape, dt))

        def sem(name):
            s = es.enter_context(nc.semaphore("to_" + name))
            sems.append(s)
            return s

        sems = []
        place, _ = uses(ORDER)

        w_qkv1 = sb("w_qkv1", [KC, NK, 3 * C])
        w_proj1 = sb("w_proj1", [KC, NK, C])
        w_qkv2 = sb("w_qkv2", [KC, NK, (NPAIR + HKV) * 128 + HKV * D2])
        w_out2 = sb("w_out2", [128, NPAIR, C])
        w_router = sb("w_router", [KC, NK, E])
        b_qk1 = sb("b_qk1", [KC, 2 * NK])
        q_factor = sb("q_factor", [KC, NK])
        qb = sb("qb", [KC, NK])
        b_v1 = sb("b_v1", [P, C])
        b_proj1 = sb("b_proj1", [P, C])
        norm1 = sb("norm1", [KC, NK])
        norm2_row = sb("norm2_row", [P, C])
        near = sb("near", [P, P], BF16)
        future = sb("future", [P, P], BF16)
        rope = sb("rope", [128, 2, KEEP])
        neg_half = sb("neg_half", [P, T])

        hid = [sb(f"hid{j}", [P, T, C]) for j in range(2)]
        nrm = [sb(f"nrm{j}", [P, T, C]) for j in range(2)]
        tmp = [sb(f"tmp{j}", [P, T, C]) for j in range(2)]
        xT = [sb(f"xT{j}", [KC, NK, KEEP]) for j in range(2)]
        stats = [sb(f"stats{j}", [P, T, 6]) for j in range(2)]
        mv = [sb(f"mv{j}", [P, T, 2]) for j in range(2)]
        var = [sb(f"var{j}", [P, T]) for j in range(2)]
        rstd = [sb(f"rstd{j}", [P, T]) for j in range(2)]
        big = [sb(f"big{j}", [128, 2 * H1 * KEEP], BF16) for j in range(2)]
        Aq = [x[0:R_ALL, 0:H1 * KEEP].rearrange("p (h n) -> p h n", h=H1) for x in big]
        Ak = [x[0:R_ALL, H1 * KEEP:].rearrange("p (h n) -> p h n", h=H1) for x in big]
        q2 = [x[:, 0:H1 * KEEP].bitcast(F32).rearrange("p (u n) -> p u n", u=NPAIR) for x in big]
        k2 = [x[:, H1 * KEEP:].bitcast(F32).rearrange("p (g x n) -> p g x n", g=HKV, x=2) for x in big]
        vals = [sb(f"vals{j}", [P, T, H1, VW]) for j in range(2)]
        mx = [sb(f"mx{j}", [P, H1, T]) for j in range(2)]
        rowp = [sb(f"rowp{j}", [P, T, PARTS * H1], BF16) for j in range(2)]
        junk = sb("junk", [P, C])
        mtmp = sb("mtmp", [P, 2, H1, T])
        mrow = [sb(f"mrow{j}", [PARTS * H1, KEEP], BF16) for j in range(2)]
        v2 = [sb(f"v2{j}", [P, T, HKV * D2]) for j in range(2)]
        attn = [sb(f"attn{j}", [128, NPAIR, KEEP]) for j in range(2)]
        logit = [sb(f"logit{j}", [P, T, E]) for j in range(2)]
        qk32 = [sb(f"qk32_{i}", [128, KEEP]) for i in range(2)]
        rest = [sb(f"rest{i}", [128, KEEP]) for i in range(2)]
        part_room = sb("part_room", [128, 2 * PARTS * KEEP], BF16)
        parts = [part_room[0:KC, i * PARTS * KEEP:(i + 1) * PARTS * KEEP].rearrange("p (s n) -> p s n", s=PARTS)
                 for i in range(2)]
        pr = [part_room[0:P, i * 2 * KEEP:(i + 1) * 2 * KEEP].bitcast(F32) for i in range(3)]
        pt = [sb(f"pt{i}", [P, T, KEEP]) for i in range(3)]
        probs = [t[:, 0:GH, :] for t in pt[0:2]]
        recip = sb("recip", [P, T, H1])
        nm = [sb(f"nm{i}", [P, 1]) for i in range(4)]
        den = [sb(f"den{i}", [P, 1]) for i in range(4)]
        rden = [sb(f"rden{i}", [P, 1]) for i in range(4)]

        setup_in = es.enter_context(nc.semaphore("to_setup_in"))
        setup_dve = es.enter_context(nc.semaphore("to_setup_dve"))

        with nc.Block() as block:
            loads = [(w_qkv1, "w_qkv1"), (w_proj1, "w_proj1"), (w_qkv2, "w_qkv2"), (w_router, "w_router")]

            @block.sync
            def _(sp):
                for t, n in loads:
                    sp.dma_start(t[:, :, :], a[n].rearrange("(k p) n -> p k n", p=KC)).then_inc(setup_in, 16)
                sp.dma_start(w_out2[:, :, :], a["w_out2"].rearrange("(u p) n -> p u n", p=128)).then_inc(setup_in, 16)
                sp.dma_start(rope[:, :, :], a["rope"]).then_inc(setup_in, 16)
                sp.dma_start(b_qk1[:, :], a["b_qk1"]).then_inc(setup_in, 16)
                sp.dma_start(q_factor[:, :], a["q_factor"]).then_inc(setup_in, 16)
                sp.dma_start(norm1[:, :], a["norm1"]).then_inc(setup_in, 16)

            @block.scalar
            def _(act):
                for t, n in ((b_v1, "b_v1"), (b_proj1, "b_proj1"), (norm2_row, "norm2_row")):
                    act.dma_start(t[:, :], a[n].broadcast_to([P, C])).then_inc(setup_in, 16)
                act.dma_start(near[:, :], a["near"]).then_inc(setup_in, 16)
                act.dma_start(future[:, :], a["future"]).then_inc(setup_in, 16)

            @block.vector
            def _(dve):
                link = chain(dve, setup_dve)
                dve.wait_ge(setup_in, 16 * 14)
                nc.vector.memset(neg_half[:, :], -0.5)
                for j in range(2):
                    nc.vector.memset(vals[j][:, :, :, :], 1.0)
                nc.vector.tensor_tensor(qb[:, :], b_qk1[:, 0:NK], q_factor[:, :], ALU.mult)
                link(nc.vector.engine_nop())

        filled = [sem(f"filled{r}") for r in range(4)]
        emptied = [sem(f"emptied{r}") for r in range(4)]
        hid_loaded = [sem(f"hid_loaded{j}") for j in range(2)]
        rows_loaded = [sem(f"rows_loaded{j}") for j in range(2)]
        dve_self = sem("dve_self")
        var_ready, rstd_ready = sem("var_ready"), sem("rstd_ready")
        nrm_ready = sem("nrm_ready")
        qk32_ready, rest_ready = sem("qk32_ready"), sem("rest_ready")
        mid_ready, lo_ready = sem("mid_ready"), sem("lo_ready")
        parts_out = [sem(f"parts_out{i}") for i in range(2)]
        prod_in = [sem(f"prod_in{j}") for j in range(2)]
        rowp_ready = sem("rowp_ready")
        mrow_in = [sem(f"mrow_in{j}") for j in range(2)]
        probs_used = sem("probs_used")
        zeroed = sem("zeroed")
        swapped = [sem(f"swapped{i}") for i in range(2)]
        cos_ready, sin_ready, rot_ready = sem("cos_ready"), sem("sin_ready"), sem("rot_ready")
        nm_ready, prn_ready = sem("nm_ready"), sem("prn_ready")
        stored = sem("stored")

        VAR = numbered("norm1_stats", "norm2_stats", "norm2_rms", "rms3_stats")
        NRM = numbered("norm1", "rms2", "rms3")
        TURN = numbered("turn1", "turn2", "turn3")
        QK, VAL, MP = numbered("qk_split"), numbered("v1"), numbered("max_parts")
        EXP, GROUP, HEADS = numbered("exp_sum"), numbered("group_end"), numbered("heads_out")
        ROT, V2 = numbered("rotate"), numbered("v2")
        CAUSAL, PAIR, LOGIT = numbered("causal"), numbered("pair_end"), numbered("route_logits")
        NROT = NPAIR + HKV
        TURNED = {1: "norm1", 2: "rms2", 3: "rms3"}

        USED = {s: n + 1 for n, s in enumerate(x for x in ORDER if x[0] == "exp_sum" and x[3] < T - 1)}

        def taken(eng, *keys):
            for key in keys:
                r, n = place[key]
                eng.wait_ge(emptied[r], n)

        def summed(eng, step):
            if step[3] < T - 1:
                eng.wait_ge(probs_used, USED[step])
            else:
                r, n = place[("sum", step[1], step[2])]
                eng.wait_ge(filled[r], n)

        with nc.Fori(0, B // 2) as turn:
          with nc.Block() as block:

            @block.sync
            def _(sp):
                for j in range(2):
                    sp.dma_start(hid[j][:, :, :], kept_d[bass.ds((turn * 2 + j) * NIN, KEEP), :]
                                 .rearrange("(t p) c -> p t c", p=P)).then_inc(hid_loaded[j], 16)
                for j in range(2):
                    for h in range(H1):
                        sp.dma_start(Aq[j][R_PROD:R_MAX, h, :], a["dist_q"]).then_inc(rows_loaded[j], 16)
                        sp.dma_start(Ak[j][R_PROD:R_ALL, h, :], a["dist_k"]).then_inc(rows_loaded[j], 16)
                for step in ORDER:
                    kind, j, *w = step
                    if kind == "qk_split":
                        for m in range(2 * NK):
                            n = 2 * NK * (QK[step] - 1) + m
                            sp.wait_ge(lo_ready, n + 1)
                            side, k = divmod(m, NK)
                            sp.dma_start(parts_d[j, side, :, k * KC:(k + 1) * KC, :].rearrange("s p n -> p s n"),
                                         parts[n % 2][:, :, :]).then_inc(parts_out[n % 2], 16)
                        for i in range(2):
                            sp.wait_ge(parts_out[i], 16 * NK * QK[step])
                        for side, (dst, sel) in enumerate(((Aq, Q_PART), (Ak, K_PART))):
                            for g in range(NPROD):
                                sp.dma_start(dst[j][g * D1:(g + 1) * D1, :, :],
                                             parts_d[j, side, sel[g]].rearrange("(h d) n -> d h n", d=D1))\
                                    .then_inc(prod_in[j], 16)
                    elif kind == "max_parts":
                        taken(sp, step)
                        for s in range(PARTS):
                            for h in range(H1):
                                sp.dma_start(Aq[j][R_MAX + s:R_MAX + s + 1, h, :],
                                             mrow[j][s * H1 + h:s * H1 + h + 1, :]).then_inc(mrow_in[j], 16)
                    elif kind == "rotate":
                        for m in range(NROT):
                            n = NROT * (ROT[step] - 1) + m
                            taken(sp, (kind, j, m))
                            if n >= 2:
                                sp.wait_ge(rot_ready, n - 1)
                            for r in range(4):
                                o = 32 * (r ^ 1)
                                sp.dma_start(rest[n % 2][32 * r:32 * r + 32, :], qk32[n % 2][o:o + 32, :])\
                                    .then_inc(swapped[n % 2], 16)
                    elif kind == "rms3":
                        sp.wait_ge(nrm_ready, NRM[step])
                        t0 = (turn * 2 + j) * T
                        sp.dma_start(moe_in_d[bass.ds(t0, T)].rearrange("t p c -> p t c"),
                                     nrm[j][:, :, :]).then_inc(stored, 16)
                        sp.dma_start(res_d[bass.ds(t0, T)].rearrange("t p c -> p t c"),
                                     hid[j][:, :, :]).then_inc(stored, 16)
                    elif kind == "route_logits":
                        taken(sp, step)
                        sp.dma_start(logit_d[bass.ds((turn * 2 + j) * T, T)].rearrange("t p c -> p t c"),
                                     logit[j][:, :, :]).then_inc(stored, 16)
                sp.wait_ge(stored, 2 * 3 * 16)

            @block.tensor
            def _(pe):
                def begin(key):
                    r, n = place[key]
                    if n > 1:
                        pe.wait_ge(emptied[r], n - 1)
                    return region[r], filled[r]

                def turn_rows(src, key0, key1):
                    for key, tiles in ((key0, range(T - 1)), (key1, range(T - 1, T))):
                        dst, done = begin(key)
                        for k in range(NK):
                            for t in tiles:
                                o = 512 * k + P * (t - tiles[0])
                                ins = nc.tensor.transpose(dst[0:KC, o:o + P], src[:, t, k * KC:(k + 1) * KC],
                                                          ident[0:P, 0:P])
                        ins.then_inc(done, 1)

                def rows_times(lhs, rhs, steps, key0, key1):
                    for key, tiles in ((key0, range(T - 1)), (key1, range(T - 1, T))):
                        dst, done = begin(key)
                        for t in tiles:
                            o = CS * (t - tiles[0])
                            for k in range(steps):
                                ins = nc.tensor.matmul(dst[0:P, o:o + C], lhs[:, k, t * P:(t + 1) * P], rhs[:, k, :],
                                                       start=(k == 0), stop=(k == steps - 1))
                        ins.then_inc(done, 1)

                def channels_times(lhs, rhs, rows, key):
                    dst, done = begin(key)
                    for c in range(NCH):
                        for k in range(NK):
                            ins = nc.tensor.matmul(dst[0:rows, c * CS:c * CS + CH], lhs[:, k, :],
                                                   rhs[:, k, c * CH:(c + 1) * CH], start=(k == 0), stop=(k == NK - 1))
                    ins.then_inc(done, 1)

                def scores1(dst, rows, lhs, rhs, tile):
                    for c in range(NCH):
                        ins = nc.tensor.matmul(dst[0:P, c * CS:c * CS + CH], lhs[0:rows, tile * P:(tile + 1) * P],
                                               rhs[0:rows, c * CH:(c + 1) * CH], start=True, stop=False,
                                               skip_group_check=True)
                        lo, hi = max(tile * P, c * CH), min((tile + 1) * P, (c + 1) * CH)
                        if lo < hi:
                            ins = nc.tensor.matmul(dst[0:P, c * CS + lo - c * CH:c * CS + hi - c * CH],
                                                   identb[0:P, 0:P], near[:, lo - tile * P:hi - tile * P],
                                                   start=False, stop=True, skip_group_check=True)
                    return ins

                pending_sum = []

                def weighted_sum():
                    step = pending_sum.pop()
                    _, j, g, k = step
                    dst, done = begin(("sum", j, g)) if k == 0 else (region[3], filled[3])
                    taken(pe, *(("exp_sum", j, g, k, hl) for hl in range(GH)))
                    for c in range(NCH):
                        for hl in range(GH):
                            ins = nc.tensor.matmul(
                                dst[VW * hl:VW * (hl + 1), c * CS:c * CS + CH], vals[j][:, k, g * GH + hl, :],
                                probs[EXP[step] % 2][:, hl, c * CH:(c + 1) * CH],
                                start=(k == 0 and c % 2 == 0), stop=(k == T - 1), skip_group_check=True)
                    ins.then_inc(probs_used if k < T - 1 else done, 1)

                pending_turn = []

                def turn_weights():
                    step = pending_turn.pop(0)
                    _, j, u, x, i = step
                    n = CAUSAL[step]
                    dst, done = begin(("turn_p", j, u, x, i))
                    pe.wait_ge(prn_ready, n)
                    for k in range(i + 1):
                        ins = nc.tensor.transpose(dst[0:P, PK * k:PK * k + P], pr[n % 3][:, k * P:(k + 1) * P],
                                                  ident[0:P, 0:P])
                    ins.then_inc(done, 1)

                for step in ORDER:
                    kind, j, *w = step
                    if kind in ("turn1", "turn2", "turn3"):
                        n = int(kind[-1])
                        pe.wait_ge(nrm_ready, NRM[(TURNED[n], j)])
                        turn_rows(tmp[j] if n == 2 else nrm[j], (kind, j, 0), (kind, j, 1))
                    elif kind == "qk_split":
                        taken(pe, ("turn1", j, 0), ("turn1", j, 1))
                        for m in range(2 * NK):
                            channels_times(w_qkv1[:, :, m * KC:(m + 1) * KC], xT[j], KC, (kind, j, m))
                    elif kind == "v1":
                        rows_times(xT[j], w_qkv1[:, :, 2 * C:3 * C], NK, (kind, j, 0), (kind, j, 1))
                    elif kind == "row_max":
                        h, i = w
                        if h == 0 and i == 0:
                            pe.wait_ge(prod_in[j], 16 * 2 * NPROD)
                            pe.wait_ge(rows_loaded[j], 16 * 2 * H1)
                        dst, done = begin((kind, j, h, i))
                        scores1(dst, R_MAX, Aq[j][:, h, :], Ak[j][:, h, :], i).then_inc(done, 1)
                    elif kind == "max_parts":
                        pe.wait_ge(rowp_ready, MP[step])
                        dst, done = begin((kind, j))
                        for t in range(T):
                            ins = nc.tensor.matmul(dst[0:PARTS * H1, PK * t:PK * t + P], rowp[j][:, t, :],
                                                   identb[0:P, 0:P], start=True, stop=True)
                        ins.then_inc(done, 1)
                    elif kind == "exp_sum":
                        g, k = w
                        if g == 0 and k == 0:
                            pe.wait_ge(mrow_in[j], 16 * PARTS * H1)
                            taken(pe, ("v1", j, 0), ("v1", j, 1))
                        for hl in range(GH):
                            h = g * GH + hl
                            dst, done = begin((kind, j, g, k, hl))
                            scores1(dst, R_ALL, Ak[j][:, h, :], Aq[j][:, h, :], k).then_inc(done, 1)
                        if pending_sum:
                            weighted_sum()
                        pending_sum.append(step)
                    elif kind == "group_end":
                        if pending_sum and pending_sum[0][1:3] == (j, w[0]):
                            weighted_sum()
                    elif kind == "heads_out":
                        taken(pe, *(("sum", j, g) for g in range(NG)))
                        for t in range(T):
                            dst, done = begin(("turn_n", j, t))
                            for g in range(NG):
                                ins = nc.tensor.transpose(dst[0:P, 128 * g:128 * g + 128],
                                                          attn[j][:, g, t * P:(t + 1) * P], ident[:, :])
                            ins.then_inc(done, 1)
                        taken(pe, *(("turn_n", j, t) for t in range(T)))
                        turn_rows(tmp[j], ("turn_o", j, 0), ("turn_o", j, 1))
                        taken(pe, ("turn_o", j, 0), ("turn_o", j, 1))
                        rows_times(xT[j], w_proj1, NK, ("proj1", j, 0), ("proj1", j, 1))
                    elif kind == "rotate":
                        taken(pe, ("turn2", j, 0), ("turn2", j, 1))
                        for m in range(NROT):
                            channels_times(w_qkv2[:, :, m * 128:(m + 1) * 128], xT[j], 128, (kind, j, m))
                    elif kind == "v2":
                        rows_times(xT[j], w_qkv2[:, :, NROT * 128:], NK, (kind, j, 0), (kind, j, 1))
                    elif kind == "causal":
                        u, x, i = w
                        if (u, x, i) == (0, 0, 0):
                            pe.wait_ge(rot_ready, NROT * ROT[("rotate", j)])
                            pe.wait_ge(zeroed, 2 * ROT[("rotate", j)])
                            taken(pe, ("v2", j, 0), ("v2", j, 1))
                        dst, done = begin((kind, j, u, x, i))
                        slots = dst[0:P, :].rearrange("p (t n) -> p t n", n=PK)[:, :, 0:P]
                        keys = k2[j][:, u // 2, x, :].rearrange("p (t n) -> p t n", n=P)
                        lhs = q2[j][:, u, i * P:(i + 1) * P]
                        near_end = min(i + 1, T - 1)
                        for lo, hi in ((0, near_end), (near_end, i + 1)):
                            if lo < hi:
                                nc.tensor.matmul(slots[:, lo:hi, :], lhs, keys[:, lo:hi, :], start=True, stop=False,
                                                 skip_group_check=True)
                        nc.tensor.matmul(slots[:, i, :], identb[0:P, 0:P], future[:, :], start=False, stop=True,
                                         skip_group_check=True).then_inc(done, 1)
                        pending_turn.append(step)
                        if len(pending_turn) > 2:
                            turn_weights()
                    elif kind == "pair_end":
                        u, = w
                        while pending_turn and pending_turn[0][1:3] == (j, u):
                            turn_weights()
                        dst, done = begin((kind, j, u))
                        taken(pe, ("turn_p", j, u, 1, T - 1))
                        first = 2 * (PAIR[step] - 1)
                        half = 3 * P
                        for k in range(T):
                            for lo, hi, o in ((k * P, half, k * P), (max(half, k * P), KEEP, 512 + max(half, k * P) - half)):
                                if lo >= hi:
                                    continue
                                for x in range(2):
                                    ins = nc.tensor.matmul(
                                        dst[D2 * x:D2 * (x + 1), o:o + hi - lo], v2[j][:, k, D2 * (u // 2):D2 * (u // 2 + 1)],
                                        pt[(first + x) % 3][:, k, lo:hi], start=(k == 0), stop=(k == T - 1),
                                        skip_group_check=True)
                        ins.then_inc(done, 1)
                    elif kind == "out2":
                        taken(pe, ("pair_end", j, NPAIR - 1))
                        rows_times(attn[j], w_out2, NPAIR, (kind, j, 0), (kind, j, 1))
                    elif kind == "route_logits":
                        taken(pe, ("turn3", j, 0), ("turn3", j, 1))
                        dst, done = begin((kind, j))
                        for t in range(T):
                            for k in range(NK):
                                ins = nc.tensor.matmul(dst[0:P, E * t:E * t + E], xT[j][:, k, t * P:(t + 1) * P],
                                                       w_router[:, k, :], start=(k == 0), stop=(k == NK - 1))
                        ins.then_inc(done, 1)

            @block.scalar
            def _(act):
                def full(key):
                    r, n = place[key]
                    act.wait_ge(filled[r], n)
                    return region[r], emptied[r]

                def take_turned(j, key0, key1, scale=None):
                    for key, lo, hi in ((key0, 0, T - 1), (key1, T - 1, T)):
                        src, done = full(key)
                        n = (hi - lo) * P
                        if scale is None:
                            ins = nc.scalar.copy(xT[j][:, :, lo * P:hi * P],
                                                 src[0:KC, :].rearrange("p (k n) -> p k n", k=NK)[:, :, 0:n])
                        else:
                            for k in range(NK):
                                ins = nc.scalar.activation(xT[j][:, k, lo * P:hi * P], src[0:KC, 512 * k:512 * k + n],
                                                           ACT.Copy, scale=scale[:, k:k + 1])
                        ins.then_inc(done, 1)

                for step in ORDER:
                    kind, j, *w = step
                    if kind in ("turn1", "turn2", "turn3"):
                        take_turned(j, (kind, j, 0), (kind, j, 1), norm1 if kind == "turn2" else None)
                    elif kind == "qk_split":
                        for m in range(2 * NK):
                            n = 2 * NK * (QK[step] - 1) + m
                            if n >= 2:
                                act.wait_ge(rest_ready, n - 1)
                                act.wait_ge(parts_out[n % 2], 16 * (n // 2))
                            src, done = full((kind, j, m))
                            side, k = divmod(m, NK)
                            scale = q_factor[:, k:k + 1] if side == 0 else 1.0
                            bias = qb[:, k:k + 1] if side == 0 else b_qk1[:, NK + k:NK + k + 1]
                            for dst in (qk32[n % 2][0:KC, :], parts[n % 2][:, HI, :]):
                                ins = nc.scalar.activation(dst.rearrange("p (c n) -> p c n", n=CH), chunks(src, KC),
                                                           ACT.Identity, bias=bias, scale=scale)
                                ins.then_inc(qk32_ready if dst.dtype == F32 else done, 1)
                    elif kind == "max_parts":
                        src, done = full((kind, j))
                        ins = nc.scalar.copy(mrow[j][:, :].rearrange("p (t n) -> p t n", n=P),
                                             src[0:PARTS * H1, :].rearrange("p (t n) -> p t n", n=PK)[:, 0:T, 0:P])
                        ins.then_inc(done, 1)
                    elif kind == "exp_sum":
                        g, k = w
                        n = EXP[step]
                        if n > 2:
                            summed(act, step_before(step, 2))
                        for hl in range(GH):
                            src, done = full((kind, j, g, k, hl))
                            ins = nc.scalar.activation(
                                probs[n % 2][:, hl, :].rearrange("p (c n) -> p c n", n=CH), chunks(src, P),
                                ACT.Exp, scale=SLOPES[g * GH + hl])
                            ins.then_inc(done, 1)
                    elif kind == "group_end":
                        src, done = full(("sum", j, w[0]))
                        ins = nc.scalar.copy(attn[j][:, w[0], :].rearrange("p (c n) -> p c n", n=CH), chunks(src))
                        ins.then_inc(done, 1)
                    elif kind == "heads_out":
                        take_turned(j, ("turn_o", j, 0), ("turn_o", j, 1))
                    elif kind == "rotate":
                        for m in range(NROT):
                            n = NROT * (ROT[step] - 1) + m
                            if n >= 2:
                                act.wait_ge(cos_ready, n - 1)
                                act.wait_ge(swapped[n % 2], 64 * (n // 2))
                            src, done = full((kind, j, m))
                            ins = nc.scalar.activation(qk32[n % 2][:, :].rearrange("p (c n) -> p c n", n=CH), chunks(src),
                                                       ACT.Copy, scale=D2 ** -0.5 if m < NPAIR else 1.0)
                            ins.then_inc(done, 1)
                    elif kind == "v2":
                        for i, (lo, hi) in enumerate(((0, T - 1), (T - 1, T))):
                            src, done = full((kind, j, i))
                            ins = nc.scalar.copy(v2[j][:, lo:hi, :],
                                                 src[0:P, :].rearrange("p (t n) -> p t n", n=CS)[:, 0:hi - lo, 0:C])
                            ins.then_inc(done, 1)
                    elif kind == "causal":
                        u, x, i = w
                        n = CAUSAL[step]
                        src, done = full((kind, j, u, x, i))
                        act.wait_ge(nm_ready, n)
                        if n > 3:
                            r, m = place[("turn_p", *step_before(step, 3)[1:])]
                            act.wait_ge(filled[r], m)
                        ins = nc.scalar.activation(
                            pr[n % 3][:, 0:(i + 1) * P].rearrange("p (t n) -> p t n", n=P),
                            src[0:P, :].rearrange("p (t n) -> p t n", n=PK)[:, 0:i + 1, 0:P],
                            ACT.Exp, bias=nm[n % 4][:, 0:1], accum_out=den[n % 4][:, 0:1])
                        ins.then_inc(done, 1)
                    elif kind == "route_logits":
                        src, done = full((kind, j))
                        ins = nc.scalar.copy(logit[j][:, :, :], src[0:P, 0:T * E].rearrange("p (t e) -> p t e", e=E))
                        ins.then_inc(done, 1)

            @block.vector
            def _(dve):
                link = chain(dve, dve_self)

                def full(key):
                    r, n = place[key]
                    dve.wait_ge(filled[r], n)
                    return region[r], emptied[r]

                def rows(src, n):
                    return src[0:P, :].rearrange("p (t n) -> p t n", n=CS)[:, 0:n, 0:C]

                def wide(row, n):
                    return row[:, :].unsqueeze(1).broadcast_to([P, n, C])

                def mean_of_squares(src, j):
                    for t in range(T):
                        link(nc.vector.tensor_tensor_reduce(junk[:, :], src[:, t, :], src[:, t, :], 1.0 / C, RMS_EPS,
                                                            ALU.mult, ALU.add, var[j][:, t:t + 1]))
                    nc.vector.engine_nop().then_inc(var_ready, 1)

                pending_norm, pending_take = [], []

                def normalise():
                    step = pending_norm.pop(0)
                    n, i = CAUSAL[step], step[-1]
                    taken(dve, step)
                    link(nc.vector.reciprocal(rden[n % 4][:, :], den[n % 4][:, :]))
                    v = pr[n % 3][:, 0:(i + 1) * P]
                    nc.vector.tensor_scalar(v, v, rden[n % 4][:, 0:1], None, ALU.mult).then_inc(prn_ready, 1)

                def take_turned():
                    step = pending_take.pop(0)
                    _, j, u, x, i = step
                    head = 2 * (PAIR[("pair_end", j, u)] - 1) + x
                    src, done = full(("turn_p", j, u, x, i))
                    if head >= 3 and i == 0:
                        first = list(PAIR)[(head - 3) // 2]
                        r, n = place[first]
                        dve.wait_ge(filled[r], n)
                    ins = nc.vector.tensor_copy(pt[head % 3][:, 0:i + 1, i * P:(i + 1) * P],
                                                src[0:P, :].rearrange("p (t n) -> p t n", n=PK)[:, 0:i + 1, 0:P])
                    ins.then_inc(done, 1)

                for step in ORDER:
                    kind, j, *w = step
                    if kind in ("norm1_stats", "norm2_stats"):
                        if kind == "norm1_stats":
                            dve.wait_ge(hid_loaded[j], 16)
                        for t in range(T):
                            link(nc.vector.bn_stats(stats[j][:, t, :], hid[j][:, t, :]), wait=t == T - 1)
                        for t in range(T):
                            link(nc.vector.bn_aggr(mv[j][:, t, :], stats[j][:, t, :]), wait=t == T - 1)
                        nc.vector.tensor_scalar(var[j][:, :], mv[j][:, :, 1], LN_EPS, None, ALU.add)\
                            .then_inc(var_ready, 1)
                    elif kind in ("norm1", "norm2"):
                        dve.wait_ge(rstd_ready, VAR[(kind + "_stats", j)])
                        for t in range(T):
                            ins = nc.vector.tensor_scalar(nrm[j][:, t, :], hid[j][:, t, :], mv[j][:, t, 0:1],
                                                          rstd[j][:, t:t + 1], ALU.subtract, ALU.mult)
                            if kind == "norm2":
                                link(ins, wait=t == T - 1)
                        if kind == "norm1":
                            ins.then_inc(nrm_ready, 1)
                    elif kind == "norm2_rms":
                        mean_of_squares(nrm[j], j)
                    elif kind == "rms2":
                        dve.wait_ge(rstd_ready, VAR[("norm2_rms", j)])
                        for t in range(T):
                            ins = nc.vector.tensor_scalar(tmp[j][:, t, :], nrm[j][:, t, :], rstd[j][:, t:t + 1], None,
                                                          ALU.mult)
                        ins.then_inc(nrm_ready, 1)
                    elif kind == "qk_split":
                        for m in range(2 * NK):
                            n = 2 * NK * (QK[step] - 1) + m
                            dve.wait_ge(qk32_ready, n + 1)
                            taken(dve, (kind, j, m))
                            if n >= 2:
                                dve.wait_ge(lo_ready, n - 1)
                            i = n % 2
                            nc.vector.tensor_tensor(rest[i][0:KC, :], qk32[i][0:KC, :], parts[i][:, HI, :],
                                                    ALU.subtract).then_inc(rest_ready, 1)
                            dve.wait_ge(rest_ready, n + 1)
                            nc.vector.tensor_copy(parts[i][:, MID, :], rest[i][0:KC, :]).then_inc(mid_ready, 1)
                    elif kind == "v1":
                        for i, (lo, hi) in enumerate(((0, T - 1), (T - 1, T))):
                            src, done = full((kind, j, i))
                            ins = nc.vector.tensor_tensor(
                                vals[j][:, lo:hi, :, 0:D1], rows(src, hi - lo).rearrange("p t (h d) -> p t h d", d=D1),
                                wide(b_v1, hi - lo).rearrange("p t (h d) -> p t h d", d=D1), ALU.add)
                            ins.then_inc(done, 1)
                    elif kind == "row_max":
                        h, i = w
                        src, done = full((kind, j, h, i))
                        nc.vector.tensor_reduce(mx[j][:, h, i:i + 1], chunks(src, P), AX.XY, ALU.max)\
                            .then_inc(done, 1)
                    elif kind == "max_parts":
                        taken(dve, ("row_max", j, H1 - 1, T - 1))
                        by_tile = [rowp[j][:, :, s * H1:(s + 1) * H1].rearrange("p t h -> p h t") for s in range(PARTS)]
                        link(nc.vector.tensor_scalar(mtmp[:, 0], mx[j][:, :, :], -1.0, None, ALU.mult))
                        link(nc.vector.tensor_copy(by_tile[HI], mtmp[:, 0]))
                        link(nc.vector.tensor_tensor(mtmp[:, 1], mtmp[:, 0], by_tile[HI], ALU.subtract))
                        link(nc.vector.tensor_copy(by_tile[MID], mtmp[:, 1]))
                        nc.vector.tensor_tensor(by_tile[LO], mtmp[:, 1], by_tile[MID], ALU.subtract)\
                            .then_inc(rowp_ready, 1)
                    elif kind == "heads_out":
                        link(nc.vector.tensor_tensor(nrm[j][:, :, :], hid[j][:, :, :], wide(b_proj1, T), ALU.add))
                        for t in range(T):
                            src, done = full(("turn_n", j, t))
                            v = src[0:P, 0:H1 * VW].rearrange("p (h n) -> p h n", n=VW)
                            link(nc.vector.reciprocal(recip[:, t, :], v[:, :, D1]))
                            ins = nc.vector.tensor_tensor(
                                tmp[j][:, t, :].rearrange("p (h d) -> p h d", d=D1), v[:, :, 0:D1],
                                recip[:, t, :].unsqueeze(2).broadcast_to([P, H1, D1]), ALU.mult)
                            ins.then_inc(done, 1)
                        for i, (lo, hi) in enumerate(((0, T - 1), (T - 1, T))):
                            src, done = full(("proj1", j, i))
                            ins = nc.vector.tensor_tensor(hid[j][:, lo:hi, :], rows(src, hi - lo), nrm[j][:, lo:hi, :], ALU.add)
                            ins.then_inc(done, 1)
                            taken(dve, ("proj1", j, i))
                    elif kind == "rotate":
                        for m in range(NROT):
                            n = NROT * (ROT[step] - 1) + m
                            i = n % 2
                            if m < NPAIR:
                                put = [(slice(0, 128), q2[j][:, m, :])]
                            else:
                                g = m - NPAIR
                                put = [(slice(0, D2), k2[j][0:D2, g, 0, :]), (slice(D2, 128), k2[j][D2:128, g, 1, :])]
                            taken(dve, (kind, j, m))
                            for q, (s, dst) in enumerate(put):
                                ins = nc.vector.tensor_tensor(dst, qk32[i][s, :], rope[s, 0, :], ALU.mult)
                                if q < len(put) - 1:
                                    link(ins, wait=False)
                            ins.then_inc(cos_ready, 1)
                            dve.wait_ge(cos_ready, n + 1)
                            dve.wait_ge(sin_ready, n + 1)
                            for q, (s, dst) in enumerate(put):
                                ins = nc.vector.tensor_tensor(dst, dst, rest[i][s, :], ALU.add)
                                if q < len(put) - 1:
                                    link(ins, wait=False)
                            ins.then_inc(rot_ready, 1)
                    elif kind == "causal":
                        u, x, i = w
                        n = CAUSAL[step]
                        src, done = full((kind, j, u, x, i))
                        nc.vector.tensor_reduce(nm[n % 4][:, :],
                                                src[0:P, :].rearrange("p (t n) -> p t n", n=PK)[:, 0:i + 1, 0:P],
                                                AX.XY, ALU.max, negate=True).then_inc(nm_ready, 1)
                        pending_norm.append(step)
                        pending_take.append(step)
                        if len(pending_norm) > 1:
                            normalise()
                        if len(pending_take) > 3:
                            take_turned()
                    elif kind == "pair_end":
                        u, = w
                        while pending_norm and pending_norm[0][1:3] == (j, u):
                            normalise()
                        while pending_take and pending_take[0][1:3] == (j, u):
                            take_turned()
                        src, done = full((kind, j, u))
                        half = 3 * P
                        link(nc.vector.tensor_copy(attn[j][:, u, 0:half], src[:, 0:half]), wait=False)
                        ins = nc.vector.tensor_copy(attn[j][:, u, half:KEEP], src[:, 512:512 + KEEP - half])
                        ins.then_inc(done, 1)
                    elif kind == "out2":
                        for i, (lo, hi) in enumerate(((0, T - 1), (T - 1, T))):
                            src, done = full((kind, j, i))
                            ins = nc.vector.tensor_tensor(tmp[j][:, lo:hi, :], rows(src, hi - lo), nrm[j][:, lo:hi, :], ALU.add)
                            ins.then_inc(done, 1)
                            taken(dve, (kind, j, i))
                            link(nc.vector.tensor_tensor(hid[j][:, lo:hi, :], hid[j][:, lo:hi, :], tmp[j][:, lo:hi, :], ALU.add),
                                 wait=False)
                    elif kind == "rms3_stats":
                        mean_of_squares(tmp[j], j)
                    elif kind == "rms3":
                        dve.wait_ge(rstd_ready, VAR[("rms3_stats", j)])
                        for t in range(T):
                            ins = nc.vector.scalar_tensor_tensor(out=nrm[j][:, t, :], in0=tmp[j][:, t, :],
                                                                 scalar=rstd[j][:, t:t + 1], in1=norm2_row[:, :],
                                                                 op0=ALU.mult, op1=ALU.mult)
                        ins.then_inc(nrm_ready, 1)

            @block.gpsimd
            def _(pool):
                for step in ORDER:
                    kind, j, *w = step
                    if step in VAR:
                        pool.wait_ge(var_ready, VAR[step])
                        nc.gpsimd.tensor_tensor(rstd[j][:, :], var[j][:, :], neg_half[:, :], ALU.pow)\
                            .then_inc(rstd_ready, 1)
                    elif kind == "qk_split":
                        for m in range(2 * NK):
                            n = 2 * NK * (QK[step] - 1) + m
                            pool.wait_ge(mid_ready, n + 1)
                            i = n % 2
                            nc.gpsimd.tensor_tensor(parts[i][:, LO, :], rest[i][0:KC, :], parts[i][:, MID, :],
                                                    ALU.subtract).then_inc(lo_ready, 1)
                    elif kind == "heads_out":
                        taken(pool, ("turn_n", j, T - 1))
                        for q, half in enumerate((k2[j][D2:128, :, 0, :], k2[j][0:D2, :, 1, :])):
                            nc.gpsimd.memset(half, 0.0).then_inc(zeroed, 1)
                            pool.wait_ge(zeroed, 2 * (HEADS[step] - 1) + q + 1)
                    elif kind == "rotate":
                        for m in range(NROT):
                            n = NROT * (ROT[step] - 1) + m
                            pool.wait_ge(swapped[n % 2], 64 * (n // 2 + 1))
                            nc.gpsimd.tensor_tensor(rest[n % 2][:, :], rest[n % 2][:, :], rope[:, 1, :], ALU.mult)\
                                .then_inc(sin_ready, 1)

          nc.all_engine_barrier(sems_to_clear=range(sems[0].num, sems[-1].num + 1))


def experts(nc, a, region, ident, identb, moe_in_d, res_d, logit_d, slot_x_d, slot_y_d, out):
    es = ExitStack()
    with es:
        def sb(name, shape, dt=F32):
            return es.enter_context(nc.sbuf_tensor("x_" + name, shape, dt))

        def sem(name):
            return es.enter_context(nc.semaphore("ex_" + name))

        logit = sb("logit", [P, NT, E])
        rows_in = sb("rows_in", [P, NT, C])
        res = sb("res", [P, NT, C])
        before32, before = sb("before32", [P, P]), sb("before", [P, P], BF16)
        ones = sb("ones", [P, P], BF16)
        counts = sb("counts", [P, N_CNT])
        top = sb("top", [P, NT, 8])
        top_i = sb("top_i", [P, NT, 8], U32)
        top_f = sb("top_f", [P, NT, TOPK])
        gap = sb("gap", [P, NT])
        share = [sb(f"share{k}", [P, NT]) for k in range(TOPK)]
        hot = [sb(f"hot{k}", [P, NT, E]) for k in range(TOPK)]
        hot_sum = sb("hot_sum", [P, NT, E], BF16)
        total, upto = sb("total", [P, E, NT]), sb("upto", [P, E, NT])
        pos, picked = sb("pos", [P, NT, E]), sb("picked", [P, NT, E])
        over = sb("over", [P, E, WMAX])
        n_tiles, end, base = sb("n_tiles", [P, E]), sb("end", [P, E]), sb("base", [P, E])
        passed, who = sb("passed", [1, NST, E]), sb("who", [1, NST])
        who_i = sb("who_i", [1, NST], I32)
        slot = sb("slot", [P, NT])
        slot_i = [sb(f"slot_i{k}", [P, NT], I32) for k in range(TOPK)]
        w_gu = [sb(f"w_gu{i}", [KC, NK, 2 * FF]) for i in range(2)]
        w_dn = [sb(f"w_dn{i}", [ST, MF, C]) for i in range(2)]
        x_t = [sb(f"x_t{i}", [ST, C]) for i in range(2)]
        xT = [sb(f"xT{i}", [KC, NK, ST]) for i in range(2)]
        act_g = [sb(f"act_g{i}", [ST, MF, ST]) for i in range(2)]
        hidden = [sb(f"hidden{i}", [ST, MF, ST]) for i in range(2)]
        y_t = [sb(f"y_t{i}", [ST, C]) for i in range(2)]
        y_in = sb("y_in", [P, NT * TOPK, C])

        logit_in, rows_loaded, res_in, tables_in = sem("logit_in"), sem("rows_loaded"), sem("res_in"), sem("tables_in")
        dve_self = sem("dve_self")
        gap_ready, share_exp = sem("gap_ready"), sem("share_exp")
        hot_ready, prefix_ready = sem("hot_ready"), sem("prefix_ready")
        slots_ready, who_ready = sem("slots_ready"), sem("who_ready")
        scattered, gathered = sem("scattered"), [sem(f"gathered{b}") for b in range(B)]
        gu_free, dn_free = sem("gu_free"), sem("dn_free")
        gu_in = [sem(f"gu_in{i}") for i in range(2)]
        dn_in = [sem(f"dn_in{i}") for i in range(2)]
        x_in = [sem(f"x_in{i}") for i in range(2)]
        x_turned, xT_ready = sem("x_turned"), sem("xT_ready")
        gu_done, g_ready, h_ready = sem("gu_done"), sem("g_ready"), sem("h_ready")
        y_done, y_ready = sem("y_done"), sem("y_ready")
        y_out = [sem(f"y_out{i}") for i in range(2)]
        combined, stored = sem("combined"), sem("stored")

        c0 = 0
        number = counts[:, c0:c0 + E]
        c0 += E
        thresholds = counts[:, c0:c0 + WMAX]
        c0 += WMAX
        tile_no = counts[0:1, c0:c0 + NST]
        c0 += NST
        restart = counts[:, c0:c0 + E * NT]
        c0 += E * NT
        no_restart = counts[:, c0:c0 + E]
        def third(m, up):
            at = 512 * (m % 2) + up * ST
            return region[1 + m // 2][:, at:at + ST]

        with nc.Block() as block:
            @block.sync
            def _(sp):
                def load(n, s):
                    e = sp.value_load(who_i[0:1, bass.ds(n, 1)], min_val=0, max_val=E - 1)
                    sp.wait_ge(gu_free, n + 1)
                    sp.dma_start(x_t[s][:, :], slot_x_d[bass.ds(n * ST, ST), :]).then_inc(x_in[s], 16)
                    sp.dma_start(w_gu[s][:, :, :], a["w_gate_up"][bass.ds(e, 1)]
                                 .rearrange("e (k p) n -> p (e k) n", p=KC)).then_inc(gu_in[s], 16)
                    sp.wait_ge(dn_free, n + 1)
                    sp.dma_start(w_dn[s][:, :, :], a["w_down"][bass.ds(e, 1)]
                                 .rearrange("e (k p) n -> p (e k) n", p=ST)).then_inc(dn_in[s], 16)

                def store(n, s):
                    sp.wait_ge(y_ready, n + 1)
                    sp.dma_start(slot_y_d[bass.ds(n * ST, ST), :], y_t[s][:, :]).then_inc(y_out[s], 16)

                sp.dma_start(logit[:, :, :], logit_d.rearrange("t p e -> p t e")).then_inc(logit_in, 16)
                sp.dma_start(rows_in[:, :, :], moe_in_d.rearrange("t p c -> p t c")).then_inc(rows_loaded, 16)
                sp.wait_ge(who_ready, 1)
                sp.wait_ge(scattered, 16 * NT * TOPK)
                for s in range(2):
                    load(s, s)
                with sp.Fori(0, NST // 2 - 1) as it:
                    for s in range(2):
                        load(it * 2 + (2 + s), s)
                        store(it * 2 + s, s)
                for s in range(2):
                    store(NST - 2 + s, s)
                for b in range(B):
                    sp.wait_ge(combined, b + 1)
                    sp.dma_start(out[b].rearrange("(t p) c -> p t c", p=P),
                                 res[:, b * T:(b + 1) * T, :]).then_inc(stored, 16)
                sp.wait_ge(stored, 16 * B)

            @block.scalar
            def _(act):
                act.dma_start(before32[:, :], a["before"]).then_inc(tables_in, 16)
                act.dma_start(counts[:, :], a["counts"].broadcast_to([P, N_CNT])).then_inc(tables_in, 16)
                act.dma_start(res[:, :, :], res_d.rearrange("t p c -> p t c")).then_inc(res_in, 16)
                act.wait_ge(gap_ready, 1)
                nc.scalar.activation(share[1][:, :], gap[:, :], ACT.Exp).then_inc(share_exp, 1)
                for s in range(2):
                    act.sem_inc(y_out[s], 16)

                def gates(n, s):
                    for m in range(MF):
                        act.wait_ge(gu_done, n * MF + (m + 1))
                        nc.scalar.activation(act_g[s][:, m, :], third(m, 0), ACT.Silu)\
                            .then_inc(g_ready, 1)

                def take_y(n, s, turn):
                    act.wait_ge(y_done, n + 1)
                    act.wait_ge(y_out[s], turn * 16 + 16)
                    nc.scalar.copy(y_t[s][:, :], region[3][:, 512 * s:512 * s + C]).then_inc(y_ready, 1)

                gates(0, 0)
                with act.Fori(0, NST // 2 - 1) as it:
                    for s in range(2):
                        gates(it * 2 + (1 + s), 1 - s)
                        take_y(it * 2 + s, s, it)
                gates(NST - 1, 1)
                for s in range(2):
                    take_y(NST - 2 + s, s, NST // 2 - 1)

            @block.vector
            def _(dve):
                link = chain(dve, dve_self)
                dve.wait_ge(logit_in, 16)
                for t in range(NT):
                    link(nc.vector.max(top[:, t, :], logit[:, t, :]), wait=t == NT - 1)
                for t in range(NT):
                    link(nc.vector.max_index(top_i[:, t, :], top[:, t, :], logit[:, t, :]), wait=t == NT - 1)
                nc.vector.tensor_tensor(gap[:, :], top[:, :, 1], top[:, :, 0], ALU.subtract).then_inc(gap_ready, 1)
                link(nc.vector.tensor_copy(top_f[:, :, :], top_i[:, :, 0:TOPK]))
                dve.wait_ge(tables_in, 32)
                link(nc.vector.tensor_copy(before[:, :], before32[:, :]), wait=False)
                link(nc.vector.memset(ones[:, :], 1.0), wait=False)
                for k in range(TOPK):
                    link(nc.vector.tensor_tensor(hot[k][:, :, :], number.unsqueeze(1).broadcast_to([P, NT, E]),
                                                 top_f[:, :, k:k + 1].broadcast_to([P, NT, E]), ALU.is_equal))
                nc.vector.tensor_tensor(hot_sum[:, :, :], hot[0][:, :, :], hot[1][:, :, :], ALU.add)\
                    .then_inc(hot_ready, 1)
                dve.wait_ge(share_exp, 1)
                link(nc.vector.tensor_scalar(gap[:, :], share[1][:, :], 1.0, None, ALU.add))
                link(nc.vector.reciprocal(share[0][:, :], gap[:, :]))
                link(nc.vector.tensor_tensor(share[1][:, :], share[1][:, :], share[0][:, :], ALU.mult))
                dve.wait_ge(prefix_ready, 1)
                by_tile = lambda r: r[0:P, 0:NT * E].rearrange("p (t e) -> p t e", e=E)
                link(nc.vector.tensor_copy(total[:, :, :].rearrange("p e t -> p t e"), by_tile(region[1])))
                link(nc.vector.tensor_tensor_scan(upto[:, :, :].rearrange("p e t -> p (e t)"), restart,
                                                  total[:, :, :].rearrange("p e t -> p (e t)"), 0.0, ALU.mult, ALU.add))
                link(nc.vector.tensor_tensor(over[:, :, :], upto[:, :, NT - 1:NT].broadcast_to([P, E, WMAX]),
                                             thresholds.unsqueeze(1).broadcast_to([P, E, WMAX]), ALU.is_gt))
                link(nc.vector.tensor_reduce(n_tiles[:, :], over[:, :, :], AX.X, ALU.add))
                link(nc.vector.tensor_tensor_scan(end[:, :], no_restart, n_tiles[:, :], 0.0, ALU.mult, ALU.add))
                link(nc.vector.tensor_tensor(base[:, :], end[:, :], n_tiles[:, :], ALU.subtract))
                link(nc.vector.tensor_scalar(base[:, :], base[:, :], float(ST), None, ALU.mult))
                link(nc.vector.tensor_tensor(passed[:, :, :], tile_no.unsqueeze(2).broadcast_to([1, NST, E]),
                                             end[0:1, :].unsqueeze(1).broadcast_to([1, NST, E]), ALU.is_ge))
                link(nc.vector.tensor_reduce(who[:, :], passed[:, :, :], AX.X, ALU.add))
                link(nc.vector.tensor_scalar(who[:, :], who[:, :], float(E - 1), None, ALU.min))
                nc.vector.tensor_copy(who_i[:, :], who[:, :]).then_inc(who_ready, 1)
                link(nc.vector.tensor_tensor(upto[:, :, :], upto[:, :, :], total[:, :, :], ALU.subtract))
                link(nc.vector.tensor_tensor(pos[:, :, :], by_tile(region[0]),
                                             upto[:, :, :].rearrange("p e t -> p t e"), ALU.add))
                link(nc.vector.tensor_tensor(pos[:, :, :], pos[:, :, :],
                                             base[:, :].unsqueeze(1).broadcast_to([P, NT, E]), ALU.add))
                for k in range(TOPK):
                    link(nc.vector.tensor_tensor(picked[:, :, :], hot[k][:, :, :], pos[:, :, :], ALU.mult))
                    link(nc.vector.tensor_reduce(slot[:, :], picked[:, :, :], AX.X, ALU.add))
                    ins = nc.vector.tensor_copy(slot_i[k][:, :], slot[:, :])
                    ins.then_inc(slots_ready, 1)
                    dve.wait_ge(slots_ready, k + 1)

                def take_x(n, s):
                    dve.wait_ge(x_turned, n + 1)
                    nc.vector.tensor_copy(xT[s][:, :, :], region[0][0:KC, 512 * s:512 * s + NK * ST]
                                          .rearrange("p (k n) -> p k n", k=NK)).then_inc(xT_ready, 1)

                def products(n, s):
                    for m in range(MF):
                        dve.wait_ge(g_ready, n * MF + (m + 1))
                        nc.vector.tensor_tensor(hidden[s][:, m, :], third(m, 1), act_g[s][:, m, :],
                                                ALU.mult).then_inc(h_ready, 1)

                take_x(0, 0)
                take_x(1, 1)
                products(0, 0)
                with dve.Fori(0, NST // 2 - 1) as it:
                    for s in range(2):
                        take_x(it * 2 + (2 + s), s)
                        products(it * 2 + (1 + s), 1 - s)
                products(NST - 1, 1)
                dve.wait_ge(res_in, 16)
                for b in range(B):
                    dve.wait_ge(gathered[b], 16 * T * TOPK)
                    for k in range(TOPK):
                        for t in range(b * T, (b + 1) * T):
                            ins = nc.vector.scalar_tensor_tensor(
                                out=res[:, t, :], in0=y_in[:, t * TOPK + k, :], scalar=share[k][:, t:t + 1],
                                in1=res[:, t, :], op0=ALU.mult, op1=ALU.add)
                            if k == 0:
                                link(ins, wait=t == (b + 1) * T - 1)
                    ins.then_inc(combined, 1)

            @block.tensor
            def _(pe):
                pe.wait_ge(hot_ready, 1)
                pairs_in = hot_sum[:, :, :].rearrange("p t e -> p (t e)")
                nc.tensor.matmul(region[0][0:P, 0:NT * E], before[:, :], pairs_in, start=True, stop=True)
                nc.tensor.matmul(region[1][0:P, 0:NT * E], ones[:, :], pairs_in, start=True, stop=True)\
                    .then_inc(prefix_ready, 1)
                pe.sem_inc(gu_free, 2)
                pe.sem_inc(dn_free, 2)
                pe.wait_ge(slots_ready, TOPK)

                def turn_x(n, s, turn):
                    pe.wait_ge(x_in[s], turn * 16 + 16)
                    for k in range(NK):
                        ins = nc.tensor.transpose(region[0][0:KC, 512 * s + k * ST:512 * s + (k + 1) * ST],
                                                  x_t[s][:, k * KC:(k + 1) * KC], ident[:, :])
                    ins.then_inc(x_turned, 1)

                def gate_up(n, s, turn, first=False):
                    pe.wait_ge(xT_ready, n + 1)
                    pe.wait_ge(gu_in[s], turn * 16 + 16)
                    for m in range(MF):
                        if not first:
                            pe.wait_ge(h_ready, n * MF + (m + 1 - MF))
                        for up, o in enumerate((0, FF)):
                            for k in range(NK):
                                ins = nc.tensor.matmul(third(m, up),
                                                       w_gu[s][:, k, o + m * ST:o + (m + 1) * ST], xT[s][:, k, :],
                                                       start=(k == 0), stop=(k == NK - 1))
                        ins.then_inc(gu_done, 1)
                    pe.wait_ge(gu_done, n * MF + MF)
                    pe.sem_inc(gu_free, 1)

                def down(n, s, turn, first=False):
                    pe.wait_ge(dn_in[s], turn * 16 + 16)
                    pe.wait_ge(h_ready, n * MF + MF)
                    if not first:
                        pe.wait_ge(y_ready, n - 1)
                    for m in range(MF):
                        ins = nc.tensor.matmul(region[3][:, 512 * s:512 * s + C], hidden[s][:, m, :], w_dn[s][:, m, :],
                                               start=(m == 0), stop=(m == MF - 1))
                    ins.then_inc(y_done, 1)
                    pe.wait_ge(y_done, n + 1)
                    pe.sem_inc(dn_free, 1)

                last = NST // 2 - 1
                turn_x(0, 0, 0)
                turn_x(1, 1, 0)
                gate_up(0, 0, 0, first=True)
                turn_x(2, 0, 1)
                gate_up(1, 1, 0)
                down(0, 0, 0, first=True)
                turn_x(3, 1, 1)
                gate_up(2, 0, 1)
                down(1, 1, 0, first=True)
                with pe.Fori(1, last) as it:
                    turn_x(it * 2 + 2, 0, it + 1)
                    gate_up(it * 2 + 1, 1, it)
                    down(it * 2, 0, it)
                    turn_x(it * 2 + 3, 1, it + 1)
                    gate_up(it * 2 + 2, 0, it + 1)
                    down(it * 2 + 1, 1, it)
                gate_up(NST - 1, 1, last)
                down(NST - 2, 0, last)
                down(NST - 1, 1, last)

            @block.gpsimd
            def _(pool):
                pool.wait_ge(rows_loaded, 16)
                for k in range(TOPK):
                    pool.wait_ge(slots_ready, k + 1)
                    for t in range(NT):
                        nc.gpsimd.indirect_dma_start(
                            slot_x_d, bass.IndirectOffsetOnAxis(ap=slot_i[k][:, t:t + 1], axis=0),
                            rows_in[:, t, :], None).then_inc(scattered, 16)
                for s in range(2):
                    pool.wait_ge(y_out[s], 16 * (NST // 2 + 1))
                for b in range(B):
                    for t in range(b * T, (b + 1) * T):
                        for k in range(TOPK):
                            nc.gpsimd.indirect_dma_start(
                                y_in[:, t * TOPK + k, :], None, slot_y_d,
                                bass.IndirectOffsetOnAxis(ap=slot_i[k][:, t:t + 1], axis=0)).then_inc(gathered[b], 16)


def lay_out(x, L0_tok_w, L0_tok_b, L0_attn_w_qkv, L0_attn_b_qkv, L0_attn_w_proj, L0_attn_b_proj, L0_ffn_norm1_w,
            L0_ffn_w_qkv, L0_ffn_w_out, L0_ffn_norm2_w, L0_ffn_w_router, L0_ffn_w_gate_up, L0_ffn_w_down):
    r = {"x": x, "tok_w": L0_tok_w.reshape(1, C), "tok_b": L0_tok_b.reshape(1, 1)}
    r["w_qkv1"] = L0_attn_w_qkv.T
    r["b_qk1"] = L0_attn_b_qkv[:2 * C].reshape(2 * NK, KC).T
    r["b_v1"] = L0_attn_b_qkv[2 * C:].reshape(1, C)
    r["w_proj1"] = L0_attn_w_proj.T
    r["b_proj1"] = L0_attn_b_proj.reshape(1, C)
    r["norm1"] = L0_ffn_norm1_w.reshape(NK, KC).T
    r["norm2_row"] = L0_ffn_norm2_w.reshape(1, C)
    w = L0_ffn_w_qkv
    nq, nk = H2 * D2, HKV * D2
    q = w[:, :nq].reshape(C, H2, HALF, 2).transpose(0, 1, 3, 2).reshape(C, nq)
    k = w[:, nq:nq + nk].reshape(C, HKV, HALF, 2).transpose(0, 1, 3, 2).reshape(C, HKV, 1, D2)
    k = np.broadcast_to(k, (C, HKV, 2, D2)).reshape(C, 2 * nk)
    r["w_qkv2"] = np.concatenate([q, k, w[:, nq + nk:]], axis=1)
    r["w_out2"] = L0_ffn_w_out
    r["w_router"] = L0_ffn_w_router
    r["w_gate_up"] = L0_ffn_w_gate_up
    r["w_down"] = L0_ffn_w_down
    r.update(constants())
    return {n: np.ascontiguousarray(v) for n, v in r.items()}


def kernel(**inputs):
    import concourse.bacc as bacc
    from concourse.bass_utils import run_bass_kernel_spmd

    nc = bacc.Bacc("TRN2", target_bir_lowering=False, num_devices=1)
    arrays, aps = {}, {}
    for name, v in lay_out(**{n: np.asarray(v) for n, v in inputs.items()}).items():
        arrays[f"in_{name}"] = v
        aps[name] = nc.dram_tensor(f"in_{name}", v.shape, mybir.dt.from_np(v.dtype), kind="ExternalInput").ap()
    out = nc.dram_tensor("out", [B, KEEP, C], F32, kind="ExternalOutput").ap()
    audio_tower(nc, aps, out)
    r = run_bass_kernel_spmd(nc, [arrays], core_ids=[0])
    return r.results[0]["out"]
```

```python
from contextlib import ExitStack

import numpy as np
import concourse.bass as bass
from concourse import mybir

ALU = mybir.AluOpType
ACT = mybir.ActivationFunctionType
AX = mybir.AxisListType
F32 = mybir.dt.float32
BF16 = mybir.dt.bfloat16
I32 = mybir.dt.int32
U32 = mybir.dt.uint32

B, NIN, C = 4, 750, 192
KEEP = int(round(NIN * 0.7))
P_IN = 125
T_IN = NIN // P_IN
P = 105
T = KEEP // P
CH = 175
NCH = KEEP // CH
CS = 256
KC = 96
NK = C // KC

H1, D1 = 12, 16
PARTS = 3
HI, MID, LO = range(PARTS)
Q_PART = [HI, HI, HI, MID, MID, LO]
K_PART = [HI, MID, LO, HI, MID, HI]
NPROD = len(Q_PART)
R_PROD = NPROD * D1
R_DIST = 4 * T
R_MAX = R_PROD + R_DIST
R_ALL = R_MAX + PARTS
GH = 4
NG = H1 // GH
VW = 32

H2, HKV, D2 = 12, 3, 64
HALF = D2 // 2
NPAIR = H2 // 2
PK = 128
THETA = 10000.0

E, TOPK, FF = 16, 2, 384
NTOK = B * KEEP
NT = B * T
ST = 128
NST = (NTOK * TOPK + E * (ST - 1)) // ST
NSLOT = NST * ST
MF = FF // ST
WMAX = -(-NTOK // ST)
RX = 4

LN_EPS, RMS_EPS = 1e-5, 1e-6
SLOPES = [float(np.float32(2.0 ** (-8.0 / H1)) ** np.float32(h + 1)) for h in range(H1)]


def constants():
    c = {}
    c["ident"] = np.eye(128, dtype=np.float32)
    n = np.arange(KEEP)
    big, rest, tile = n // 4 * 4, n % 4, n // P
    q, k = np.zeros((R_DIST, KEEP), np.float32), np.zeros((R_DIST, KEEP), np.float32)
    for i in range(T):
        s = np.sign(tile - i)
        q[4 * i:4 * i + 4] = np.stack([big, rest, n >= 0, n >= 0]) * (tile == i)
        k[4 * i:4 * i + 4] = np.stack([s, s, -s * big, -s * rest])
    bf16 = mybir.dt.np(BF16)
    c["dist_q"] = q.astype(bf16)
    c["dist_k"] = np.concatenate([k, np.ones((PARTS, KEEP), np.float32)]).astype(bf16)
    m = np.arange(P)
    c["near"] = -np.abs(m[:, None] - m[None, :]).astype(bf16)
    c["future"] = np.where(m[None, :] > m[:, None], -1e30, 0.0).astype(bf16)
    t = np.arange(P_IN)
    c["earlier"] = (t[None, :] < t[:, None]).astype(np.float32)
    f = np.repeat(np.float32(D1 ** -0.5) / np.asarray(SLOPES, np.float32), D1)
    c["q_factor"] = np.ascontiguousarray(f.reshape(NK, KC).T.astype(np.float32))
    inv = (1.0 / np.float32(THETA) ** (np.arange(0, D2, 2, dtype=np.float32) / np.float32(D2)))
    a = np.arange(KEEP, dtype=np.float32)[None, :] * inv.astype(np.float32)[:, None]
    cos, sin = np.cos(a).astype(np.float32), np.sin(a).astype(np.float32)
    c["rope"] = np.ascontiguousarray(
        np.stack([np.concatenate([cos] * 4), np.concatenate([-sin, -sin, sin, sin])], axis=1))
    row = np.arange(128) // HALF
    c["own"] = np.stack([row % 2 == x for x in range(2)], axis=1) * np.float32(D2 ** -0.5)
    c["before"] = (m[:, None] < m[None, :]).astype(np.float32)
    marks = np.ones((E, NT), np.float32)
    marks[:, 0] = 0
    marks1 = np.ones(E, np.float32)
    c["counts"] = np.concatenate([
        np.arange(E), np.arange(WMAX) * ST, np.arange(NST), marks.ravel(), marks1]).astype(np.float32)[None]
    return c


N_CNT = E + WMAX + NST + E * NT + E


def audio_tower(nc, a, out):
    es = ExitStack()
    with es:
        def sb(name, shape, dt=F32):
            return es.enter_context(nc.sbuf_tensor(name, shape, dt))

        def dram(name, shape, dt=F32):
            return nc.dram_tensor(name, shape, dt, kind="Internal").ap()

        score_d = dram("score_d", [B * T_IN, P_IN])
        kept_d = dram("kept_d", [B * NIN, C])
        parts_d = dram("parts_d", [2, 2, PARTS, C, KEEP], BF16)
        moe_in_d = dram("moe_in_d", [NT, P, C])
        res_d = dram("res_d", [NT, P, C])
        logit_d = dram("logit_d", [NT, P, E])
        slot_x_d = dram("slot_x_d", [NSLOT, C])
        slot_y_d = dram("slot_y_d", [NSLOT, C])

        region = [es.enter_context(nc.psum_tensor(f"region{i}", [128, 1024], F32)) for i in range(4)]

        ident = sb("ident", [128, 128])
        identb = sb("identb", [128, 128], BF16)

        sort_tokens(nc, a, region, ident, identb, score_d, kept_d, slot_x_d)
        tower(nc, a, region, ident, identb, kept_d, parts_d, moe_in_d, res_d, logit_d)
        experts(nc, a, region, ident, identb, moe_in_d, res_d, logit_d, slot_x_d, slot_y_d, out)


def chain(eng, sem):
    count = [0]

    def link(ins, wait=True):
        count[0] += 1
        ins.then_inc(sem, 1)
        if wait:
            eng.wait_ge(sem, count[0])
        return count[0]
    return link


def chunks(region, rows=128):
    return region[0:rows, :].rearrange("p (c x) -> p c x", x=CS)[:, 0:NCH, 0:CH]


def sort_tokens(nc, a, region, ident, identb, score_d, kept_d, slot_x_d):
    es = ExitStack()
    with es:
        def sb(name, shape, dt=F32):
            return es.enter_context(nc.sbuf_tensor(name, shape, dt))

        def sem(name):
            return es.enter_context(nc.semaphore(name))

        NB = B * T_IN
        x_in = sb("x_in", [P_IN, NB, C])
        tok_w = sb("tok_w", [P_IN, C])
        tok_b = sb("tok_b", [P_IN, 1])
        earlier = sb("earlier", [P_IN, P_IN])
        prod = sb("prod", [P_IN, C])
        score = sb("score", [P_IN, NB])
        score_t = sb("score_t", [NB, P_IN])
        all_scores = sb("all_scores", [P_IN, B, NIN])
        hit = sb("hit", [P_IN, NIN])
        cnt = sb("cnt", [P_IN, NB, 3])
        rank = sb("rank", [P_IN, NB])
        rank_i = sb("rank_i", [P_IN, NB], I32)
        zeros = sb("zeros", [ST, NST // 4 * C])

        consts_in = sem("so_consts_in")
        x_loaded = [sem(f"so_x_loaded{b}") for b in range(B)]
        dve_self = sem("so_dve_self")
        identb_ready = sem("so_identb_ready")
        scores_ready = sem("so_scores_ready")
        scores_turned = sem("so_scores_turned")
        scores_row = sem("so_scores_row")
        scores_out = sem("so_scores_out")
        scores_back = [sem(f"so_scores_back{b}") for b in range(B)]
        ranks_ready = sem("so_ranks_ready")
        scattered = sem("so_scattered")
        zeros_ready = sem("so_zeros_ready")
        zeroed = sem("so_zeroed")

        with nc.Block() as block:
            @block.sync
            def _(sp):
                for b in range(B):
                    sp.dma_start(x_in[:, b * T_IN:(b + 1) * T_IN, :],
                                 a["x"][b].rearrange("(t p) c -> p t c", p=P_IN)).then_inc(x_loaded[b], 16)
                sp.wait_ge(scores_row, 1)
                sp.dma_start(score_d, score_t[:, :]).then_inc(scores_out, 16)
                sp.wait_ge(scores_out, 16)
                for b in range(B):
                    src = score_d[b * T_IN:(b + 1) * T_IN, :].rearrange("(a t) p -> a (t p)", a=1)
                    sp.dma_start(all_scores[:, b, :], src.broadcast_to([P_IN, NIN])).then_inc(scores_back[b], 16)

            @block.scalar
            def _(act):
                act.dma_start(tok_w[:, :], a["tok_w"].broadcast_to([P_IN, C])).then_inc(consts_in, 16)
                act.dma_start(tok_b[:, :], a["tok_b"].broadcast_to([P_IN, 1])).then_inc(consts_in, 16)
                act.dma_start(ident[:, :], a["ident"]).then_inc(consts_in, 16)
                act.dma_start(earlier[:, :], a["earlier"]).then_inc(consts_in, 16)
                act.wait_ge(zeros_ready, 1)
                v = slot_x_d.rearrange("(n p r) c -> n p (r c)", n=4, p=ST)
                for n in range(4):
                    act.dma_start(v[n], zeros[:, :]).then_inc(zeroed, 16)
                act.wait_ge(zeroed, 64)

            @block.vector
            def _(dve):
                link = chain(dve, dve_self)
                dve.wait_ge(consts_in, 64)
                nc.vector.tensor_copy(identb[:, :], ident[:, :]).then_inc(identb_ready, 1)
                dve.wait_ge(identb_ready, 1)
                for b in range(B):
                    dve.wait_ge(x_loaded[b], 16)
                    for t in range(b * T_IN, (b + 1) * T_IN):
                        link(nc.vector.tensor_tensor_reduce(prod[:, :], x_in[:, t, :], tok_w[:, :], 1.0, 0.0,
                                                            ALU.mult, ALU.add, score[:, t:t + 1]))
                link(nc.vector.tensor_scalar(score[:, :], score[:, :], tok_b[:, 0:1], None, ALU.add))
                nc.vector.engine_nop().then_inc(scores_ready, 1)
                dve.wait_ge(scores_turned, 1)
                nc.vector.tensor_copy(score_t[:, :], region[0][0:NB, 0:P_IN]).then_inc(scores_row, 1)
                for b in range(B):
                    dve.wait_ge(scores_back[b], 16)
                    for t in range(T_IN):
                        n = b * T_IN + t
                        own, lo, hi = score[:, n:n + 1], t * P_IN, (t + 1) * P_IN
                        if t:
                            link(nc.vector.tensor_scalar(hit[:, 0:lo], all_scores[:, b, 0:lo], own, 0.0,
                                                         ALU.is_ge, ALU.add, accum_out=cnt[:, n, 0:1]))
                        else:
                            link(nc.vector.memset(cnt[:, n, 0:1], 0.0))
                        link(nc.vector.tensor_scalar(hit[:, lo:NIN], all_scores[:, b, lo:NIN], own, 0.0,
                                                     ALU.is_gt, ALU.add, accum_out=cnt[:, n, 1:2]))
                        link(nc.vector.scalar_tensor_tensor(
                            out=hit[:, 0:P_IN], in0=all_scores[:, b, lo:hi], scalar=own, in1=earlier[:, :],
                            op0=ALU.is_equal, op1=ALU.mult, accum_out=cnt[:, n, 2:3]))
                    s = slice(b * T_IN, (b + 1) * T_IN)
                    link(nc.vector.tensor_reduce(rank[:, s], cnt[:, s, :], AX.X, ALU.add))
                    link(nc.vector.tensor_scalar(rank[:, s], rank[:, s], float(b * NIN), None, ALU.add))
                    nc.vector.tensor_copy(rank_i[:, s], rank[:, s]).then_inc(ranks_ready, 1)

            @block.tensor
            def _(pe):
                pe.wait_ge(scores_ready, 1)
                nc.tensor.transpose(region[0][0:NB, 0:P_IN], score[:, :], ident[0:P_IN, 0:P_IN])\
                    .then_inc(scores_turned, 1)

            @block.gpsimd
            def _(pool):
                nc.gpsimd.memset(zeros[:, :], 0.0).then_inc(zeros_ready, 1)
                for b in range(B):
                    pool.wait_ge(ranks_ready, b + 1)
                    for n in range(b * T_IN, (b + 1) * T_IN):
                        nc.gpsimd.indirect_dma_start(
                            kept_d, bass.IndirectOffsetOnAxis(ap=rank_i[:, n:n + 1], axis=0),
                            x_in[:, n, :], None).then_inc(scattered, 16)
                pool.wait_ge(scattered, 16 * NB)




def both(*kinds):
    return [(k, j) for k in kinds for j in range(2)]


def merged(x, y):
    out, n = [], 0
    for i, s in enumerate(x):
        out.append(s)
        while n * len(x) < (i + 1) * len(y):
            out.append(y[n])
            n += 1
    return out


def maxima(j):
    return [("row_max", j, h, i) for h in range(H1) for i in range(T)] + [("max_parts", j)]


def weights(j):
    out = []
    for n in range(NG * T):
        g, k = divmod(n, T)
        for hl in range(GH):
            out.append(("exp", j, g, k, hl))
            if n and hl == 1:
                out.append(("sum", j, *divmod(n - 1, T)))
            if g and k == 0 and hl == 3:
                out.append(("group_end", j, g - 1))
    return out + [("sum", j, NG - 1, T - 1), ("group_end", j, NG - 1)]


PAIR_END, PAIR_TAKE = (0, T - 1), (1, 1)


def pairs():
    out, every = [], [(j, u) for j in range(2) for u in range(NPAIR)]
    for n, (j, u) in enumerate(every):
        for x in range(2):
            for i in range(T):
                out.append(("causal", j, u, x, i))
                if n and (x, i) == PAIR_END:
                    out.append(("pair_end", *every[n - 1]))
                if n and (x, i) == PAIR_TAKE:
                    out.append(("pair_take", *every[n - 1]))
    return out + [("pair_end", *every[-1]), ("pair_take", *every[-1])]


AHEAD, TAIL = 8, 10
ORDER = (
    both("norm1_stats", "norm1", "turn1", "qk_split", "v1") + maxima(0) + maxima(1)[:AHEAD]
    + merged(weights(0)[:-TAIL], maxima(1)[AHEAD:]) + weights(0)[-TAIL:]
    + weights(1) + both("heads_out", "norm2_stats", "norm2", "norm2_rms", "rms2", "turn2")
    + [("rotate", j, m) for m in range(NPAIR + HKV) for j in range(2)] + both("v2", "split_keys")
    + pairs() + both("out2", "rms3_stats", "rms3", "turn3", "route_logits")
)


def score_banks(x, i):
    first = 2 * x
    return [first, first + 1] if i == T - 1 else [(first + i) % 4]


def turn_bank(x, k, i):
    return (i + x + (k == T - 1)) % 2


def last_users():
    user, before = {}, {}
    for n, (_, _, _, x, i) in enumerate([s for s in ORDER if s[0] == "causal"]):
        mine = score_banks(x, i)
        before[n + 1] = sorted({user[b] for b in mine if b in user})
        user.update((b, n + 1) for b in mine)
    return before


NORM_LAG, TURN_LAG, TAKE_LAG = 2, 3, 4


def step_before(step, n):
    same = [s for s in ORDER if s[0] == step[0]]
    return same[same.index(step) - n]


def numbered(*kinds):
    steps = [s for s in ORDER if s[0] in kinds]
    return {s: n + 1 for n, s in enumerate(steps)}


def uses(order):
    count, place = [0] * 4, {}

    def use(key, r):
        count[r] += 1
        place[key] = (r, count[r])

    turn = 0
    for kind, j, *w in order:
        if kind in ("turn1", "turn2", "turn3", "turn_o"):
            use((kind, j, 0), 0)
            use((kind, j, 1), 1)
        elif kind == "qk_split":
            for m in range(2 * NK):
                use((kind, j, m), m % 4)
        elif kind in ("v1", "v2", "out2"):
            use((kind, j, 0), 2)
            use((kind, j, 1), 3)
        elif kind == "row_max" and j == 0:
            use((kind, j, *w), (w[0] * T + w[1]) % 4)
        elif kind in ("row_max", "exp"):
            use((kind, j, *w), turn % 3)
            turn += 1
        elif kind == "max_parts":
            use((kind, j), 0)
        elif kind == "sum" and w[1] == 0:
            use((kind, j, w[0]), 3)
        elif kind == "heads_out":
            for t in range(T):
                use(("turn_n", j, t), t % 2)
            use(("turn_o", j, 0), 2)
            use(("turn_o", j, 1), 3)
            use(("proj1", j, 0), 0)
            use(("proj1", j, 1), 1)
        elif kind == "rotate":
            use((kind, j, *w), (2 * w[0] + j) % 4)
        elif kind == "pair_end":
            use((kind, j, *w), 3)
        elif kind == "route_logits":
            use((kind, j), 2)
    return place, count


def tower(nc, a, region, ident, identb, kept_d, parts_d, moe_in_d, res_d, logit_d):
    es = ExitStack()
    with es:
        def sb(name, shape, dt=F32):
            return es.enter_context(nc.sbuf_tensor(name, shape, dt))

        def sem(name):
            s = es.enter_context(nc.semaphore("to_" + name))
            sems.append(s)
            return s

        sems = []
        place, _ = uses(ORDER)

        w_qkv1 = sb("w_qkv1", [KC, NK, 3 * C])
        w_proj1 = sb("w_proj1", [KC, NK, C])
        w_qkv2 = sb("w_qkv2", [KC, NK, (NPAIR + HKV) * 128 + HKV * D2])
        w_out2 = sb("w_out2", [128, NPAIR, C])
        w_router = sb("w_router", [KC, NK, E])
        b_qk1 = sb("b_qk1", [KC, 2 * NK])
        q_factor = sb("q_factor", [KC, NK])
        qb = sb("qb", [KC, NK])
        b_v1 = sb("b_v1", [P, C])
        b_proj1 = sb("b_proj1", [P, C])
        norm1 = sb("norm1", [KC, NK])
        norm2_row = sb("norm2_row", [P, C])
        near = sb("near", [P, P], BF16)
        future = sb("future", [P, P], BF16)
        rope = sb("rope", [128, 2, KEEP])
        own = sb("own", [128, 2])
        neg_half = sb("neg_half", [P, T])

        hid = [sb(f"hid{j}", [P, T, C]) for j in range(2)]
        nrm = [sb(f"nrm{j}", [P, T, C]) for j in range(2)]
        tmp = [sb(f"tmp{j}", [P, T, C]) for j in range(2)]
        xT = [sb(f"xT{j}", [KC, NK, KEEP]) for j in range(2)]
        stats = [sb(f"stats{j}", [P, T, 6]) for j in range(2)]
        mv = [sb(f"mv{j}", [P, T, 2]) for j in range(2)]
        var = [sb(f"var{j}", [P, T]) for j in range(2)]
        rstd = [sb(f"rstd{j}", [P, T]) for j in range(2)]
        big = [sb(f"big{j}", [128, 2 * H1 * KEEP], BF16) for j in range(2)]
        Aq = [x[0:R_ALL, 0:H1 * KEEP].rearrange("p (h n) -> p h n", h=H1) for x in big]
        Ak = [x[0:R_ALL, H1 * KEEP:].rearrange("p (h n) -> p h n", h=H1) for x in big]
        q2 = [x[:, 0:H1 * KEEP].bitcast(F32).rearrange("p (u n) -> p u n", u=NPAIR) for x in big]
        k2 = [x[:, H1 * KEEP:].bitcast(F32).rearrange("p (g x n) -> p g x n", g=HKV, x=2) for x in big]
        vals = [sb(f"vals{j}", [128, T, H1, VW]) for j in range(2)]
        mx = [sb(f"mx{j}", [P, H1, T]) for j in range(2)]
        rowp = [sb(f"rowp{j}", [P, T, PARTS * H1], BF16) for j in range(2)]
        junk = sb("junk", [P, C])
        mtmp = sb("mtmp", [P, 2, H1, T])
        mrow = [sb(f"mrow{j}", [PARTS * H1, KEEP], BF16) for j in range(2)]
        v2 = [sb(f"v2{j}", [128, T, HKV * D2]) for j in range(2)]
        attn = [sb(f"attn{j}", [128, NPAIR, KEEP]) for j in range(2)]
        RROT = NPAIR // 2
        plain = [[x[:, i, :] for i in range(RROT)] for x in attn]
        swap = [[x[:, RROT + i, :] for i in range(RROT)] for x in attn]
        logit = [sb(f"logit{j}", [P, T, E]) for j in range(2)]
        qk32 = [sb(f"qk32_{i}", [128, KEEP]) for i in range(2)]
        rest = [sb(f"rest{i}", [128, KEEP]) for i in range(2)]
        part_room = sb("part_room", [128, 2 * PARTS * KEEP], BF16)
        parts = [part_room[0:KC, i * PARTS * KEEP:(i + 1) * PARTS * KEEP].rearrange("p (s n) -> p s n", s=PARTS)
                 for i in range(2)]
        pr = [part_room[0:P, i * 2 * KEEP:(i + 1) * 2 * KEEP].bitcast(F32) for i in range(3)]
        pr += [qk32[0][0:P, :], qk32[1][0:P, :]]
        pt = [sb(f"pt{i}", [128, T, KEEP]) for i in range(3)]
        probs = [t[:, 0:GH, :] for t in pt[0:2]]
        recip = sb("recip", [P, T, H1])
        RING = 8
        nm = sb("nm", [P, RING])
        den = sb("den", [P, RING])
        rden = sb("rden", [P, RING])

        setup_in = es.enter_context(nc.semaphore("to_setup_in"))
        setup_dve = es.enter_context(nc.semaphore("to_setup_dve"))

        with nc.Block() as block:
            loads = [(w_qkv1, "w_qkv1"), (w_proj1, "w_proj1"), (w_qkv2, "w_qkv2"), (w_router, "w_router")]

            @block.sync
            def _(sp):
                for t, n in loads:
                    sp.dma_start(t[:, :, :], a[n].rearrange("(k p) n -> p k n", p=KC)).then_inc(setup_in, 16)
                sp.dma_start(w_out2[:, :, :], a["w_out2"].rearrange("(u p) n -> p u n", p=128)).then_inc(setup_in, 16)
                sp.dma_start(rope[:, :, :], a["rope"]).then_inc(setup_in, 16)
                sp.dma_start(b_qk1[:, :], a["b_qk1"]).then_inc(setup_in, 16)
                sp.dma_start(q_factor[:, :], a["q_factor"]).then_inc(setup_in, 16)
                sp.dma_start(norm1[:, :], a["norm1"]).then_inc(setup_in, 16)
                sp.dma_start(own[:, :], a["own"]).then_inc(setup_in, 16)

            @block.scalar
            def _(act):
                for t, n in ((b_v1, "b_v1"), (b_proj1, "b_proj1"), (norm2_row, "norm2_row")):
                    act.dma_start(t[:, :], a[n].broadcast_to([P, C])).then_inc(setup_in, 16)
                act.dma_start(near[:, :], a["near"]).then_inc(setup_in, 16)
                act.dma_start(future[:, :], a["future"]).then_inc(setup_in, 16)

            @block.vector
            def _(dve):
                link = chain(dve, setup_dve)
                dve.wait_ge(setup_in, 16 * 15)
                nc.vector.memset(neg_half[:, :], -0.5)
                for t in (*pt, *v2):
                    nc.vector.memset(t[:, :, :], 0.0)
                for j in range(2):
                    nc.vector.memset(vals[j][:, :, :, :], 1.0)
                nc.vector.tensor_tensor(qb[:, :], b_qk1[:, 0:NK], q_factor[:, :], ALU.mult)
                link(nc.vector.engine_nop())

        filled = [sem(f"filled{r}") for r in range(4)]
        emptied = [sem(f"emptied{r}") for r in range(4)]
        hid_loaded = [sem(f"hid_loaded{j}") for j in range(2)]
        rows_loaded = [sem(f"rows_loaded{j}") for j in range(2)]
        dve_self = sem("dve_self")
        var_ready, rstd_ready = sem("var_ready"), sem("rstd_ready")
        nrm_ready = sem("nrm_ready")
        qk32_ready, rest_ready = sem("qk32_ready"), sem("rest_ready")
        mid_ready, lo_ready = sem("mid_ready"), sem("lo_ready")
        parts_out = [sem(f"parts_out{i}") for i in range(2)]
        prod_in = [sem(f"prod_in{j}") for j in range(2)]
        rowp_ready = sem("rowp_ready")
        mrow_in = [sem(f"mrow_in{j}") for j in range(2)]
        probs_used = sem("probs_used")
        keys_ready = sem("keys_ready")
        swapped = [[sem(f"swapped{j}_{i}") for i in range(RROT)] for j in range(2)]
        cos_ready, sin_ready, rot_ready = sem("cos_ready"), sem("sin_ready"), sem("rot_ready")
        nm_ready, prn_ready = sem("nm_ready"), sem("prn_ready")
        scored, exp_done = sem("scored"), sem("exp_done")
        turned, taken_act = sem("turned"), sem("taken_act")
        turned_last, taken_last = sem("turned_last"), sem("taken_last")
        stored = sem("stored")

        VAR = numbered("norm1_stats", "norm2_stats", "norm2_rms", "rms3_stats")
        NRM = numbered("norm1", "rms2", "rms3")
        TURN = numbered("turn1", "turn2", "turn3")
        QK, VAL, MP = numbered("qk_split"), numbered("v1"), numbered("max_parts")
        SUM, HEADS = numbered("sum"), numbered("heads_out")
        ROT, V2 = numbered("rotate"), numbered("v2")
        CAUSAL, PAIR, LOGIT = numbered("causal"), numbered("pair_end"), numbered("route_logits")
        NROT = NPAIR + HKV
        SCORE_USERS = last_users()
        STEP = {n: s for s, n in CAUSAL.items()}

        def score_tiles(x, i):
            first = score_banks(x, i)[0]
            o = 512 * (first % 2)
            return region[first // 2][0:P, o:1024].rearrange("p (t n) -> p t n", n=PK)[:, 0:i + 1, 0:P]

        def turned_tiles(x, i, lo, hi):
            o = 512 * turn_bank(x, lo, i)
            tiles = region[2][0:P, o:o + 512].rearrange("p (t n) -> p t n", n=PK)[:, :, 0:P]
            return tiles[:, 0:1, :] if lo == T - 1 else tiles[:, lo:hi, :]

        def take_turned_weights(eng, copy, step, lo, hi, ready, done):
            _, j, u, x, i = step
            head = 2 * (PAIR[("pair_end", j, u)] - 1) + x
            eng.wait_ge(*ready)
            if head >= 3:
                r, m = place[list(PAIR)[(head - 3) // 2]]
                eng.wait_ge(filled[r], m)
            copy(pt[head % 3][0:P, lo:hi, i * P:(i + 1) * P], turned_tiles(x, i, lo, hi)).then_inc(done, 1)

        def heads_done(step):
            return 2 * (PAIR[("pair_end", *step[1:3])] - 1) + step[3] + (step[4] == T - 1)

        TURNED = {1: "norm1", 2: "rms2", 3: "rms3"}

        USED = {s: n + 1 for n, s in enumerate(x for x in ORDER if x[0] == "sum" and x[3] < T - 1)}

        def taken(eng, *keys):
            for key in keys:
                r, n = place[key]
                eng.wait_ge(emptied[r], n)

        def summed(eng, step):
            if step[3] < T - 1:
                eng.wait_ge(probs_used, USED[step])
            else:
                r, n = place[("sum", step[1], step[2])]
                eng.wait_ge(filled[r], n)

        with nc.Fori(0, B // 2) as turn:
          with nc.Block() as block:

            @block.sync
            def _(sp):
                for j in range(2):
                    sp.dma_start(hid[j][:, :, :], kept_d[bass.ds((turn * 2 + j) * NIN, KEEP), :]
                                 .rearrange("(t p) c -> p t c", p=P)).then_inc(hid_loaded[j], 16)
                for j in range(2):
                    for rows, name in ((Aq[j][R_PROD:R_MAX], "dist_q"), (Ak[j][R_PROD:R_ALL], "dist_k")):
                        sp.dma_start(rows, a[name].unsqueeze(1).broadcast_to([a[name].shape[0], H1, KEEP]))\
                            .then_inc(rows_loaded[j], 16)
                for step in ORDER:
                    kind, j, *w = step
                    if kind == "qk_split":
                        for m in range(2 * NK):
                            n = 2 * NK * (QK[step] - 1) + m
                            sp.wait_ge(lo_ready, n + 1)
                            side, k = divmod(m, NK)
                            sp.dma_start(parts_d[j, side, :, k * KC:(k + 1) * KC, :].rearrange("s p n -> p s n"),
                                         parts[n % 2][:, :, :]).then_inc(parts_out[n % 2], 16)
                        for i in range(2):
                            sp.wait_ge(parts_out[i], 16 * NK * QK[step])
                        for side, (dst, sel) in enumerate(((Aq, Q_PART), (Ak, K_PART))):
                            for g in range(NPROD):
                                sp.dma_start(dst[j][g * D1:(g + 1) * D1, :, :],
                                             parts_d[j, side, sel[g]].rearrange("(h d) n -> d h n", d=D1))\
                                    .then_inc(prod_in[j], 16)
                    elif kind == "max_parts":
                        taken(sp, step)
                        sp.dma_start(Aq[j][R_MAX:R_ALL, :, :], mrow[j][:, :]).then_inc(mrow_in[j], 16)
                    elif kind == "rotate":
                        m, = w
                        taken(sp, step)
                        if m >= RROT:
                            sp.wait_ge(rot_ready, ROT[("rotate", j, m - RROT)])
                        sp.dma_start(swap[j][m % RROT][0:64, :], plain[j][m % RROT][64:128, :])\
                            .then_inc(swapped[j][m % RROT], 16)
                        sp.dma_start(swap[j][m % RROT][64:128, :], plain[j][m % RROT][0:64, :])\
                            .then_inc(swapped[j][m % RROT], 16)
                    elif kind == "rms3":
                        sp.wait_ge(nrm_ready, NRM[step])
                        t0 = (turn * 2 + j) * T
                        sp.dma_start(moe_in_d[bass.ds(t0, T)].rearrange("t p c -> p t c"),
                                     nrm[j][:, :, :]).then_inc(stored, 16)
                        sp.dma_start(res_d[bass.ds(t0, T)].rearrange("t p c -> p t c"),
                                     hid[j][:, :, :]).then_inc(stored, 16)
                    elif kind == "route_logits":
                        taken(sp, step)
                        sp.dma_start(logit_d[bass.ds((turn * 2 + j) * T, T)].rearrange("t p c -> p t c"),
                                     logit[j][:, :, :]).then_inc(stored, 16)
                sp.wait_ge(stored, 2 * 3 * 16)

            @block.tensor
            def _(pe):
                def begin(key):
                    r, n = place[key]
                    if n > 1:
                        pe.wait_ge(emptied[r], n - 1)
                    return region[r], filled[r]

                def turn_rows(src, key0, key1):
                    for key, tiles in ((key0, range(T - 1)), (key1, range(T - 1, T))):
                        dst, done = begin(key)
                        for k in range(NK):
                            for t in tiles:
                                o = 512 * k + P * (t - tiles[0])
                                ins = nc.tensor.transpose(dst[0:KC, o:o + P], src[:, t, k * KC:(k + 1) * KC],
                                                          ident[0:P, 0:P])
                        ins.then_inc(done, 1)

                def rows_times(lhs, rhs, steps, key0, key1):
                    for key, tiles in ((key0, range(T - 1)), (key1, range(T - 1, T))):
                        dst, done = begin(key)
                        for t in tiles:
                            o = CS * (t - tiles[0])
                            for k in range(steps):
                                ins = nc.tensor.matmul(dst[0:P, o:o + C], lhs[:, k, t * P:(t + 1) * P], rhs[:, k, :],
                                                       start=(k == 0), stop=(k == steps - 1))
                        ins.then_inc(done, 1)

                def channels_times(lhs, rhs, rows, key):
                    dst, done = begin(key)
                    for c in range(NCH):
                        for k in range(NK):
                            ins = nc.tensor.matmul(dst[0:rows, c * CS:c * CS + CH], lhs[:, k, :],
                                                   rhs[:, k, c * CH:(c + 1) * CH], start=(k == 0), stop=(k == NK - 1))
                    ins.then_inc(done, 1)

                def scores1(dst, rows, lhs, rhs, tile):
                    for c in range(NCH):
                        ins = nc.tensor.matmul(dst[0:P, c * CS:c * CS + CH], lhs[0:rows, tile * P:(tile + 1) * P],
                                               rhs[0:rows, c * CH:(c + 1) * CH], start=True, stop=False,
                                               skip_group_check=True)
                        lo, hi = max(tile * P, c * CH), min((tile + 1) * P, (c + 1) * CH)
                        if lo < hi:
                            ins = nc.tensor.matmul(dst[0:P, c * CS + lo - c * CH:c * CS + hi - c * CH],
                                                   identb[0:P, 0:P], near[:, lo - tile * P:hi - tile * P],
                                                   start=False, stop=True, skip_group_check=True)
                    return ins

                def weighted_sum(step):
                    _, j, g, k = step
                    dst, done = begin(("sum", j, g)) if k == 0 else (region[3], filled[3])
                    taken(pe, *(("exp", j, g, k, hl) for hl in range(GH)))
                    for c in range(NCH):
                        for hl in range(GH):
                            ins = nc.tensor.matmul(
                                dst[VW * hl:VW * (hl + 1), c * CS:c * CS + CH], vals[j][:, k, g * GH + hl, :],
                                probs[SUM[step] % 2][:, hl, c * CH:(c + 1) * CH],
                                start=(k == 0 and c % 2 == 0), stop=(k == T - 1), skip_group_check=True)
                    ins.then_inc(probs_used if k < T - 1 else done, 1)

                pending_turn = []

                def turn_weights():
                    step = pending_turn.pop(0)
                    _, j, u, x, i = step
                    n = CAUSAL[step]
                    pe.wait_ge(prn_ready, n)
                    if i == 0 and heads_done(step):
                        pe.wait_ge(taken_last, heads_done(step))
                    elif n > 2:
                        pe.wait_ge(taken_act, n - 2)
                    for k in range(min(i + 1, T - 1)):
                        ins = nc.tensor.transpose(turned_tiles(x, i, 0, T - 1)[:, k, :],
                                                  pr[n % 5][:, k * P:(k + 1) * P], ident[0:P, 0:P])
                    ins.then_inc(turned, 1)
                    if i == T - 1:
                        pe.wait_ge(taken_act, n - 1)
                        nc.tensor.transpose(turned_tiles(x, i, i, T)[:, 0, :], pr[n % 5][:, i * P:T * P],
                                            ident[0:P, 0:P]).then_inc(turned_last, 1)

                for step in ORDER:
                    kind, j, *w = step
                    if kind in ("turn1", "turn2", "turn3"):
                        n = int(kind[-1])
                        pe.wait_ge(nrm_ready, NRM[(TURNED[n], j)])
                        turn_rows(tmp[j] if n == 2 else nrm[j], (kind, j, 0), (kind, j, 1))
                    elif kind == "qk_split":
                        taken(pe, ("turn1", j, 0), ("turn1", j, 1))
                        for m in range(2 * NK):
                            channels_times(w_qkv1[:, :, m * KC:(m + 1) * KC], xT[j], KC, (kind, j, m))
                    elif kind == "v1":
                        rows_times(xT[j], w_qkv1[:, :, 2 * C:3 * C], NK, (kind, j, 0), (kind, j, 1))
                    elif kind == "row_max":
                        h, i = w
                        if h == 0 and i == 0:
                            pe.wait_ge(prod_in[j], 16 * 2 * NPROD)
                            pe.wait_ge(rows_loaded[j], 16 * 2)
                        dst, done = begin((kind, j, h, i))
                        scores1(dst, R_MAX, Aq[j][:, h, :], Ak[j][:, h, :], i).then_inc(done, 1)
                    elif kind == "max_parts":
                        pe.wait_ge(rowp_ready, MP[step])
                        dst, done = begin((kind, j))
                        for t in range(T):
                            ins = nc.tensor.matmul(dst[0:PARTS * H1, PK * t:PK * t + P], rowp[j][:, t, :],
                                                   identb[0:P, 0:P], start=True, stop=True)
                        ins.then_inc(done, 1)
                    elif kind == "exp":
                        g, k, hl = w
                        if w == [0, 0, 0]:
                            pe.wait_ge(mrow_in[j], 16)
                            taken(pe, ("v1", j, 0), ("v1", j, 1))
                        h = g * GH + hl
                        dst, done = begin(step)
                        scores1(dst, R_ALL, Ak[j][:, h, :], Aq[j][:, h, :], k).then_inc(done, 1)
                    elif kind == "sum":
                        weighted_sum(step)
                    elif kind == "heads_out":
                        taken(pe, *(("sum", j, g) for g in range(NG)))
                        for t in range(T):
                            dst, done = begin(("turn_n", j, t))
                            for g in range(NG):
                                ins = nc.tensor.transpose(dst[0:P, 128 * g:128 * g + 128],
                                                          attn[j][:, g, t * P:(t + 1) * P], ident[:, :])
                            ins.then_inc(done, 1)
                        taken(pe, *(("turn_n", j, t) for t in range(T)))
                        turn_rows(tmp[j], ("turn_o", j, 0), ("turn_o", j, 1))
                        taken(pe, ("turn_o", j, 0), ("turn_o", j, 1))
                        rows_times(xT[j], w_proj1, NK, ("proj1", j, 0), ("proj1", j, 1))
                    elif kind == "rotate":
                        m, = w
                        if m == 0:
                            taken(pe, ("turn2", j, 0), ("turn2", j, 1))
                        channels_times(w_qkv2[:, :, m * 128:(m + 1) * 128], xT[j], 128, step)
                    elif kind == "v2":
                        rows_times(xT[j], w_qkv2[:, :, NROT * 128:], NK, (kind, j, 0), (kind, j, 1))
                    elif kind == "causal":
                        u, x, i = w
                        if (u, x, i) == (0, 0, 0):
                            pe.wait_ge(rot_ready, ROT[("rotate", j, NROT - 1)])
                            pe.wait_ge(keys_ready, 2 * j + 2)
                            taken(pe, ("v2", 1, 0), ("v2", 1, 1), *(("rotate", 1, m) for m in range(NROT)))
                        for m in SCORE_USERS[CAUSAL[step]]:
                            pe.wait_ge(exp_done, m)
                        slots = score_tiles(x, i)
                        keys = k2[j][:, u // 2, x, :].rearrange("p (t n) -> p t n", n=P)
                        lhs = q2[j][:, u, i * P:(i + 1) * P]
                        near_end = min(i + 1, T - 1)
                        for lo, hi in ((0, near_end), (near_end, i + 1)):
                            if lo < hi:
                                nc.tensor.matmul(slots[:, lo:hi, :], lhs, keys[:, lo:hi, :], start=True, stop=False,
                                                 skip_group_check=True)
                        nc.tensor.matmul(slots[:, i, :], identb[0:P, 0:P], future[:, :], start=False, stop=True,
                                         skip_group_check=True).then_inc(scored, 1)
                        pending_turn.append(step)
                        if len(pending_turn) > TURN_LAG:
                            turn_weights()
                    elif kind == "pair_end":
                        u, = w
                        while pending_turn and pending_turn[0][1:3] == (j, u):
                            turn_weights()
                        dst, done = begin((kind, j, u))
                        last = ("causal", j, u, 1, T - 1)
                        pe.wait_ge(taken_act, CAUSAL[last])
                        pe.wait_ge(taken_last, heads_done(last))
                        first = 2 * (PAIR[step] - 1)
                        half = 3 * P
                        for k in range(T):
                            for lo, hi, o in ((k * P, half, k * P), (max(half, k * P), KEEP, 512 + max(half, k * P) - half)):
                                if lo >= hi:
                                    continue
                                for x in range(2):
                                    ins = nc.tensor.matmul(
                                        dst[D2 * x:D2 * (x + 1), o:o + hi - lo], v2[j][:, k, D2 * (u // 2):D2 * (u // 2 + 1)],
                                        pt[(first + x) % 3][:, k, lo:hi], start=(k == 0), stop=(k == T - 1),
                                        skip_group_check=True)
                        ins.then_inc(done, 1)
                    elif kind == "out2":
                        taken(pe, ("pair_end", j, NPAIR - 1))
                        rows_times(attn[j], w_out2, NPAIR, (kind, j, 0), (kind, j, 1))
                    elif kind == "route_logits":
                        taken(pe, ("turn3", j, 0), ("turn3", j, 1))
                        dst, done = begin((kind, j))
                        for t in range(T):
                            for k in range(NK):
                                ins = nc.tensor.matmul(dst[0:P, E * t:E * t + E], xT[j][:, k, t * P:(t + 1) * P],
                                                       w_router[:, k, :], start=(k == 0), stop=(k == NK - 1))
                        ins.then_inc(done, 1)

            @block.scalar
            def _(act):
                def full(key):
                    r, n = place[key]
                    act.wait_ge(filled[r], n)
                    return region[r], emptied[r]

                def take_turned(j, key0, key1, scale=None):
                    for key, lo, hi in ((key0, 0, T - 1), (key1, T - 1, T)):
                        src, done = full(key)
                        n = (hi - lo) * P
                        if scale is None:
                            ins = nc.scalar.copy(xT[j][:, :, lo * P:hi * P],
                                                 src[0:KC, :].rearrange("p (k n) -> p k n", k=NK)[:, :, 0:n])
                        else:
                            for k in range(NK):
                                ins = nc.scalar.activation(xT[j][:, k, lo * P:hi * P], src[0:KC, 512 * k:512 * k + n],
                                                           ACT.Copy, scale=scale[:, k:k + 1])
                        ins.then_inc(done, 1)

                pending_take = []

                def take_weights():
                    step = pending_take.pop(0)
                    take_turned_weights(act, nc.scalar.copy, step, 0, min(step[-1] + 1, T - 1),
                                        (turned, CAUSAL[step]), taken_act)

                for step in ORDER:
                    kind, j, *w = step
                    if kind in ("turn1", "turn2", "turn3"):
                        take_turned(j, (kind, j, 0), (kind, j, 1), norm1 if kind == "turn2" else None)
                    elif kind == "qk_split":
                        for m in range(2 * NK):
                            n = 2 * NK * (QK[step] - 1) + m
                            if n >= 2:
                                act.wait_ge(rest_ready, n - 1)
                                act.wait_ge(parts_out[n % 2], 16 * (n // 2))
                            src, done = full((kind, j, m))
                            side, k = divmod(m, NK)
                            scale = q_factor[:, k:k + 1] if side == 0 else 1.0
                            bias = qb[:, k:k + 1] if side == 0 else b_qk1[:, NK + k:NK + k + 1]
                            for dst in (qk32[n % 2][0:KC, :], parts[n % 2][:, HI, :]):
                                ins = nc.scalar.activation(dst.rearrange("p (c n) -> p c n", n=CH), chunks(src, KC),
                                                           ACT.Identity, bias=bias, scale=scale)
                                ins.then_inc(qk32_ready if dst.dtype == F32 else done, 1)
                    elif kind == "max_parts":
                        src, done = full((kind, j))
                        ins = nc.scalar.copy(mrow[j][:, :].rearrange("p (t n) -> p t n", n=P),
                                             src[0:PARTS * H1, :].rearrange("p (t n) -> p t n", n=PK)[:, 0:T, 0:P])
                        ins.then_inc(done, 1)
                    elif kind == "exp":
                        g, k, hl = w
                        n = SUM[("sum", j, g, k)]
                        if n > 2 and hl == 0:
                            summed(act, step_before(("sum", j, g, k), 2))
                        src, done = full(step)
                        ins = nc.scalar.activation(
                            probs[n % 2][0:P, hl, :].rearrange("p (c n) -> p c n", n=CH), chunks(src, P),
                            ACT.Exp, scale=SLOPES[g * GH + hl])
                        ins.then_inc(done, 1)
                    elif kind == "group_end":
                        src, done = full(("sum", j, w[0]))
                        ins = nc.scalar.copy(attn[j][:, w[0], :].rearrange("p (c n) -> p c n", n=CH), chunks(src))
                        ins.then_inc(done, 1)
                    elif kind == "heads_out":
                        take_turned(j, ("turn_o", j, 0), ("turn_o", j, 1))
                    elif kind == "rotate":
                        m, = w
                        if m >= RROT:
                            before = ROT[("rotate", j, m - RROT)]
                            act.wait_ge(rot_ready, before)
                        src, done = full(step)
                        nc.scalar.copy(plain[j][m % RROT].rearrange("p (c n) -> p c n", n=CH), chunks(src))\
                            .then_inc(done, 1)
                    elif kind == "split_keys":
                        act.wait_ge(rot_ready, ROT[("rotate", j, NROT - 1)])
                        nc.scalar.activation(k2[j][:, :, 1, :], k2[j][:, :, 0, :], ACT.Copy, scale=own[:, 1:2])\
                            .then_inc(keys_ready, 1)
                        act.wait_ge(keys_ready, 2 * j + 1)
                        nc.scalar.activation(k2[j][:, :, 0, :], k2[j][:, :, 0, :], ACT.Copy, scale=own[:, 0:1])\
                            .then_inc(keys_ready, 1)
                    elif kind == "v2":
                        for i, (lo, hi) in enumerate(((0, T - 1), (T - 1, T))):
                            src, done = full((kind, j, i))
                            ins = nc.scalar.copy(v2[j][0:P, lo:hi, :],
                                                 src[0:P, :].rearrange("p (t n) -> p t n", n=CS)[:, 0:hi - lo, 0:C])
                            ins.then_inc(done, 1)
                    elif kind == "causal":
                        u, x, i = w
                        n = CAUSAL[step]
                        pending_take.append(step)
                        if len(pending_take) > TAKE_LAG:
                            take_weights()
                        act.wait_ge(nm_ready, n)
                        if n > 5:
                            act.wait_ge(turned, n - 5)
                        nc.scalar.activation(
                            pr[n % 5][:, 0:(i + 1) * P].rearrange("p (t n) -> p t n", n=P),
                            score_tiles(x, i), ACT.Exp, bias=nm[:, n % RING:n % RING + 1],
                            accum_out=den[:, n % RING:n % RING + 1]).then_inc(exp_done, 1)
                    elif kind == "pair_end":
                        while pending_take and pending_take[0][1:3] == (j, w[0]):
                            take_weights()
                    elif kind == "route_logits":
                        src, done = full((kind, j))
                        ins = nc.scalar.copy(logit[j][:, :, :], src[0:P, 0:T * E].rearrange("p (t e) -> p t e", e=E))
                        ins.then_inc(done, 1)

            @block.vector
            def _(dve):
                link = chain(dve, dve_self)

                def full(key):
                    r, n = place[key]
                    dve.wait_ge(filled[r], n)
                    return region[r], emptied[r]

                def rows(src, n):
                    return src[0:P, :].rearrange("p (t n) -> p t n", n=CS)[:, 0:n, 0:C]

                def wide(row, n):
                    return row[:, :].unsqueeze(1).broadcast_to([P, n, C])

                def mean_of_squares(src, j):
                    for t in range(T):
                        link(nc.vector.tensor_tensor_reduce(junk[:, :], src[:, t, :], src[:, t, :], 1.0 / C, RMS_EPS,
                                                            ALU.mult, ALU.add, var[j][:, t:t + 1]))
                    nc.vector.engine_nop().then_inc(var_ready, 1)

                pending_norm, pending_take = [], []

                def normalise():
                    step = pending_norm.pop(0)
                    n, i = CAUSAL[step], step[-1]
                    dve.wait_ge(exp_done, n)
                    link(nc.vector.reciprocal(rden[:, n % RING:n % RING + 1], den[:, n % RING:n % RING + 1]))
                    v = pr[n % 5][:, 0:(i + 1) * P]
                    nc.vector.tensor_scalar(v, v, rden[:, n % RING:n % RING + 1], None, ALU.mult).then_inc(prn_ready, 1)

                def take_weights():
                    step = pending_take.pop(0)
                    if step[-1] == T - 1:
                        take_turned_weights(dve, nc.vector.tensor_copy, step, T - 1, T,
                                            (turned_last, heads_done(step)), taken_last)

                for step in ORDER:
                    kind, j, *w = step
                    if kind in ("norm1_stats", "norm2_stats"):
                        if kind == "norm1_stats":
                            dve.wait_ge(hid_loaded[j], 16)
                        for t in range(T):
                            link(nc.vector.bn_stats(stats[j][:, t, :], hid[j][:, t, :]), wait=t == T - 1)
                        for t in range(T):
                            link(nc.vector.bn_aggr(mv[j][:, t, :], stats[j][:, t, :]), wait=t == T - 1)
                        nc.vector.tensor_scalar(var[j][:, :], mv[j][:, :, 1], LN_EPS, None, ALU.add)\
                            .then_inc(var_ready, 1)
                    elif kind in ("norm1", "norm2"):
                        dve.wait_ge(rstd_ready, VAR[(kind + "_stats", j)])
                        for t in range(T):
                            ins = nc.vector.tensor_scalar(nrm[j][:, t, :], hid[j][:, t, :], mv[j][:, t, 0:1],
                                                          rstd[j][:, t:t + 1], ALU.subtract, ALU.mult)
                            if kind == "norm2":
                                link(ins, wait=t == T - 1)
                        if kind == "norm1":
                            ins.then_inc(nrm_ready, 1)
                    elif kind == "norm2_rms":
                        mean_of_squares(nrm[j], j)
                    elif kind == "rms2":
                        dve.wait_ge(rstd_ready, VAR[("norm2_rms", j)])
                        for t in range(T):
                            ins = nc.vector.tensor_scalar(tmp[j][:, t, :], nrm[j][:, t, :], rstd[j][:, t:t + 1], None,
                                                          ALU.mult)
                        ins.then_inc(nrm_ready, 1)
                    elif kind == "qk_split":
                        for m in range(2 * NK):
                            n = 2 * NK * (QK[step] - 1) + m
                            dve.wait_ge(qk32_ready, n + 1)
                            taken(dve, (kind, j, m))
                            if n >= 2:
                                dve.wait_ge(lo_ready, n - 1)
                            i = n % 2
                            nc.vector.tensor_tensor(rest[i][0:KC, :], qk32[i][0:KC, :], parts[i][:, HI, :],
                                                    ALU.subtract).then_inc(rest_ready, 1)
                            dve.wait_ge(rest_ready, n + 1)
                            nc.vector.tensor_copy(parts[i][:, MID, :], rest[i][0:KC, :]).then_inc(mid_ready, 1)
                    elif kind == "v1":
                        for i, (lo, hi) in enumerate(((0, T - 1), (T - 1, T))):
                            src, done = full((kind, j, i))
                            ins = nc.vector.tensor_tensor(
                                vals[j][0:P, lo:hi, :, 0:D1], rows(src, hi - lo).rearrange("p t (h d) -> p t h d", d=D1),
                                wide(b_v1, hi - lo).rearrange("p t (h d) -> p t h d", d=D1), ALU.add)
                            ins.then_inc(done, 1)
                    elif kind == "row_max":
                        h, i = w
                        src, done = full((kind, j, h, i))
                        nc.vector.tensor_reduce(mx[j][:, h, i:i + 1], chunks(src, P), AX.XY, ALU.max)\
                            .then_inc(done, 1)
                    elif kind == "max_parts":
                        taken(dve, ("row_max", j, H1 - 1, T - 1))
                        by_tile = [rowp[j][:, :, s * H1:(s + 1) * H1].rearrange("p t h -> p h t") for s in range(PARTS)]
                        link(nc.vector.tensor_scalar(mtmp[:, 0], mx[j][:, :, :], -1.0, None, ALU.mult))
                        link(nc.vector.tensor_copy(by_tile[HI], mtmp[:, 0]))
                        link(nc.vector.tensor_tensor(mtmp[:, 1], mtmp[:, 0], by_tile[HI], ALU.subtract))
                        link(nc.vector.tensor_copy(by_tile[MID], mtmp[:, 1]))
                        nc.vector.tensor_tensor(by_tile[LO], mtmp[:, 1], by_tile[MID], ALU.subtract)\
                            .then_inc(rowp_ready, 1)
                    elif kind == "heads_out":
                        link(nc.vector.tensor_tensor(nrm[j][:, :, :], hid[j][:, :, :], wide(b_proj1, T), ALU.add))
                        for t in range(T):
                            src, done = full(("turn_n", j, t))
                            v = src[0:P, 0:H1 * VW].rearrange("p (h n) -> p h n", n=VW)
                            link(nc.vector.reciprocal(recip[:, t, :], v[:, :, D1]))
                            ins = nc.vector.tensor_tensor(
                                tmp[j][:, t, :].rearrange("p (h d) -> p h d", d=D1), v[:, :, 0:D1],
                                recip[:, t, :].unsqueeze(2).broadcast_to([P, H1, D1]), ALU.mult)
                            ins.then_inc(done, 1)
                        for i, (lo, hi) in enumerate(((0, T - 1), (T - 1, T))):
                            src, done = full(("proj1", j, i))
                            ins = nc.vector.tensor_tensor(hid[j][:, lo:hi, :], rows(src, hi - lo), nrm[j][:, lo:hi, :], ALU.add)
                            ins.then_inc(done, 1)
                            taken(dve, ("proj1", j, i))
                    elif kind == "rotate":
                        m, = w
                        dst = q2[j][:, m, :] if m < NPAIR else k2[j][:, m - NPAIR, 0, :]
                        taken(dve, step)
                        nc.vector.tensor_tensor(dst, plain[j][m % RROT], rope[:, 0, :], ALU.mult)\
                            .then_inc(cos_ready, 1)
                        dve.wait_ge(cos_ready, ROT[step])
                        dve.wait_ge(sin_ready, ROT[step])
                        nc.vector.tensor_tensor(dst, dst, swap[j][m % RROT], ALU.add).then_inc(rot_ready, 1)
                    elif kind == "causal":
                        u, x, i = w
                        n = CAUSAL[step]
                        pending_norm.append(step)
                        pending_take.append(step)
                        if len(pending_take) > TAKE_LAG:
                            take_weights()
                        if len(pending_norm) > NORM_LAG:
                            normalise()
                        dve.wait_ge(scored, n)
                        nc.vector.tensor_reduce(nm[:, n % RING:n % RING + 1], score_tiles(x, i), AX.XY, ALU.max,
                                                negate=True).then_inc(nm_ready, 1)
                    elif kind == "pair_end":
                        u, = w
                        while pending_norm and pending_norm[0][1:3] == (j, u):
                            normalise()
                        while pending_take and pending_take[0][1:3] == (j, u):
                            take_weights()
                    elif kind == "pair_take":
                        u, = w
                        src, done = full(("pair_end", j, u))
                        half = 3 * P
                        link(nc.vector.tensor_copy(attn[j][:, u, 0:half], src[:, 0:half]), wait=False)
                        ins = nc.vector.tensor_copy(attn[j][:, u, half:KEEP], src[:, 512:512 + KEEP - half])
                        ins.then_inc(done, 1)
                    elif kind == "out2":
                        for i, (lo, hi) in enumerate(((0, T - 1), (T - 1, T))):
                            src, done = full((kind, j, i))
                            ins = nc.vector.tensor_tensor(tmp[j][:, lo:hi, :], rows(src, hi - lo), nrm[j][:, lo:hi, :], ALU.add)
                            ins.then_inc(done, 1)
                            taken(dve, (kind, j, i))
                            link(nc.vector.tensor_tensor(hid[j][:, lo:hi, :], hid[j][:, lo:hi, :], tmp[j][:, lo:hi, :], ALU.add),
                                 wait=False)
                    elif kind == "rms3_stats":
                        mean_of_squares(tmp[j], j)
                    elif kind == "rms3":
                        dve.wait_ge(rstd_ready, VAR[("rms3_stats", j)])
                        for t in range(T):
                            ins = nc.vector.scalar_tensor_tensor(out=nrm[j][:, t, :], in0=tmp[j][:, t, :],
                                                                 scalar=rstd[j][:, t:t + 1], in1=norm2_row[:, :],
                                                                 op0=ALU.mult, op1=ALU.mult)
                        ins.then_inc(nrm_ready, 1)

            @block.gpsimd
            def _(pool):
                for step in ORDER:
                    kind, j, *w = step
                    if step in VAR:
                        pool.wait_ge(var_ready, VAR[step])
                        nc.gpsimd.tensor_tensor(rstd[j][:, :], var[j][:, :], neg_half[:, :], ALU.pow)\
                            .then_inc(rstd_ready, 1)
                    elif kind == "qk_split":
                        for m in range(2 * NK):
                            n = 2 * NK * (QK[step] - 1) + m
                            pool.wait_ge(mid_ready, n + 1)
                            i = n % 2
                            nc.gpsimd.tensor_tensor(parts[i][:, LO, :], rest[i][0:KC, :], parts[i][:, MID, :],
                                                    ALU.subtract).then_inc(lo_ready, 1)
                    elif kind == "rotate":
                        m, = w
                        pool.wait_ge(swapped[j][m % RROT], 32 * (m // RROT + 1))
                        nc.gpsimd.tensor_tensor(swap[j][m % RROT], swap[j][m % RROT], rope[:, 1, :], ALU.mult)\
                            .then_inc(sin_ready, 1)

          nc.all_engine_barrier(sems_to_clear=range(sems[0].num, sems[-1].num + 1))


def experts(nc, a, region, ident, identb, moe_in_d, res_d, logit_d, slot_x_d, slot_y_d, out):
    es = ExitStack()
    with es:
        def sb(name, shape, dt=F32):
            return es.enter_context(nc.sbuf_tensor("x_" + name, shape, dt))

        def sem(name):
            return es.enter_context(nc.semaphore("ex_" + name))

        logit = sb("logit", [P, NT, E])
        rows_in = sb("rows_in", [P, NT, C])
        res = sb("res", [P, NT, C])
        before32, before = sb("before32", [P, P]), sb("before", [P, P], BF16)
        ones = sb("ones", [P, P], BF16)
        counts = sb("counts", [P, N_CNT])
        top = sb("top", [P, NT, 8])
        top_i = sb("top_i", [P, NT, 8], U32)
        top_f = sb("top_f", [P, NT, TOPK])
        gap = sb("gap", [P, NT])
        share = [sb(f"share{k}", [P, NT]) for k in range(TOPK)]
        hot = [sb(f"hot{k}", [P, NT, E]) for k in range(TOPK)]
        hot_sum = sb("hot_sum", [P, NT, E], BF16)
        total, upto = sb("total", [P, E, NT]), sb("upto", [P, E, NT])
        pos, picked = sb("pos", [P, NT, E]), sb("picked", [P, NT, E])
        over = sb("over", [P, E, WMAX])
        n_tiles, end, base = sb("n_tiles", [P, E]), sb("end", [P, E]), sb("base", [P, E])
        passed, who = sb("passed", [1, NST, E]), sb("who", [1, NST])
        who_i = sb("who_i", [1, NST], I32)
        slot = sb("slot", [P, NT])
        slot_i = [sb(f"slot_i{k}", [P, NT], I32) for k in range(TOPK)]
        w_gu = [sb(f"w_gu{i}", [KC, NK, 2 * FF]) for i in range(RX)]
        w_dn = [sb(f"w_dn{i}", [ST, MF, C]) for i in range(RX)]
        x_t = [sb(f"x_t{i}", [ST, C]) for i in range(RX)]
        xT = [sb(f"xT{i}", [KC, NK, ST]) for i in range(2)]
        act_g = [sb(f"act_g{i}", [ST, MF, ST]) for i in range(2)]
        hidden = [sb(f"hidden{i}", [ST, MF, ST]) for i in range(2)]
        y_t = [sb(f"y_t{i}", [ST, C]) for i in range(RX)]
        y_in = sb("y_in", [P, NT * TOPK, C])

        logit_in, rows_loaded, res_in, tables_in = sem("logit_in"), sem("rows_loaded"), sem("res_in"), sem("tables_in")
        dve_self = sem("dve_self")
        gap_ready, share_exp = sem("gap_ready"), sem("share_exp")
        hot_ready, prefix_ready = sem("hot_ready"), sem("prefix_ready")
        slots_ready, who_ready = sem("slots_ready"), sem("who_ready")
        scattered, gathered = sem("scattered"), [sem(f"gathered{b}") for b in range(B)]
        gu_free, dn_free = sem("gu_free"), sem("dn_free")
        gu_in = [sem(f"gu_in{i}") for i in range(RX)]
        dn_in = [sem(f"dn_in{i}") for i in range(RX)]
        x_in = [sem(f"x_in{i}") for i in range(RX)]
        x_turned, xT_ready = sem("x_turned"), sem("xT_ready")
        gu_done, g_ready, h_ready = sem("gu_done"), sem("g_ready"), sem("h_ready")
        y_done, y_ready = sem("y_done"), sem("y_ready")
        y_out = [sem(f"y_out{i}") for i in range(RX)]
        combined, stored = sem("combined"), sem("stored")

        c0 = 0
        number = counts[:, c0:c0 + E]
        c0 += E
        thresholds = counts[:, c0:c0 + WMAX]
        c0 += WMAX
        tile_no = counts[0:1, c0:c0 + NST]
        c0 += NST
        restart = counts[:, c0:c0 + E * NT]
        c0 += E * NT
        no_restart = counts[:, c0:c0 + E]
        def third(m, up):
            at = 512 * (m % 2) + up * ST
            return region[1 + m // 2][:, at:at + ST]

        LAST = NST // RX - 1
        assert NST % RX == 0

        with nc.Block() as block:
            @block.sync
            def _(sp):
                def load(n, s):
                    e = sp.value_load(who_i[0:1, bass.ds(n, 1)], min_val=0, max_val=E - 1)
                    sp.wait_ge(gu_free, n + 1)
                    sp.dma_start(x_t[s][:, :], slot_x_d[bass.ds(n * ST, ST), :]).then_inc(x_in[s], 16)
                    sp.dma_start(w_gu[s][:, :, :], a["w_gate_up"][bass.ds(e, 1)]
                                 .rearrange("e (k p) n -> p (e k) n", p=KC)).then_inc(gu_in[s], 16)
                    sp.wait_ge(dn_free, n + 1)
                    sp.dma_start(w_dn[s][:, :, :], a["w_down"][bass.ds(e, 1)]
                                 .rearrange("e (k p) n -> p (e k) n", p=ST)).then_inc(dn_in[s], 16)

                def store(n, s):
                    sp.wait_ge(y_ready, n + 1)
                    sp.dma_start(slot_y_d[bass.ds(n * ST, ST), :], y_t[s][:, :]).then_inc(y_out[s], 16)

                sp.dma_start(logit[:, :, :], logit_d.rearrange("t p e -> p t e")).then_inc(logit_in, 16)
                sp.dma_start(rows_in[:, :, :], moe_in_d.rearrange("t p c -> p t c")).then_inc(rows_loaded, 16)
                sp.wait_ge(who_ready, 1)
                sp.wait_ge(scattered, 16 * NT * TOPK)
                for s in range(RX):
                    load(s, s)
                with sp.Fori(0, LAST) as it:
                    for s in range(RX):
                        store(it * RX + s, s)
                        load(it * RX + (RX + s), s)
                for s in range(RX):
                    store(NST - RX + s, s)
                for b in range(B):
                    sp.wait_ge(combined, b + 1)
                    sp.dma_start(out[b].rearrange("(t p) c -> p t c", p=P),
                                 res[:, b * T:(b + 1) * T, :]).then_inc(stored, 16)
                sp.wait_ge(stored, 16 * B)

            @block.scalar
            def _(act):
                act.dma_start(before32[:, :], a["before"]).then_inc(tables_in, 16)
                act.dma_start(counts[:, :], a["counts"].broadcast_to([P, N_CNT])).then_inc(tables_in, 16)
                act.dma_start(res[:, :, :], res_d.rearrange("t p c -> p t c")).then_inc(res_in, 16)
                act.wait_ge(gap_ready, 1)
                nc.scalar.activation(share[1][:, :], gap[:, :], ACT.Exp).then_inc(share_exp, 1)
                for s in range(RX):
                    act.sem_inc(y_out[s], 16)

                def gates(n, s):
                    for m in range(MF):
                        act.wait_ge(gu_done, n * MF + (m + 1))
                        nc.scalar.activation(act_g[s % 2][:, m, :], third(m, 0), ACT.Silu)\
                            .then_inc(g_ready, 1)

                def take_y(n, s, turn):
                    act.wait_ge(y_done, n + 1)
                    act.wait_ge(y_out[s], turn * 16 + 16)
                    o = 512 * (s % 2)
                    nc.scalar.copy(y_t[s][:, :], region[3][:, o:o + C]).then_inc(y_ready, 1)

                gates(0, 0)
                with act.Fori(0, LAST) as it:
                    for s in range(RX):
                        gates(it * RX + (1 + s), s + 1)
                        take_y(it * RX + s, s, it)
                for s in range(RX):
                    if s < RX - 1:
                        gates(NST - RX + s + 1, s + 1)
                    take_y(NST - RX + s, s, LAST)

            @block.vector
            def _(dve):
                link = chain(dve, dve_self)
                dve.wait_ge(logit_in, 16)
                for t in range(NT):
                    link(nc.vector.max(top[:, t, :], logit[:, t, :]), wait=t == NT - 1)
                for t in range(NT):
                    link(nc.vector.max_index(top_i[:, t, :], top[:, t, :], logit[:, t, :]), wait=t == NT - 1)
                nc.vector.tensor_tensor(gap[:, :], top[:, :, 1], top[:, :, 0], ALU.subtract).then_inc(gap_ready, 1)
                link(nc.vector.tensor_copy(top_f[:, :, :], top_i[:, :, 0:TOPK]))
                dve.wait_ge(tables_in, 32)
                link(nc.vector.tensor_copy(before[:, :], before32[:, :]), wait=False)
                link(nc.vector.memset(ones[:, :], 1.0), wait=False)
                for k in range(TOPK):
                    link(nc.vector.tensor_tensor(hot[k][:, :, :], number.unsqueeze(1).broadcast_to([P, NT, E]),
                                                 top_f[:, :, k:k + 1].broadcast_to([P, NT, E]), ALU.is_equal))
                nc.vector.tensor_tensor(hot_sum[:, :, :], hot[0][:, :, :], hot[1][:, :, :], ALU.add)\
                    .then_inc(hot_ready, 1)
                dve.wait_ge(share_exp, 1)
                link(nc.vector.tensor_scalar(gap[:, :], share[1][:, :], 1.0, None, ALU.add))
                link(nc.vector.reciprocal(share[0][:, :], gap[:, :]))
                link(nc.vector.tensor_tensor(share[1][:, :], share[1][:, :], share[0][:, :], ALU.mult))
                dve.wait_ge(prefix_ready, 1)
                by_tile = lambda r: r[0:P, 0:NT * E].rearrange("p (t e) -> p t e", e=E)
                link(nc.vector.tensor_copy(total[:, :, :].rearrange("p e t -> p t e"), by_tile(region[1])))
                link(nc.vector.tensor_tensor_scan(upto[:, :, :].rearrange("p e t -> p (e t)"), restart,
                                                  total[:, :, :].rearrange("p e t -> p (e t)"), 0.0, ALU.mult, ALU.add))
                link(nc.vector.tensor_tensor(over[:, :, :], upto[:, :, NT - 1:NT].broadcast_to([P, E, WMAX]),
                                             thresholds.unsqueeze(1).broadcast_to([P, E, WMAX]), ALU.is_gt))
                link(nc.vector.tensor_reduce(n_tiles[:, :], over[:, :, :], AX.X, ALU.add))
                link(nc.vector.tensor_tensor_scan(end[:, :], no_restart, n_tiles[:, :], 0.0, ALU.mult, ALU.add))
                link(nc.vector.tensor_tensor(base[:, :], end[:, :], n_tiles[:, :], ALU.subtract))
                link(nc.vector.tensor_scalar(base[:, :], base[:, :], float(ST), None, ALU.mult))
                link(nc.vector.tensor_tensor(passed[:, :, :], tile_no.unsqueeze(2).broadcast_to([1, NST, E]),
                                             end[0:1, :].unsqueeze(1).broadcast_to([1, NST, E]), ALU.is_ge))
                link(nc.vector.tensor_reduce(who[:, :], passed[:, :, :], AX.X, ALU.add))
                link(nc.vector.tensor_scalar(who[:, :], who[:, :], float(E - 1), None, ALU.min))
                nc.vector.tensor_copy(who_i[:, :], who[:, :]).then_inc(who_ready, 1)
                link(nc.vector.tensor_tensor(upto[:, :, :], upto[:, :, :], total[:, :, :], ALU.subtract))
                link(nc.vector.tensor_tensor(pos[:, :, :], by_tile(region[0]),
                                             upto[:, :, :].rearrange("p e t -> p t e"), ALU.add))
                link(nc.vector.tensor_tensor(pos[:, :, :], pos[:, :, :],
                                             base[:, :].unsqueeze(1).broadcast_to([P, NT, E]), ALU.add))
                for k in range(TOPK):
                    link(nc.vector.tensor_tensor(picked[:, :, :], hot[k][:, :, :], pos[:, :, :], ALU.mult))
                    link(nc.vector.tensor_reduce(slot[:, :], picked[:, :, :], AX.X, ALU.add))
                    ins = nc.vector.tensor_copy(slot_i[k][:, :], slot[:, :])
                    ins.then_inc(slots_ready, 1)
                    dve.wait_ge(slots_ready, k + 1)

                def take_x(n, s):
                    dve.wait_ge(x_turned, n + 1)
                    o = 512 * (s % 2)
                    nc.vector.tensor_copy(xT[s % 2][:, :, :], region[0][0:KC, o:o + NK * ST]
                                          .rearrange("p (k n) -> p k n", k=NK)).then_inc(xT_ready, 1)

                def products(n, s):
                    for m in range(MF):
                        dve.wait_ge(g_ready, n * MF + (m + 1))
                        nc.vector.tensor_tensor(hidden[s % 2][:, m, :], third(m, 1), act_g[s % 2][:, m, :],
                                                ALU.mult).then_inc(h_ready, 1)

                take_x(0, 0)
                take_x(1, 1)
                products(0, 0)
                with dve.Fori(0, LAST) as it:
                    for s in range(RX):
                        take_x(it * RX + (2 + s), s)
                        products(it * RX + (1 + s), s + 1)
                for s in range(RX - 1):
                    if s < RX - 2:
                        take_x(NST - RX + 2 + s, s)
                    products(NST - RX + 1 + s, s + 1)
                dve.wait_ge(res_in, 16)
                for b in range(B):
                    dve.wait_ge(gathered[b], 16 * T * TOPK)
                    for k in range(TOPK):
                        for t in range(b * T, (b + 1) * T):
                            ins = nc.vector.scalar_tensor_tensor(
                                out=res[:, t, :], in0=y_in[:, t * TOPK + k, :], scalar=share[k][:, t:t + 1],
                                in1=res[:, t, :], op0=ALU.mult, op1=ALU.add)
                            if k == 0:
                                link(ins, wait=t == (b + 1) * T - 1)
                    ins.then_inc(combined, 1)

            @block.tensor
            def _(pe):
                pe.wait_ge(hot_ready, 1)
                pairs_in = hot_sum[:, :, :].rearrange("p t e -> p (t e)")
                nc.tensor.matmul(region[0][0:P, 0:NT * E], before[:, :], pairs_in, start=True, stop=True)
                nc.tensor.matmul(region[1][0:P, 0:NT * E], ones[:, :], pairs_in, start=True, stop=True)\
                    .then_inc(prefix_ready, 1)
                pe.sem_inc(gu_free, RX)
                pe.sem_inc(dn_free, RX)
                pe.wait_ge(slots_ready, TOPK)

                def turn_x(n, s, turn):
                    pe.wait_ge(x_in[s], turn * 16 + 16)
                    for k in range(NK):
                        o = 512 * (s % 2) + k * ST
                        ins = nc.tensor.transpose(region[0][0:KC, o:o + ST],
                                                  x_t[s][:, k * KC:(k + 1) * KC], ident[:, :])
                    ins.then_inc(x_turned, 1)

                def gate_up(n, s, turn, first=False):
                    pe.wait_ge(xT_ready, n + 1)
                    pe.wait_ge(gu_in[s], turn * 16 + 16)
                    for m in range(MF):
                        if not first:
                            pe.wait_ge(h_ready, n * MF + (m + 1 - MF))
                        for up, o in enumerate((0, FF)):
                            for k in range(NK):
                                ins = nc.tensor.matmul(third(m, up),
                                                       w_gu[s][:, k, o + m * ST:o + (m + 1) * ST], xT[s % 2][:, k, :],
                                                       start=(k == 0), stop=(k == NK - 1))
                        ins.then_inc(gu_done, 1)
                    pe.wait_ge(gu_done, n * MF + MF)
                    pe.sem_inc(gu_free, 1)

                def down(n, s, turn, first=False):
                    pe.wait_ge(dn_in[s], turn * 16 + 16)
                    pe.wait_ge(h_ready, n * MF + MF)
                    if not first:
                        pe.wait_ge(y_ready, n - 1)
                    o = 512 * (s % 2)
                    for m in range(MF):
                        ins = nc.tensor.matmul(region[3][:, o:o + C], hidden[s % 2][:, m, :], w_dn[s][:, m, :],
                                               start=(m == 0), stop=(m == MF - 1))
                    ins.then_inc(y_done, 1)
                    pe.wait_ge(y_done, n + 1)
                    pe.sem_inc(dn_free, 1)

                def tile_step(it, s, first=False, last=False):
                    n, after = it * RX + s, lambda d: (s + d) % RX
                    wrap = lambda d: it + (s + d) // RX
                    if not (last and s + 2 >= RX):
                        turn_x(n + 2, after(2), wrap(2))
                    if not (last and s + 1 >= RX):
                        gate_up(n + 1, after(1), wrap(1))
                    down(n, s, it, first=first and s < 2)

                turn_x(0, 0, 0)
                turn_x(1, 1, 0)
                gate_up(0, 0, 0, first=True)
                for s in range(RX):
                    tile_step(0, s, first=True)
                with pe.Fori(1, LAST) as it:
                    for s in range(RX):
                        tile_step(it, s)
                for s in range(RX):
                    tile_step(LAST, s, last=True)

            @block.gpsimd
            def _(pool):
                pool.wait_ge(rows_loaded, 16)
                for k in range(TOPK):
                    pool.wait_ge(slots_ready, k + 1)
                    for t in range(NT):
                        nc.gpsimd.indirect_dma_start(
                            slot_x_d, bass.IndirectOffsetOnAxis(ap=slot_i[k][:, t:t + 1], axis=0),
                            rows_in[:, t, :], None).then_inc(scattered, 16)
                for s in range(RX):
                    pool.wait_ge(y_out[s], 16 * (NST // RX + 1))
                for b in range(B):
                    for t in range(b * T, (b + 1) * T):
                        for k in range(TOPK):
                            nc.gpsimd.indirect_dma_start(
                                y_in[:, t * TOPK + k, :], None, slot_y_d,
                                bass.IndirectOffsetOnAxis(ap=slot_i[k][:, t:t + 1], axis=0)).then_inc(gathered[b], 16)


def lay_out(x, L0_tok_w, L0_tok_b, L0_attn_w_qkv, L0_attn_b_qkv, L0_attn_w_proj, L0_attn_b_proj, L0_ffn_norm1_w,
            L0_ffn_w_qkv, L0_ffn_w_out, L0_ffn_norm2_w, L0_ffn_w_router, L0_ffn_w_gate_up, L0_ffn_w_down):
    r = {"x": x, "tok_w": L0_tok_w.reshape(1, C), "tok_b": L0_tok_b.reshape(1, 1)}
    r["w_qkv1"] = L0_attn_w_qkv.T
    r["b_qk1"] = L0_attn_b_qkv[:2 * C].reshape(2 * NK, KC).T
    r["b_v1"] = L0_attn_b_qkv[2 * C:].reshape(1, C)
    r["w_proj1"] = L0_attn_w_proj.T
    r["b_proj1"] = L0_attn_b_proj.reshape(1, C)
    r["norm1"] = L0_ffn_norm1_w.reshape(NK, KC).T
    r["norm2_row"] = L0_ffn_norm2_w.reshape(1, C)
    w = L0_ffn_w_qkv
    nq, nk = H2 * D2, HKV * D2
    q = w[:, :nq].reshape(C, NPAIR, 2, HALF, 2).transpose(0, 1, 4, 2, 3).reshape(C, nq)
    k = w[:, nq:nq + nk].reshape(C, HKV, HALF, 2).transpose(0, 1, 3, 2).reshape(C, HKV, 2, 1, HALF)
    k = np.broadcast_to(k, (C, HKV, 2, 2, HALF)).reshape(C, 2 * nk)
    r["w_qkv2"] = np.concatenate([q, k, w[:, nq + nk:]], axis=1)
    r["w_out2"] = L0_ffn_w_out
    r["w_router"] = L0_ffn_w_router
    r["w_gate_up"] = L0_ffn_w_gate_up
    r["w_down"] = L0_ffn_w_down
    r.update(constants())
    return {n: np.ascontiguousarray(v) for n, v in r.items()}


def kernel(**inputs):
    import concourse.bacc as bacc
    from concourse.bass_utils import run_bass_kernel_spmd

    nc = bacc.Bacc("TRN2", target_bir_lowering=False, num_devices=1)
    arrays, aps = {}, {}
    for name, v in lay_out(**{n: np.asarray(v) for n, v in inputs.items()}).items():
        arrays[f"in_{name}"] = v
        aps[name] = nc.dram_tensor(f"in_{name}", v.shape, mybir.dt.from_np(v.dtype), kind="ExternalInput").ap()
    out = nc.dram_tensor("out", [B, KEEP, C], F32, kind="ExternalOutput").ap()
    audio_tower(nc, aps, out)
    r = run_bass_kernel_spmd(nc, [arrays], core_ids=[0])
    return r.results[0]["out"]
```

```python
from contextlib import ExitStack

import numpy as np
import concourse.bass as bass
from concourse import mybir

ALU = mybir.AluOpType
ACT = mybir.ActivationFunctionType
AX = mybir.AxisListType
F32 = mybir.dt.float32
BF16 = mybir.dt.bfloat16
I32 = mybir.dt.int32
U32 = mybir.dt.uint32

B, NIN, C = 4, 750, 192
KEEP = int(round(NIN * 0.7))
P_IN = 125
T_IN = NIN // P_IN
P = 105
T = KEEP // P
CH = 175
NCH = KEEP // CH
CS = 256
KC = 96
NK = C // KC

H1, D1 = 12, 16
PARTS = 3
HI, MID, LO = range(PARTS)
Q_PART = [HI, HI, HI, MID, MID, LO]
K_PART = [HI, MID, LO, HI, MID, HI]
NPROD = len(Q_PART)
R_PROD = NPROD * D1
R_DIST = 4 * T
R_MAX = R_PROD + R_DIST
R_ALL = R_MAX + PARTS
GH = 4
NG = H1 // GH
VW = 32

H2, HKV, D2 = 12, 3, 64
HALF = D2 // 2
NPAIR = H2 // 2
PK = 128
THETA = 10000.0

E, TOPK, FF = 16, 2, 384
NTOK = B * KEEP
NT = B * T
ST = 128
NST = (NTOK * TOPK + E * (ST - 1)) // ST
NSLOT = NST * ST
MF = FF // ST
WMAX = -(-NTOK // ST)
RX = 4

LN_EPS, RMS_EPS = 1e-5, 1e-6
SLOPES = [float(np.float32(2.0 ** (-8.0 / H1)) ** np.float32(h + 1)) for h in range(H1)]


def constants():
    c = {}
    c["ident"] = np.eye(128, dtype=np.float32)
    n = np.arange(KEEP)
    big, rest, tile = n // 4 * 4, n % 4, n // P
    q, k = np.zeros((R_DIST, KEEP), np.float32), np.zeros((R_DIST, KEEP), np.float32)
    for i in range(T):
        s = np.sign(tile - i)
        q[4 * i:4 * i + 4] = np.stack([big, rest, n >= 0, n >= 0]) * (tile == i)
        k[4 * i:4 * i + 4] = np.stack([s, s, -s * big, -s * rest])
    bf16 = mybir.dt.np(BF16)
    c["dist_q"] = q.astype(bf16)
    c["dist_k"] = np.concatenate([k, np.ones((PARTS, KEEP), np.float32)]).astype(bf16)
    m = np.arange(P)
    c["near"] = -np.abs(m[:, None] - m[None, :]).astype(bf16)
    c["future"] = np.where(m[None, :] > m[:, None], -1e30, 0.0).astype(bf16)
    t = np.arange(P_IN)
    c["earlier"] = (t[None, :] < t[:, None]).astype(np.float32)
    f = np.repeat(np.float32(D1 ** -0.5) / np.asarray(SLOPES, np.float32), D1)
    c["q_factor"] = np.ascontiguousarray(f.reshape(NK, KC).T.astype(np.float32))
    inv = (1.0 / np.float32(THETA) ** (np.arange(0, D2, 2, dtype=np.float32) / np.float32(D2)))
    a = np.arange(KEEP, dtype=np.float32)[None, :] * inv.astype(np.float32)[:, None]
    cos, sin = np.cos(a).astype(np.float32), np.sin(a).astype(np.float32)
    c["rope"] = np.ascontiguousarray(
        np.stack([np.concatenate([cos] * 4), np.concatenate([-sin, -sin, sin, sin])], axis=1))
    row = np.arange(128) // HALF
    c["own"] = np.stack([row % 2 == x for x in range(2)], axis=1) * np.float32(D2 ** -0.5)
    c["before"] = (m[:, None] < m[None, :]).astype(np.float32)
    marks = np.ones((E, NT), np.float32)
    marks[:, 0] = 0
    marks1 = np.ones(E, np.float32)
    c["counts"] = np.concatenate([
        np.arange(ST), np.arange(WMAX) * ST, np.arange(NST), marks.ravel(), marks1]).astype(np.float32)[None]
    pair = np.arange(NT)[None, None, :] * P + m[:, None, None] + np.arange(TOPK)[None, :, None] * NTOK + 1
    c["pair_no"] = np.stack([pair // 64, pair % 64], axis=3).astype(np.float32)
    slot = np.arange(NST)[None, :] * ST + np.arange(ST)[:, None]
    c["spare"] = np.concatenate([1 + NTOK * TOPK + slot, 1 + NTOK + slot[:, 0:1]], axis=1).astype(np.float32)
    return c


N_CNT = ST + WMAX + NST + E * NT + E


def audio_tower(nc, a, out):
    es = ExitStack()
    with es:
        def sb(name, shape, dt=F32):
            return es.enter_context(nc.sbuf_tensor(name, shape, dt))

        def dram(name, shape, dt=F32):
            return nc.dram_tensor(name, shape, dt, kind="Internal").ap()

        score_d = dram("score_d", [B * T_IN, P_IN])
        kept_d = dram("kept_d", [B * NIN, C])
        parts_d = dram("parts_d", [2, 2, PARTS, C, KEEP], BF16)
        moe_in_d = dram("moe_in_d", [NTOK + ST, C])
        res_d = dram("res_d", [NT, P, C])
        logit_d = dram("logit_d", [NT, P, E])
        pair_y_d = dram("pair_y_d", [NTOK * TOPK + NSLOT, C])

        region = [es.enter_context(nc.psum_tensor(f"region{i}", [128, 1024], F32)) for i in range(4)]

        ident = sb("ident", [128, 128])
        with ExitStack() as lasting_room:
            keep = lasting(lasting_room, nc, ident)
            sort_tokens(nc, a, region, keep, score_d, kept_d, moe_in_d)
            tower(nc, a, region, keep, kept_d, parts_d, moe_in_d, res_d, logit_d)
        experts(nc, a, region, ident, moe_in_d, res_d, logit_d, pair_y_d, out)


def chain(eng, sem):
    count = [0]

    def link(ins, wait=True):
        count[0] += 1
        ins.then_inc(sem, 1)
        if wait:
            eng.wait_ge(sem, count[0])
        return count[0]
    return link


def chunks(region, rows=128):
    return region[0:rows, :].rearrange("p (c x) -> p c x", x=CS)[:, 0:NCH, 0:CH]


class Lasting:
    pass


def lasting(es, nc, ident):
    def sb(name, shape, dt=F32):
        return es.enter_context(nc.sbuf_tensor(name, shape, dt))

    k = Lasting()
    k.ident, k.identb = ident, sb("identb", [128, 128], BF16)
    k.w_qkv1 = sb("w_qkv1", [KC, NK, 3 * C])
    k.w_proj1 = sb("w_proj1", [KC, NK, C])
    k.w_qkv2 = sb("w_qkv2", [KC, NK, (NPAIR + HKV) * 128 + HKV * D2])
    k.w_out2 = sb("w_out2", [128, NPAIR, C])
    k.w_router = sb("w_router", [KC, NK, E])
    k.b_qk1 = sb("b_qk1", [KC, 2 * NK])
    k.q_factor = sb("q_factor", [KC, NK])
    k.qb = sb("qb", [KC, NK])
    k.b_v1 = sb("b_v1", [P, C])
    k.b_proj1 = sb("b_proj1", [P, C])
    k.norm1 = sb("norm1", [KC, NK])
    k.norm2_row = sb("norm2_row", [P, C])
    k.near = sb("near", [P, P], BF16)
    k.future = sb("future", [P, P], BF16)
    k.rope = sb("rope", [128, 2, KEEP])
    k.own = sb("own", [128, 2])
    k.neg_half = sb("neg_half", [P, T])
    k.vals = [sb(f"vals{j}", [128, T, H1, VW]) for j in range(2)]
    k.v2 = [sb(f"v2{j}", [128, T, HKV * D2]) for j in range(2)]
    k.pt = [sb(f"pt{i}", [128, T, KEEP]) for i in range(3)]
    return k


def sort_tokens(nc, a, region, keep, score_d, kept_d, moe_in_d):
    es = ExitStack()
    with es:
        def sb(name, shape, dt=F32):
            return es.enter_context(nc.sbuf_tensor(name, shape, dt))

        def sem(name):
            return es.enter_context(nc.semaphore(name))

        ident, identb = keep.ident, keep.identb
        NB = B * T_IN
        x_in = sb("x_in", [P_IN, NB, C])
        tok_w = sb("tok_w", [P_IN, C])
        tok_b = sb("tok_b", [P_IN, 1])
        earlier = sb("earlier", [P_IN, P_IN])
        prod = sb("prod", [P_IN, T_IN, C])
        score = sb("score", [P_IN, NB])
        score_t = [sb(f"score_t{b}", [T_IN, P_IN]) for b in range(B)]
        all_scores = sb("all_scores", [P_IN, B, NIN])
        hit = sb("hit", [P_IN, T_IN // 2, NIN])
        same = sb("same", [P_IN, T_IN // 2, P_IN])
        cnt = sb("cnt", [P_IN, NB, 3])
        rank = sb("rank", [P_IN, NB])
        rank_i = sb("rank_i", [P_IN, NB], I32)
        zeros = sb("zeros", [ST, C])

        consts_in, tok_in = sem("so_consts_in"), sem("so_tok_in")
        x_loaded = [sem(f"so_x_loaded{b}") for b in range(B)]
        dve_self = sem("so_dve_self")
        tables_ready, weights_in = sem("so_tables_ready"), sem("so_weights_in")
        scores_ready = sem("so_scores_ready")
        scores_turned = sem("so_scores_turned")
        scores_row = sem("so_scores_row")
        scores_out = sem("so_scores_out")
        scores_back = [sem(f"so_scores_back{b}") for b in range(B)]
        ranks_ready = sem("so_ranks_ready")
        scattered = sem("so_scattered")
        zeros_ready, filled = sem("so_zeros_ready"), sem("so_filled")
        zeroed = sem("so_zeroed")

        with nc.Block() as block:
            @block.sync
            def _(sp):
                for b in range(B):
                    sp.dma_start(x_in[:, b * T_IN:(b + 1) * T_IN, :],
                                 a["x"][b].rearrange("(t p) c -> p t c", p=P_IN)).then_inc(x_loaded[b], 16)
                for b in range(B):
                    sp.wait_ge(scores_row, b + 1)
                    sp.dma_start(score_d[b * T_IN:(b + 1) * T_IN, :], score_t[b][:, :]).then_inc(scores_out, 16)
                    sp.wait_ge(scores_out, 16 * (b + 1))
                    src = score_d[b * T_IN:(b + 1) * T_IN, :].rearrange("(a t) p -> a (t p)", a=1)
                    sp.dma_start(all_scores[:, b, :], src.broadcast_to([P_IN, NIN])).then_inc(scores_back[b], 16)
                for t, n in ((keep.w_qkv1, "w_qkv1"), (keep.w_proj1, "w_proj1"), (keep.w_qkv2, "w_qkv2"),
                             (keep.w_router, "w_router")):
                    sp.dma_start(t[:, :, :], a[n].rearrange("(k p) n -> p k n", p=KC)).then_inc(weights_in, 16)
                sp.dma_start(keep.w_out2[:, :, :], a["w_out2"].rearrange("(u p) n -> p u n", p=128))\
                    .then_inc(weights_in, 16)
                sp.dma_start(keep.rope[:, :, :], a["rope"]).then_inc(weights_in, 16)
                for t, n in ((keep.norm1, "norm1"), (keep.own, "own"), (keep.near, "near"), (keep.future, "future")):
                    sp.dma_start(t[:, :], a[n]).then_inc(weights_in, 16)
                for t, n in ((keep.b_v1, "b_v1"), (keep.b_proj1, "b_proj1"), (keep.norm2_row, "norm2_row")):
                    sp.dma_start(t[:, :], a[n].broadcast_to([P, C])).then_inc(weights_in, 16)
                sp.wait_ge(weights_in, 16 * 13)

            @block.scalar
            def _(act):
                act.dma_start(tok_w[:, :], a["tok_w"].broadcast_to([P_IN, C])).then_inc(tok_in, 16)
                act.dma_start(tok_b[:, :], a["tok_b"].broadcast_to([P_IN, 1])).then_inc(tok_in, 16)
                act.dma_start(ident[:, :], a["ident"]).then_inc(consts_in, 16)
                act.dma_start(keep.b_qk1[:, :], a["b_qk1"]).then_inc(consts_in, 16)
                act.dma_start(keep.q_factor[:, :], a["q_factor"]).then_inc(consts_in, 16)
                act.dma_start(earlier[:, :], a["earlier"]).then_inc(consts_in, 16)
                act.wait_ge(zeros_ready, 1)
                act.dma_start(moe_in_d[NTOK:NTOK + ST, :], zeros[:, :]).then_inc(zeroed, 16)
                for b in range(B):
                    act.wait_ge(scores_turned, b + 1)
                    nc.scalar.copy(score_t[b][:, :], region[b][0:T_IN, 0:P_IN]).then_inc(scores_row, 1)
                act.wait_ge(zeroed, 16)

            @block.vector
            def _(dve):
                link = chain(dve, dve_self)
                dve.wait_ge(tok_in, 32)
                for b in range(B):
                    dve.wait_ge(x_loaded[b], 16)
                    for t in range(T_IN):
                        n = b * T_IN + t
                        link(nc.vector.tensor_tensor_reduce(prod[:, t, :], x_in[:, n, :], tok_w[:, :], 1.0, 0.0,
                                                            ALU.mult, ALU.add, score[:, n:n + 1]), wait=t == T_IN - 1)
                    s = slice(b * T_IN, (b + 1) * T_IN)
                    nc.vector.tensor_scalar(score[:, s], score[:, s], tok_b[:, 0:1], None, ALU.add)\
                        .then_inc(scores_ready, 1)
                dve.wait_ge(scores_ready, B)
                dve.wait_ge(consts_in, 64)
                nc.vector.tensor_copy(identb[:, :], ident[:, :])
                nc.vector.tensor_tensor(keep.qb[:, :], keep.b_qk1[:, 0:NK], keep.q_factor[:, :], ALU.mult)\
                    .then_inc(tables_ready, 1)
                dve.wait_ge(tables_ready, 1)
                half = T_IN // 2
                for b in range(B):
                    dve.wait_ge(scores_back[b], 16)
                    for t in range(T_IN):
                        n, i = b * T_IN + t, t % half
                        own, lo, hi = score[:, n:n + 1], t * P_IN, (t + 1) * P_IN
                        if t:
                            link(nc.vector.tensor_scalar(hit[:, i, 0:lo], all_scores[:, b, 0:lo], own, 0.0,
                                                         ALU.is_ge, ALU.add, accum_out=cnt[:, n, 0:1]), wait=False)
                        else:
                            link(nc.vector.memset(cnt[:, n, 0:1], 0.0), wait=False)
                        link(nc.vector.tensor_scalar(hit[:, i, lo:NIN], all_scores[:, b, lo:NIN], own, 0.0,
                                                     ALU.is_gt, ALU.add, accum_out=cnt[:, n, 1:2]), wait=False)
                        link(nc.vector.scalar_tensor_tensor(
                            out=same[:, i, :], in0=all_scores[:, b, lo:hi], scalar=own, in1=earlier[:, :],
                            op0=ALU.is_equal, op1=ALU.mult, accum_out=cnt[:, n, 2:3]), wait=i == half - 1)
                        if i == half - 1:
                            s = slice(n + 1 - half, n + 1)
                            link(nc.vector.tensor_reduce(rank[:, s], cnt[:, s, :], AX.X, ALU.add))
                            link(nc.vector.tensor_scalar(rank[:, s], rank[:, s], float(b * NIN), None, ALU.add))
                            nc.vector.tensor_copy(rank_i[:, s], rank[:, s]).then_inc(ranks_ready, 1)

            @block.tensor
            def _(pe):
                pe.wait_ge(consts_in, 64)
                for b in range(B):
                    pe.wait_ge(scores_ready, b + 1)
                    nc.tensor.transpose(region[b][0:T_IN, 0:P_IN], score[:, b * T_IN:(b + 1) * T_IN],
                                        ident[0:P_IN, 0:P_IN]).then_inc(scores_turned, 1)

            @block.gpsimd
            def _(pool):
                nc.gpsimd.memset(zeros[:, :], 0.0).then_inc(zeros_ready, 1)
                nc.gpsimd.memset(keep.neg_half[:, :], -0.5)
                for t in keep.vals:
                    nc.gpsimd.memset(t[:, :, :, :], 1.0)
                for t in (*keep.pt, *keep.v2):
                    ins = nc.gpsimd.memset(t[:, :, :], 0.0)
                ins.then_inc(filled, 1)
                pool.wait_ge(filled, 1)
                half = T_IN // 2
                for g in range(2 * B):
                    pool.wait_ge(ranks_ready, g + 1)
                    for n in range(g * half, (g + 1) * half):
                        nc.gpsimd.indirect_dma_start(
                            kept_d, bass.IndirectOffsetOnAxis(ap=rank_i[:, n:n + 1], axis=0),
                            x_in[:, n, :], None).then_inc(scattered, 16)
                pool.wait_ge(scattered, 16 * NB)




def both(*kinds):
    return [(k, j) for k in kinds for j in range(2)]


def merged(x, y):
    out, n = [], 0
    for i, s in enumerate(x):
        out.append(s)
        while n * len(x) < (i + 1) * len(y):
            out.append(y[n])
            n += 1
    return out


ROWS_LAG, LAST_MAXIMA = 3, 40


def maxima():
    out, late = [], []
    for j in range(2):
        for g in range(NG):
            for n in range(GH * T):
                if n == ROWS_LAG:
                    out += late
                out.append(("row_max", j, g * GH + n // T, n % T))
            out.append(("max_parts", j, g))
            late = [("max_rows", j, g)]
    return out + late


def first_products(j):
    return [("qk_split", j, m) for m in range(2 * NK)] + [("v1", j)]


def between(j):
    return [(k, j) for k in ("sums_out", "turn_o", "proj1", "norm2_stats", "norm2", "norm2_rms", "rms2", "turn2")]


def rotations(j):
    return [("rotate", j, m) for m in range(NPAIR + HKV)] + [("v2", j), ("split_keys", j)]


def weights(j):
    out = []

    def chunk(n, c):
        g, k = divmod(n, T)
        return ("sum", j, g, k) if c == NCH - 1 else ("part", j, g, k, c)

    for n in range(NG * T):
        g, k = divmod(n, T)
        for hl in range(GH):
            out.append(("exp", j, g, k, hl))
            if n and hl:
                out.append(chunk(n - 1, hl - 1))
            if g and k == 1 and hl == 0:
                out.append(("group_end", j, g - 1))
    return out + [chunk(NG * T - 1, c) for c in range(NCH)] + [("group_end", j, NG - 1)]


PAIR_END, PAIR_TAKE = (0, T - 1), (1, 1)


def pairs():
    out, every = [], [(j, u) for j in range(2) for u in range(NPAIR)]
    for n, (j, u) in enumerate(every):
        for x in range(2):
            for i in range(T):
                out.append(("causal", j, u, x, i))
                if n and (x, i) == PAIR_END:
                    out.append(("pair_end", *every[n - 1]))
                if n and (x, i) == PAIR_TAKE:
                    out.append(("pair_take", *every[n - 1]))
    return out + [("pair_end", *every[-1]), ("pair_take", *every[-1])]


MAXIMA = maxima()
AHEAD = GH * T + 1 + ROWS_LAG + 1
REST = AHEAD + len(weights(0))
CHAIN, TURNS = [between(j) for j in range(2)], [rotations(j) for j in range(2)]
ORDER = (
    both("norm1_stats", "norm1", "turn1") + first_products(0) + first_products(1) + MAXIMA[:AHEAD]
    + merged(weights(0), MAXIMA[AHEAD:REST])
    + merged(merged(weights(1)[:LAST_MAXIMA], MAXIMA[REST:]) + weights(1)[LAST_MAXIMA:], CHAIN[0])
    + CHAIN[1][:1] + TURNS[0][:1] + CHAIN[1][1:2] + TURNS[0][1:2] + merged(TURNS[0][2:7], CHAIN[1][2:])
    + merged(TURNS[1], TURNS[0][7:])
    + pairs() + [("out2", 0), ("rms3_stats", 0), ("rms3", 0), ("out2", 1), ("turn3", 0), ("route_logits", 0),
                 ("rms3_stats", 1), ("rms3", 1), ("turn3", 1), ("route_logits", 1)]
)


def score_banks(x, i):
    first = 2 * x
    return [first, first + 1] if i == T - 1 else [(first + i) % 4]


def turn_bank(x, k, i):
    return (i + x + (k == T - 1)) % 2


def last_users():
    user, before = {}, {}
    for n, (_, _, _, x, i) in enumerate([s for s in ORDER if s[0] == "causal"]):
        mine = score_banks(x, i)
        before[n + 1] = sorted({user[b] for b in mine if b in user})
        user.update((b, n + 1) for b in mine)
    return before


NORM_LAG, TURN_LAG, TAKE_LAG = 2, 3, 4


def step_before(step, n):
    same = [s for s in ORDER if s[0] == step[0]]
    return same[same.index(step) - n]


def numbered(*kinds):
    steps = [s for s in ORDER if s[0] in kinds]
    return {s: n + 1 for n, s in enumerate(steps)}


def uses(order):
    count, place = [0] * 4, {}

    def use(key, r):
        count[r] += 1
        place[key] = (r, count[r])

    turn = 0

    def use_next(key):
        nonlocal turn
        use(key, turn % 3)
        turn += 1

    for kind, j, *w in order:
        if kind in ("turn1", "turn2", "turn3", "turn_o", "v1", "v2", "proj1", "out2"):
            use_next((kind, j, 0))
            use_next((kind, j, 1))
        elif kind in ("qk_split", "row_max", "exp", "rotate", "max_rows", "route_logits"):
            use_next((kind, j, *w))
        elif kind == "part" and w[1:] == [0, 0]:
            use(("sum", j, w[0]), 3)
        elif kind == "sums_out":
            for t in range(T):
                use_next((kind, j, t))
        elif kind == "pair_end":
            use((kind, j, *w), 3)
    return place, count


def tower(nc, a, region, keep, kept_d, parts_d, moe_in_d, res_d, logit_d):
    es = ExitStack()
    with es:
        def sb(name, shape, dt=F32):
            return es.enter_context(nc.sbuf_tensor(name, shape, dt))

        def sem(name):
            s = es.enter_context(nc.semaphore("to_" + name))
            sems.append(s)
            return s

        sems = []
        place, _ = uses(ORDER)
        ident, identb, near, future, own = keep.ident, keep.identb, keep.near, keep.future, keep.own
        w_qkv1, w_proj1, w_qkv2, w_out2, w_router = keep.w_qkv1, keep.w_proj1, keep.w_qkv2, keep.w_out2, keep.w_router
        b_qk1, q_factor, qb, b_v1, b_proj1 = keep.b_qk1, keep.q_factor, keep.qb, keep.b_v1, keep.b_proj1
        norm1, norm2_row, rope, neg_half = keep.norm1, keep.norm2_row, keep.rope, keep.neg_half
        vals, v2, pt = keep.vals, keep.v2, keep.pt

        hid = [sb(f"hid{j}", [P, T, C]) for j in range(2)]
        nrm = [sb(f"nrm{j}", [P, T, C]) for j in range(2)]
        tmp = [sb(f"tmp{j}", [P, T, C]) for j in range(2)]
        xT = [sb(f"xT{j}", [KC, NK, KEEP]) for j in range(2)]
        stats = [sb(f"stats{j}", [P, T, 6]) for j in range(2)]
        mv = [sb(f"mv{j}", [P, T, 2]) for j in range(2)]
        var = [sb(f"var{j}", [P, T]) for j in range(2)]
        rstd = [sb(f"rstd{j}", [P, T]) for j in range(2)]
        big = [sb(f"big{j}", [128, 2 * H1 * KEEP], BF16) for j in range(2)]
        Aq = [x[0:R_ALL, 0:H1 * KEEP].rearrange("p (h n) -> p h n", h=H1) for x in big]
        Ak = [x[0:R_ALL, H1 * KEEP:].rearrange("p (h n) -> p h n", h=H1) for x in big]
        q2 = [x[:, 0:H1 * KEEP].bitcast(F32).rearrange("p (u n) -> p u n", u=NPAIR) for x in big]
        k2 = [x[:, H1 * KEEP:].bitcast(F32).rearrange("p (g x n) -> p g x n", g=HKV, x=2) for x in big]
        mx = [sb(f"mx{j}", [P, H1, T]) for j in range(2)]
        rowp = [sb(f"rowp{j}", [P, NG, T, PARTS * GH], BF16) for j in range(2)]
        junk = sb("junk", [P, C])
        mtmp = sb("mtmp", [P, 2, H1, T])
        mrow = [sb(f"mrow{j}", [128, KEEP], BF16) for j in range(2)]
        attn = [sb(f"attn{j}", [128, NPAIR, KEEP]) for j in range(2)]
        RROT = NPAIR // 2
        plain = [[x[:, i, :] for i in range(RROT)] for x in attn]
        swap = [[x[:, RROT + i, :] for i in range(RROT)] for x in attn]
        logit = [sb(f"logit{j}", [P, T, E]) for j in range(2)]
        qk32 = [sb(f"qk32_{i}", [128, KEEP]) for i in range(2)]
        rest = [sb(f"rest{i}", [128, KEEP]) for i in range(2)]
        parts = [[x[0:KC, :, :].rearrange("p u n -> p (u n)").bitcast(BF16)
                  [:, m * PARTS * KEEP:(m + 1) * PARTS * KEEP].rearrange("p (s n) -> p s n", s=PARTS)
                  for m in range(2 * NK)] for x in attn]
        pr = [sb(f"pr{i}", [P, KEEP]) for i in range(3)] + [x[0:P, :] for x in (*qk32, *rest)]
        NPR = len(pr)
        probs = [t[:, 0:GH, :] for t in pt]
        recip = sb("recip", [P, T, H1])
        RING = 8
        nm = sb("nm", [P, RING])
        den = sb("den", [P, RING])
        rden = sb("rden", [P, RING])

        filled = [sem(f"filled{r}") for r in range(4)]
        emptied = [sem(f"emptied{r}") for r in range(4)]
        hid_loaded = [sem(f"hid_loaded{j}") for j in range(2)]
        rows_loaded = [sem(f"rows_loaded{j}") for j in range(2)]
        dve_self = sem("dve_self")
        var_ready, rstd_ready = sem("var_ready"), sem("rstd_ready")
        nrm_ready = sem("nrm_ready")
        qk32_ready, rest_ready = sem("qk32_ready"), sem("rest_ready")
        mid_ready, lo_ready = sem("mid_ready"), sem("lo_ready")
        parts_out = [sem(f"parts_out{j}") for j in range(2)]
        prod_in = [sem(f"prod_in{j}") for j in range(2)]
        rowp_ready = sem("rowp_ready")
        mrow_in = [[sem(f"mrow_in{j}_{g}") for g in range(NG)] for j in range(2)]
        probs_used = sem("probs_used")
        keys_ready = sem("keys_ready")
        swapped = [[sem(f"swapped{j}_{i}") for i in range(RROT)] for j in range(2)]
        cos_ready, sin_ready, rot_ready = sem("cos_ready"), sem("sin_ready"), sem("rot_ready")
        nm_ready, prn_ready = sem("nm_ready"), sem("prn_ready")
        scored, exp_done = sem("scored"), sem("exp_done")
        turned, taken_act = sem("turned"), sem("taken_act")
        turned_last, taken_last = sem("turned_last"), sem("taken_last")
        stored = sem("stored")

        VAR = numbered("norm1_stats", "norm2_stats", "norm2_rms", "rms3_stats")
        NRM = numbered("norm1", "rms2", "rms3")
        QK, MP = numbered("qk_split"), numbered("max_parts")
        SUM = numbered("sum")
        ROT, CAUSAL, PAIR = numbered("rotate"), numbered("causal"), numbered("pair_end")
        NROT = NPAIR + HKV
        SCORE_USERS = last_users()

        def score_tiles(x, i):
            first = score_banks(x, i)[0]
            o = 512 * (first % 2)
            return region[first // 2][0:P, o:1024].rearrange("p (t n) -> p t n", n=PK)[:, 0:i + 1, 0:P]

        def turned_tiles(x, i, lo, hi):
            o = 512 * turn_bank(x, lo, i)
            tiles = region[2][0:P, o:o + 512].rearrange("p (t n) -> p t n", n=PK)[:, :, 0:P]
            return tiles[:, 0:1, :] if lo == T - 1 else tiles[:, lo:hi, :]

        def take_turned_weights(eng, copy, step, lo, hi, ready, done):
            _, j, u, x, i = step
            head = 2 * (PAIR[("pair_end", j, u)] - 1) + x
            eng.wait_ge(*ready)
            if head >= 3:
                r, m = place[list(PAIR)[(head - 3) // 2]]
                eng.wait_ge(filled[r], m)
            copy(pt[head % 3][0:P, lo:hi, i * P:(i + 1) * P], turned_tiles(x, i, lo, hi)).then_inc(done, 1)

        def heads_done(step):
            return 2 * (PAIR[("pair_end", *step[1:3])] - 1) + step[3] + (step[4] == T - 1)

        TURNED = {1: "norm1", 2: "rms2", 3: "rms3"}

        USED = {s: n + 1 for n, s in enumerate(x for x in ORDER if x[0] == "sum" and x[3] < T - 1)}

        def taken(eng, *keys):
            for key in keys:
                r, n = place[key]
                eng.wait_ge(emptied[r], n)

        def summed(eng, step):
            if step[3] < T - 1:
                eng.wait_ge(probs_used, USED[step])
            else:
                r, n = place[("sum", step[1], step[2])]
                eng.wait_ge(filled[r], n)

        with nc.Fori(0, B // 2) as turn:
          with nc.Block() as block:

            @block.sync
            def _(sp):
                for j in range(2):
                    sp.dma_start(hid[j][:, :, :], kept_d[bass.ds((turn * 2 + j) * NIN, KEEP), :]
                                 .rearrange("(t p) c -> p t c", p=P)).then_inc(hid_loaded[j], 16)
                for j in range(2):
                    for rows, name in ((Aq[j][R_PROD:R_MAX], "dist_q"), (Ak[j][R_PROD:R_ALL], "dist_k")):
                        sp.dma_start(rows, a[name].unsqueeze(1).broadcast_to([a[name].shape[0], H1, KEEP]))\
                            .then_inc(rows_loaded[j], 16)
                for step in ORDER:
                    kind, j, *w = step
                    if kind == "qk_split":
                        m, = w
                        sp.wait_ge(lo_ready, QK[step])
                        side, k = divmod(m, NK)
                        sp.dma_start(parts_d[j, side, :, k * KC:(k + 1) * KC, :].rearrange("s p n -> p s n"),
                                     parts[j][m]).then_inc(parts_out[j], 16)
                        if m < 2 * NK - 1:
                            continue
                        sp.wait_ge(parts_out[j], 16 * 2 * NK)
                        for side, (dst, sel) in enumerate(((Aq, Q_PART), (Ak, K_PART))):
                            for g in range(NPROD):
                                sp.dma_start(dst[j][g * D1:(g + 1) * D1, :, :],
                                             parts_d[j, side, sel[g]].rearrange("(h d) n -> d h n", d=D1))\
                                    .then_inc(prod_in[j], 16)
                    elif kind == "max_rows":
                        g, = w
                        taken(sp, step)
                        sp.dma_start(Aq[j][R_MAX:R_ALL, g * GH:(g + 1) * GH, :],
                                     mrow[j][32 * g:32 * g + PARTS * GH, :]).then_inc(mrow_in[j][g], 16)
                    elif kind == "rotate":
                        m, = w
                        taken(sp, step)
                        if m >= RROT:
                            sp.wait_ge(rot_ready, ROT[("rotate", j, m - RROT)])
                        sp.dma_start(swap[j][m % RROT][0:64, :], plain[j][m % RROT][64:128, :])\
                            .then_inc(swapped[j][m % RROT], 16)
                        sp.dma_start(swap[j][m % RROT][64:128, :], plain[j][m % RROT][0:64, :])\
                            .then_inc(swapped[j][m % RROT], 16)
                    elif kind == "rms3":
                        sp.wait_ge(nrm_ready, NRM[step])
                        t0 = (turn * 2 + j) * T
                        sp.dma_start(moe_in_d[bass.ds(t0 * P, T * P), :].rearrange("(t p) c -> p t c", p=P),
                                     nrm[j][:, :, :]).then_inc(stored, 16)
                        sp.dma_start(res_d[bass.ds(t0, T)].rearrange("t p c -> p t c"),
                                     hid[j][:, :, :]).then_inc(stored, 16)
                    elif kind == "route_logits":
                        taken(sp, step)
                        sp.dma_start(logit_d[bass.ds((turn * 2 + j) * T, T)].rearrange("t p c -> p t c"),
                                     logit[j][:, :, :]).then_inc(stored, 16)
                sp.wait_ge(stored, 2 * 3 * 16)

            @block.tensor
            def _(pe):
                def begin(key):
                    r, n = place[key]
                    if n > 1:
                        pe.wait_ge(emptied[r], n - 1)
                    return region[r], filled[r]

                def turn_rows(src, key0, key1):
                    for key, tiles in ((key0, range(T - 1)), (key1, range(T - 1, T))):
                        dst, done = begin(key)
                        for k in range(NK):
                            for t in tiles:
                                o = 512 * k + P * (t - tiles[0])
                                ins = nc.tensor.transpose(dst[0:KC, o:o + P], src[:, t, k * KC:(k + 1) * KC],
                                                          ident[0:P, 0:P])
                        ins.then_inc(done, 1)

                def rows_times(lhs, rhs, steps, key0, key1):
                    for key, tiles in ((key0, range(T - 1)), (key1, range(T - 1, T))):
                        dst, done = begin(key)
                        for t in tiles:
                            o = CS * (t - tiles[0])
                            for k in range(steps):
                                ins = nc.tensor.matmul(dst[0:P, o:o + C], lhs[:, k, t * P:(t + 1) * P], rhs[:, k, :],
                                                       start=(k == 0), stop=(k == steps - 1))
                        ins.then_inc(done, 1)

                def channels_times(lhs, rhs, rows, key):
                    dst, done = begin(key)
                    for c in range(NCH):
                        for k in range(NK):
                            ins = nc.tensor.matmul(dst[0:rows, c * CS:c * CS + CH], lhs[:, k, :],
                                                   rhs[:, k, c * CH:(c + 1) * CH], start=(k == 0), stop=(k == NK - 1))
                    ins.then_inc(done, 1)

                def scores1(dst, rows, lhs, rhs, tile):
                    for c in range(NCH):
                        ins = nc.tensor.matmul(dst[0:P, c * CS:c * CS + CH], lhs[0:rows, tile * P:(tile + 1) * P],
                                               rhs[0:rows, c * CH:(c + 1) * CH], start=True, stop=False,
                                               skip_group_check=True)
                        lo, hi = max(tile * P, c * CH), min((tile + 1) * P, (c + 1) * CH)
                        if lo < hi:
                            ins = nc.tensor.matmul(dst[0:P, c * CS + lo - c * CH:c * CS + hi - c * CH],
                                                   identb[0:P, 0:P], near[:, lo - tile * P:hi - tile * P],
                                                   start=False, stop=True, skip_group_check=True)
                    return ins

                def weighted_sum(j, g, k, c):
                    if c == 0:
                        if k == 0:
                            begin(("sum", j, g))
                        taken(pe, *(("exp", j, g, k, hl) for hl in range(GH)))
                    for hl in range(GH):
                        ins = nc.tensor.matmul(
                            region[3][VW * hl:VW * (hl + 1), c * CS:c * CS + CH], vals[j][:, k, g * GH + hl, :],
                            probs[SUM[("sum", j, g, k)] % 3][:, hl, c * CH:(c + 1) * CH],
                            start=(k == 0 and c % 2 == 0), stop=(k == T - 1), skip_group_check=True)
                    if c == NCH - 1:
                        ins.then_inc(probs_used if k < T - 1 else filled[3], 1)

                pending_turn = []

                def turn_weights():
                    step = pending_turn.pop(0)
                    _, j, u, x, i = step
                    n = CAUSAL[step]
                    pe.wait_ge(prn_ready, n)
                    if i == 0 and heads_done(step):
                        pe.wait_ge(taken_last, heads_done(step))
                    elif n > 2:
                        pe.wait_ge(taken_act, n - 2)
                    for k in range(min(i + 1, T - 1)):
                        ins = nc.tensor.transpose(turned_tiles(x, i, 0, T - 1)[:, k, :],
                                                  pr[n % NPR][:, k * P:(k + 1) * P], ident[0:P, 0:P])
                    ins.then_inc(turned, 1)
                    if i == T - 1:
                        pe.wait_ge(taken_act, n - 1)
                        nc.tensor.transpose(turned_tiles(x, i, i, T)[:, 0, :], pr[n % NPR][:, i * P:T * P],
                                            ident[0:P, 0:P]).then_inc(turned_last, 1)

                for step in ORDER:
                    kind, j, *w = step
                    if kind in ("turn1", "turn2", "turn3"):
                        n = int(kind[-1])
                        pe.wait_ge(nrm_ready, NRM[(TURNED[n], j)])
                        turn_rows(tmp[j] if n == 2 else nrm[j], (kind, j, 0), (kind, j, 1))
                    elif kind == "qk_split":
                        m, = w
                        if m == 0:
                            taken(pe, ("turn1", j, 0), ("turn1", j, 1))
                        channels_times(w_qkv1[:, :, m * KC:(m + 1) * KC], xT[j], KC, step)
                    elif kind == "v1":
                        rows_times(xT[j], w_qkv1[:, :, 2 * C:3 * C], NK, (kind, j, 0), (kind, j, 1))
                    elif kind == "row_max":
                        h, i = w
                        if h == 0 and i == 0:
                            pe.wait_ge(prod_in[j], 16 * 2 * NPROD)
                            pe.wait_ge(rows_loaded[j], 16 * 2)
                        dst, done = begin((kind, j, h, i))
                        scores1(dst, R_MAX, Aq[j][:, h, :], Ak[j][:, h, :], i).then_inc(done, 1)
                    elif kind == "max_rows":
                        g, = w
                        pe.wait_ge(rowp_ready, MP[("max_parts", j, g)])
                        dst, done = begin(step)
                        for t in range(T):
                            ins = nc.tensor.matmul(dst[32 * g:32 * g + PARTS * GH, PK * t:PK * t + P], rowp[j][:, g, t, :],
                                                   identb[0:P, 0:P], start=True, stop=True)
                        ins.then_inc(done, 1)
                    elif kind == "exp":
                        g, k, hl = w
                        if (k, hl) == (0, 0):
                            pe.wait_ge(mrow_in[j][g], 16)
                            taken(pe, ("v1", j, 0), ("v1", j, 1))
                        h = g * GH + hl
                        dst, done = begin(step)
                        scores1(dst, R_ALL, Ak[j][:, h, :], Aq[j][:, h, :], k).then_inc(done, 1)
                    elif kind == "part":
                        weighted_sum(j, *w)
                    elif kind == "sum":
                        weighted_sum(j, *w, NCH - 1)
                    elif kind == "sums_out":
                        taken(pe, *(("sum", j, g) for g in range(NG)))
                        for t in range(T):
                            dst, done = begin((kind, j, t))
                            for g in range(NG):
                                ins = nc.tensor.transpose(dst[0:P, 128 * g:128 * g + 128],
                                                          attn[j][:, g, t * P:(t + 1) * P], ident[:, :])
                            ins.then_inc(done, 1)
                    elif kind == "turn_o":
                        taken(pe, *(("sums_out", j, t) for t in range(T)))
                        turn_rows(tmp[j], ("turn_o", j, 0), ("turn_o", j, 1))
                    elif kind == "proj1":
                        taken(pe, ("turn_o", j, 0), ("turn_o", j, 1))
                        rows_times(xT[j], w_proj1, NK, ("proj1", j, 0), ("proj1", j, 1))
                    elif kind == "rotate":
                        m, = w
                        if m == 0:
                            taken(pe, ("turn2", j, 0), ("turn2", j, 1))
                        channels_times(w_qkv2[:, :, m * 128:(m + 1) * 128], xT[j], 128, step)
                    elif kind == "v2":
                        rows_times(xT[j], w_qkv2[:, :, NROT * 128:], NK, (kind, j, 0), (kind, j, 1))
                    elif kind == "causal":
                        u, x, i = w
                        if (u, x, i) == (0, 0, 0):
                            pe.wait_ge(rot_ready, ROT[("rotate", j, NROT - 1)])
                            pe.wait_ge(keys_ready, 2 * j + 2)
                            taken(pe, ("v2", 1, 0), ("v2", 1, 1), *(("rotate", 1, m) for m in range(NROT)))
                        for m in SCORE_USERS[CAUSAL[step]]:
                            pe.wait_ge(exp_done, m)
                        slots = score_tiles(x, i)
                        keys = k2[j][:, u // 2, x, :].rearrange("p (t n) -> p t n", n=P)
                        lhs = q2[j][:, u, i * P:(i + 1) * P]
                        near_end = min(i + 1, T - 1)
                        for lo, hi in ((0, near_end), (near_end, i + 1)):
                            if lo < hi:
                                nc.tensor.matmul(slots[:, lo:hi, :], lhs, keys[:, lo:hi, :], start=True, stop=False,
                                                 skip_group_check=True)
                        nc.tensor.matmul(slots[:, i, :], identb[0:P, 0:P], future[:, :], start=False, stop=True,
                                         skip_group_check=True).then_inc(scored, 1)
                        pending_turn.append(step)
                        if len(pending_turn) > TURN_LAG:
                            turn_weights()
                    elif kind == "pair_end":
                        u, = w
                        while pending_turn and pending_turn[0][1:3] == (j, u):
                            turn_weights()
                        dst, done = begin((kind, j, u))
                        last = ("causal", j, u, 1, T - 1)
                        pe.wait_ge(taken_act, CAUSAL[last])
                        pe.wait_ge(taken_last, heads_done(last))
                        first = 2 * (PAIR[step] - 1)
                        half = 3 * P
                        for k in range(T):
                            for lo, hi, o in ((k * P, half, k * P), (max(half, k * P), KEEP, 512 + max(half, k * P) - half)):
                                if lo >= hi:
                                    continue
                                for x in range(2):
                                    ins = nc.tensor.matmul(
                                        dst[D2 * x:D2 * (x + 1), o:o + hi - lo], v2[j][:, k, D2 * (u // 2):D2 * (u // 2 + 1)],
                                        pt[(first + x) % 3][:, k, lo:hi], start=(k == 0), stop=(k == T - 1),
                                        skip_group_check=True)
                        ins.then_inc(done, 1)
                    elif kind == "out2":
                        taken(pe, ("pair_end", j, NPAIR - 1))
                        rows_times(attn[j], w_out2, NPAIR, (kind, j, 0), (kind, j, 1))
                    elif kind == "route_logits":
                        taken(pe, ("turn3", j, 0), ("turn3", j, 1))
                        dst, done = begin((kind, j))
                        for t in range(T):
                            for k in range(NK):
                                ins = nc.tensor.matmul(dst[0:P, E * t:E * t + E], xT[j][:, k, t * P:(t + 1) * P],
                                                       w_router[:, k, :], start=(k == 0), stop=(k == NK - 1))
                        ins.then_inc(done, 1)

            @block.scalar
            def _(act):
                def full(key):
                    r, n = place[key]
                    act.wait_ge(filled[r], n)
                    return region[r], emptied[r]

                def take_turned(j, key0, key1, scale=None):
                    for key, lo, hi in ((key0, 0, T - 1), (key1, T - 1, T)):
                        src, done = full(key)
                        n = (hi - lo) * P
                        if scale is None:
                            ins = nc.scalar.copy(xT[j][:, :, lo * P:hi * P],
                                                 src[0:KC, :].rearrange("p (k n) -> p k n", k=NK)[:, :, 0:n])
                        else:
                            for k in range(NK):
                                ins = nc.scalar.activation(xT[j][:, k, lo * P:hi * P], src[0:KC, 512 * k:512 * k + n],
                                                           ACT.Copy, scale=scale[:, k:k + 1])
                        ins.then_inc(done, 1)

                pending_take = []

                def take_weights():
                    step = pending_take.pop(0)
                    take_turned_weights(act, nc.scalar.copy, step, 0, min(step[-1] + 1, T - 1),
                                        (turned, CAUSAL[step]), taken_act)

                for step in ORDER:
                    kind, j, *w = step
                    if kind in ("turn1", "turn2", "turn3"):
                        take_turned(j, (kind, j, 0), (kind, j, 1), norm1 if kind == "turn2" else None)
                    elif kind == "qk_split":
                        m, = w
                        n = QK[step] - 1
                        if n >= 2:
                            act.wait_ge(rest_ready, n - 1)
                        src, done = full(step)
                        side, k = divmod(m, NK)
                        scale = q_factor[:, k:k + 1] if side == 0 else 1.0
                        bias = qb[:, k:k + 1] if side == 0 else b_qk1[:, NK + k:NK + k + 1]
                        for dst in (qk32[n % 2][0:KC, :], parts[j][m][:, HI, :]):
                            ins = nc.scalar.activation(dst.rearrange("p (c n) -> p c n", n=CH), chunks(src, KC),
                                                       ACT.Identity, bias=bias, scale=scale)
                            ins.then_inc(qk32_ready if dst.dtype == F32 else done, 1)
                    elif kind == "max_rows":
                        g, = w
                        src, done = full(step)
                        rows = slice(32 * g, 32 * g + PARTS * GH)
                        ins = nc.scalar.copy(mrow[j][rows, :].rearrange("p (t n) -> p t n", n=P),
                                             src[rows, :].rearrange("p (t n) -> p t n", n=PK)[:, 0:T, 0:P])
                        ins.then_inc(done, 1)
                    elif kind == "exp":
                        g, k, hl = w
                        n = SUM[("sum", j, g, k)]
                        if n > 3 and hl == 0:
                            summed(act, step_before(("sum", j, g, k), 3))
                        src, done = full(step)
                        ins = nc.scalar.activation(
                            probs[n % 3][0:P, hl, :].rearrange("p (c n) -> p c n", n=CH), chunks(src, P),
                            ACT.Exp, scale=SLOPES[g * GH + hl])
                        ins.then_inc(done, 1)
                    elif kind == "group_end":
                        src, done = full(("sum", j, w[0]))
                        ins = nc.scalar.copy(attn[j][:, w[0], :].rearrange("p (c n) -> p c n", n=CH), chunks(src))
                        ins.then_inc(done, 1)
                    elif kind == "turn_o":
                        take_turned(j, ("turn_o", j, 0), ("turn_o", j, 1))
                    elif kind == "rotate":
                        m, = w
                        if m >= RROT:
                            before = ROT[("rotate", j, m - RROT)]
                            act.wait_ge(rot_ready, before)
                        src, done = full(step)
                        nc.scalar.copy(plain[j][m % RROT].rearrange("p (c n) -> p c n", n=CH), chunks(src))\
                            .then_inc(done, 1)
                    elif kind == "split_keys":
                        act.wait_ge(rot_ready, ROT[("rotate", j, NROT - 1)])
                        nc.scalar.activation(k2[j][:, :, 1, :], k2[j][:, :, 0, :], ACT.Copy, scale=own[:, 1:2])\
                            .then_inc(keys_ready, 1)
                        act.wait_ge(keys_ready, 2 * j + 1)
                        nc.scalar.activation(k2[j][:, :, 0, :], k2[j][:, :, 0, :], ACT.Copy, scale=own[:, 0:1])\
                            .then_inc(keys_ready, 1)
                    elif kind == "v2":
                        for i, (lo, hi) in enumerate(((0, T - 1), (T - 1, T))):
                            src, done = full((kind, j, i))
                            ins = nc.scalar.copy(v2[j][0:P, lo:hi, :],
                                                 src[0:P, :].rearrange("p (t n) -> p t n", n=CS)[:, 0:hi - lo, 0:C])
                            ins.then_inc(done, 1)
                    elif kind == "causal":
                        u, x, i = w
                        n = CAUSAL[step]
                        pending_take.append(step)
                        if len(pending_take) > TAKE_LAG:
                            take_weights()
                        act.wait_ge(nm_ready, n)
                        if n > NPR:
                            act.wait_ge(turned, n - NPR)
                        nc.scalar.activation(
                            pr[n % NPR][:, 0:(i + 1) * P].rearrange("p (t n) -> p t n", n=P),
                            score_tiles(x, i), ACT.Exp, bias=nm[:, n % RING:n % RING + 1],
                            accum_out=den[:, n % RING:n % RING + 1]).then_inc(exp_done, 1)
                    elif kind == "pair_end":
                        while pending_take and pending_take[0][1:3] == (j, w[0]):
                            take_weights()
                    elif kind == "route_logits":
                        src, done = full((kind, j))
                        ins = nc.scalar.copy(logit[j][:, :, :], src[0:P, 0:T * E].rearrange("p (t e) -> p t e", e=E))
                        ins.then_inc(done, 1)

            @block.vector
            def _(dve):
                link = chain(dve, dve_self)

                def full(key):
                    r, n = place[key]
                    dve.wait_ge(filled[r], n)
                    return region[r], emptied[r]

                def rows(src, n):
                    return src[0:P, :].rearrange("p (t n) -> p t n", n=CS)[:, 0:n, 0:C]

                def wide(row, n):
                    return row[:, :].unsqueeze(1).broadcast_to([P, n, C])

                def mean_of_squares(src, j):
                    for t in range(T):
                        link(nc.vector.tensor_tensor_reduce(junk[:, :], src[:, t, :], src[:, t, :], 1.0 / C, RMS_EPS,
                                                            ALU.mult, ALU.add, var[j][:, t:t + 1]))
                    nc.vector.engine_nop().then_inc(var_ready, 1)

                pending_norm, pending_take = [], []

                def normalise():
                    step = pending_norm.pop(0)
                    n, i = CAUSAL[step], step[-1]
                    dve.wait_ge(exp_done, n)
                    link(nc.vector.reciprocal(rden[:, n % RING:n % RING + 1], den[:, n % RING:n % RING + 1]))
                    v = pr[n % NPR][:, 0:(i + 1) * P]
                    nc.vector.tensor_scalar(v, v, rden[:, n % RING:n % RING + 1], None, ALU.mult).then_inc(prn_ready, 1)

                def take_weights():
                    step = pending_take.pop(0)
                    if step[-1] == T - 1:
                        take_turned_weights(dve, nc.vector.tensor_copy, step, T - 1, T,
                                            (turned_last, heads_done(step)), taken_last)

                for step in ORDER:
                    kind, j, *w = step
                    if kind in ("norm1_stats", "norm2_stats"):
                        if kind == "norm1_stats":
                            dve.wait_ge(hid_loaded[j], 16)
                        for t in range(T):
                            link(nc.vector.bn_stats(stats[j][:, t, :], hid[j][:, t, :]), wait=t == T - 1)
                        for t in range(T):
                            link(nc.vector.bn_aggr(mv[j][:, t, :], stats[j][:, t, :]), wait=t == T - 1)
                        nc.vector.tensor_scalar(var[j][:, :], mv[j][:, :, 1], LN_EPS, None, ALU.add)\
                            .then_inc(var_ready, 1)
                    elif kind in ("norm1", "norm2"):
                        dve.wait_ge(rstd_ready, VAR[(kind + "_stats", j)])
                        for t in range(T):
                            ins = nc.vector.tensor_scalar(nrm[j][:, t, :], hid[j][:, t, :], mv[j][:, t, 0:1],
                                                          rstd[j][:, t:t + 1], ALU.subtract, ALU.mult)
                            if kind == "norm2":
                                link(ins, wait=t == T - 1)
                        if kind == "norm1":
                            ins.then_inc(nrm_ready, 1)
                    elif kind == "norm2_rms":
                        mean_of_squares(nrm[j], j)
                    elif kind == "rms2":
                        dve.wait_ge(rstd_ready, VAR[("norm2_rms", j)])
                        for t in range(T):
                            ins = nc.vector.tensor_scalar(tmp[j][:, t, :], nrm[j][:, t, :], rstd[j][:, t:t + 1], None,
                                                          ALU.mult)
                        ins.then_inc(nrm_ready, 1)
                    elif kind == "qk_split":
                        m, = w
                        n = QK[step] - 1
                        i = n % 2
                        dve.wait_ge(qk32_ready, n + 1)
                        taken(dve, step)
                        if n >= 2:
                            dve.wait_ge(lo_ready, n - 1)
                        nc.vector.tensor_tensor(rest[i][0:KC, :], qk32[i][0:KC, :], parts[j][m][:, HI, :],
                                                ALU.subtract).then_inc(rest_ready, 1)
                        dve.wait_ge(rest_ready, n + 1)
                        nc.vector.tensor_copy(parts[j][m][:, MID, :], rest[i][0:KC, :]).then_inc(mid_ready, 1)
                    elif kind == "v1":
                        for i, (lo, hi) in enumerate(((0, T - 1), (T - 1, T))):
                            src, done = full((kind, j, i))
                            ins = nc.vector.tensor_tensor(
                                vals[j][0:P, lo:hi, :, 0:D1], rows(src, hi - lo).rearrange("p t (h d) -> p t h d", d=D1),
                                wide(b_v1, hi - lo).rearrange("p t (h d) -> p t h d", d=D1), ALU.add)
                            ins.then_inc(done, 1)
                    elif kind == "row_max":
                        h, i = w
                        src, done = full((kind, j, h, i))
                        nc.vector.tensor_reduce(mx[j][:, h, i:i + 1], chunks(src, P), AX.XY, ALU.max)\
                            .then_inc(done, 1)
                    elif kind == "max_parts":
                        g, = w
                        heads = slice(g * GH, (g + 1) * GH)
                        taken(dve, ("row_max", j, (g + 1) * GH - 1, T - 1))
                        by_tile = [rowp[j][:, g, :, s * GH:(s + 1) * GH].rearrange("p t h -> p h t") for s in range(PARTS)]
                        left = [mtmp[:, i, heads] for i in range(2)]
                        link(nc.vector.tensor_scalar(left[0], mx[j][:, heads, :], -1.0, None, ALU.mult))
                        link(nc.vector.tensor_copy(by_tile[HI], left[0]))
                        link(nc.vector.tensor_tensor(left[1], left[0], by_tile[HI], ALU.subtract))
                        link(nc.vector.tensor_copy(by_tile[MID], left[1]))
                        nc.vector.tensor_tensor(by_tile[LO], left[1], by_tile[MID], ALU.subtract)\
                            .then_inc(rowp_ready, 1)
                    elif kind == "sums_out":
                        link(nc.vector.tensor_tensor(nrm[j][:, :, :], hid[j][:, :, :], wide(b_proj1, T), ALU.add))
                        for t in range(T):
                            src, done = full((kind, j, t))
                            v = src[0:P, 0:H1 * VW].rearrange("p (h n) -> p h n", n=VW)
                            link(nc.vector.reciprocal(recip[:, t, :], v[:, :, D1]))
                            ins = nc.vector.tensor_tensor(
                                tmp[j][:, t, :].rearrange("p (h d) -> p h d", d=D1), v[:, :, 0:D1],
                                recip[:, t, :].unsqueeze(2).broadcast_to([P, H1, D1]), ALU.mult)
                            ins.then_inc(done, 1)
                    elif kind == "proj1":
                        for i, (lo, hi) in enumerate(((0, T - 1), (T - 1, T))):
                            src, done = full(("proj1", j, i))
                            ins = nc.vector.tensor_tensor(hid[j][:, lo:hi, :], rows(src, hi - lo), nrm[j][:, lo:hi, :], ALU.add)
                            ins.then_inc(done, 1)
                            taken(dve, ("proj1", j, i))
                    elif kind == "rotate":
                        m, = w
                        dst = q2[j][:, m, :] if m < NPAIR else k2[j][:, m - NPAIR, 0, :]
                        taken(dve, step)
                        nc.vector.tensor_tensor(dst, plain[j][m % RROT], rope[:, 0, :], ALU.mult)\
                            .then_inc(cos_ready, 1)
                        dve.wait_ge(cos_ready, ROT[step])
                        dve.wait_ge(sin_ready, ROT[step])
                        nc.vector.tensor_tensor(dst, dst, swap[j][m % RROT], ALU.add).then_inc(rot_ready, 1)
                    elif kind == "causal":
                        u, x, i = w
                        n = CAUSAL[step]
                        pending_norm.append(step)
                        pending_take.append(step)
                        if len(pending_take) > TAKE_LAG:
                            take_weights()
                        if len(pending_norm) > NORM_LAG:
                            normalise()
                        dve.wait_ge(scored, n)
                        nc.vector.tensor_reduce(nm[:, n % RING:n % RING + 1], score_tiles(x, i), AX.XY, ALU.max,
                                                negate=True).then_inc(nm_ready, 1)
                    elif kind == "pair_end":
                        u, = w
                        while pending_norm and pending_norm[0][1:3] == (j, u):
                            normalise()
                        while pending_take and pending_take[0][1:3] == (j, u):
                            take_weights()
                    elif kind == "pair_take":
                        u, = w
                        src, done = full(("pair_end", j, u))
                        half = 3 * P
                        link(nc.vector.tensor_copy(attn[j][:, u, 0:half], src[:, 0:half]), wait=False)
                        ins = nc.vector.tensor_copy(attn[j][:, u, half:KEEP], src[:, 512:512 + KEEP - half])
                        ins.then_inc(done, 1)
                    elif kind == "out2":
                        for i, (lo, hi) in enumerate(((0, T - 1), (T - 1, T))):
                            src, done = full((kind, j, i))
                            ins = nc.vector.tensor_tensor(tmp[j][:, lo:hi, :], rows(src, hi - lo), nrm[j][:, lo:hi, :], ALU.add)
                            ins.then_inc(done, 1)
                            taken(dve, (kind, j, i))
                            link(nc.vector.tensor_tensor(hid[j][:, lo:hi, :], hid[j][:, lo:hi, :], tmp[j][:, lo:hi, :], ALU.add),
                                 wait=False)
                    elif kind == "rms3_stats":
                        mean_of_squares(tmp[j], j)
                    elif kind == "rms3":
                        dve.wait_ge(rstd_ready, VAR[("rms3_stats", j)])
                        for t in range(T):
                            ins = nc.vector.scalar_tensor_tensor(out=nrm[j][:, t, :], in0=tmp[j][:, t, :],
                                                                 scalar=rstd[j][:, t:t + 1], in1=norm2_row[:, :],
                                                                 op0=ALU.mult, op1=ALU.mult)
                        ins.then_inc(nrm_ready, 1)

            @block.gpsimd
            def _(pool):
                for step in ORDER:
                    kind, j, *w = step
                    if step in VAR:
                        pool.wait_ge(var_ready, VAR[step])
                        nc.gpsimd.tensor_tensor(rstd[j][:, :], var[j][:, :], neg_half[:, :], ALU.pow)\
                            .then_inc(rstd_ready, 1)
                    elif kind == "qk_split":
                        m, = w
                        n = QK[step] - 1
                        pool.wait_ge(mid_ready, n + 1)
                        nc.gpsimd.tensor_tensor(parts[j][m][:, LO, :], rest[n % 2][0:KC, :], parts[j][m][:, MID, :],
                                                ALU.subtract).then_inc(lo_ready, 1)
                    elif kind == "rotate":
                        m, = w
                        pool.wait_ge(swapped[j][m % RROT], 32 * (m // RROT + 1))
                        nc.gpsimd.tensor_tensor(swap[j][m % RROT], swap[j][m % RROT], rope[:, 1, :], ALU.mult)\
                            .then_inc(sin_ready, 1)

          nc.all_engine_barrier(sems_to_clear=range(sems[0].num, sems[-1].num + 1))


def experts(nc, a, region, ident, moe_in_d, res_d, logit_d, pair_y_d, out):
    es = ExitStack()
    with es:
        def sb(name, shape, dt=F32):
            return es.enter_context(nc.sbuf_tensor("x_" + name, shape, dt))

        def sem(name):
            return es.enter_context(nc.semaphore("ex_" + name))

        logit = sb("logit", [P, NT, E])
        res = sb("res", [P, NT, C])
        before32, before = sb("before32", [P, P]), sb("before", [P, P], BF16)
        ones = sb("ones", [P, P], BF16)
        counts = sb("counts", [P, N_CNT])
        top = sb("top", [P, NT, 8])
        top_i = sb("top_i", [P, NT, 8], U32)
        top_f = sb("top_f", [P, NT, TOPK])
        gap = sb("gap", [P, NT])
        share = [sb(f"share{k}", [P, NT]) for k in range(TOPK)]
        hot = [sb(f"hot{k}", [P, NT, E]) for k in range(TOPK)]
        hot_sum = sb("hot_sum", [P, NT, E], BF16)
        total, upto = sb("total", [P, E, NT]), sb("upto", [P, E, NT])
        pos, picked = sb("pos", [P, NT, E]), sb("picked", [P, NT, E])
        over = sb("over", [P, E, WMAX])
        n_tiles, end, base = sb("n_tiles", [P, E]), sb("end", [P, E]), sb("base", [P, E])
        passed, who = sb("passed", [1, NST, E]), sb("who", [1, NST])
        who_i = sb("who_i", [1, NST], I32)
        pair_no = sb("pair_no", [P, TOPK, NT, 2])
        spare = sb("spare", [ST, NST + 1])
        slot = sb("slot", [P, NT])
        slot_i, lane_i = sb("slot_i", [P, NT], I32), sb("lane_i", [P, NT], I32)
        row_of = sb("row_of", [P, NT])
        lane_of = sb("lane_of", [P, NT])
        in_lane = [sb(f"in_lane{k}", [P, NT, ST], BF16) for k in range(TOPK)]
        in_row = sb("in_row", [P, NT, NST])
        pair_in_row = [sb(f"pair_in_row{k}", [P, NT, 2, NST], BF16) for k in range(TOPK)]
        digits = sb("digits", [ST, 2, NST])
        taken_by = sb("taken_by", [ST, NST])
        unused = sb("unused", [ST, NST])
        second = sb("second", [ST, NST])
        to_row, from_row = sb("to_row", [ST, NST]), sb("from_row", [ST, NST])
        to_row_i, from_row_i = sb("to_row_i", [ST, NST], I32), sb("from_row_i", [ST, NST], I32)
        w_gu = [sb(f"w_gu{i}", [KC, NK, 2 * FF]) for i in range(RX)]
        w_dn = [sb(f"w_dn{i}", [ST, MF, C]) for i in range(RX)]
        x_t = [sb(f"x_t{i}", [ST, C]) for i in range(RX)]
        xT = [sb(f"xT{i}", [KC, NK, ST]) for i in range(2)]
        act_g = [sb(f"act_g{i}", [ST, MF, ST]) for i in range(2)]
        hidden = [sb(f"hidden{i}", [ST, MF, ST]) for i in range(2)]
        y_t = [sb(f"y_t{i}", [ST, C]) for i in range(RX)]
        y_in = sb("y_in", [P, TOPK, NT, C])

        logit_in, res_in, tables_in = sem("logit_in"), sem("res_in"), sem("tables_in")
        dve_self = sem("dve_self")
        gap_ready, share_exp = sem("gap_ready"), sem("share_exp")
        hot_ready, prefix_ready = sem("hot_ready"), sem("prefix_ready")
        prefix_read, who_ready = sem("prefix_read"), sem("who_ready")
        marks_ready, pairs_found, rows_known = sem("marks_ready"), sem("pairs_found"), sem("rows_known")
        y_back = [sem(f"y_back{b}") for b in range(B)]
        gu_in = [sem(f"gu_in{i}") for i in range(RX)]
        dn_in = [sem(f"dn_in{i}") for i in range(RX)]
        x_in = [sem(f"x_in{i}") for i in range(RX)]
        x_turned, xT_ready = sem("x_turned"), sem("xT_ready")
        gu_done, g_ready, h_ready = sem("gu_done"), sem("g_ready"), sem("h_ready")
        y_done, y_ready = sem("y_done"), sem("y_ready")
        y_out = [sem(f"y_out{i}") for i in range(RX)]
        combined, stored = sem("combined"), sem("stored")

        c0 = 0
        lanes, number = counts[:, c0:c0 + ST], counts[:, c0:c0 + E]
        c0 += ST
        thresholds = counts[:, c0:c0 + WMAX]
        c0 += WMAX
        tile_no = counts[:, c0:c0 + NST]
        c0 += NST
        restart = counts[:, c0:c0 + E * NT]
        c0 += E * NT
        no_restart = counts[:, c0:c0 + E]
        def third(m, up):
            at = 512 * (m % 2) + up * ST
            return region[1 + m // 2][:, at:at + ST]

        OUT_LAG = RX + 1
        LAST = NST // RX - 1
        assert NST % RX == 0

        with nc.Block() as block:
            @block.sync
            def _(sp):
                def load(n, s, before=None):
                    e = sp.value_load(who_i[0:1, bass.ds(n, 1)], min_val=0, max_val=E - 1)
                    if before is not None:
                        sp.wait_ge(gu_done, before * MF + MF)
                    sp.dma_start(w_gu[s][:, :, :], a["w_gate_up"][bass.ds(e, 1)]
                                 .rearrange("e (k p) n -> p (e k) n", p=KC)).then_inc(gu_in[s], 16)
                    if before is not None:
                        sp.wait_ge(y_done, before + 1)
                    sp.dma_start(w_dn[s][:, :, :], a["w_down"][bass.ds(e, 1)]
                                 .rearrange("e (k p) n -> p (e k) n", p=ST)).then_inc(dn_in[s], 16)

                sp.dma_start(logit[:, :, :], logit_d.rearrange("t p e -> p t e")).then_inc(logit_in, 16)
                sp.wait_ge(who_ready, 1)
                for s in range(RX):
                    load(s, s)
                with sp.Fori(1, LAST + 1) as it:
                    for s in range(RX):
                        load(it * RX + s, s, before=it * RX + (s - RX))
                for s in range(RX):
                    sp.wait_ge(y_out[s], 16 * (LAST + 1))
                for b in range(B):
                    for k in range(TOPK):
                        first = k * NTOK + b * KEEP
                        sp.dma_start(y_in[:, k, b * T:(b + 1) * T, :], pair_y_d[first:first + KEEP, :]
                                     .rearrange("(t p) c -> p t c", p=P)).then_inc(y_back[b], 16)
                for b in range(B):
                    sp.wait_ge(combined, b + 1)
                    sp.dma_start(out[b].rearrange("(t p) c -> p t c", p=P),
                                 res[:, b * T:(b + 1) * T, :]).then_inc(stored, 16)
                sp.wait_ge(stored, 16 * B)

            @block.scalar
            def _(act):
                act.dma_start(before32[:, :], a["before"]).then_inc(tables_in, 16)
                act.dma_start(counts[:, :], a["counts"].broadcast_to([P, N_CNT])).then_inc(tables_in, 16)
                act.dma_start(pair_no[:, :, :, :], a["pair_no"]).then_inc(tables_in, 16)
                act.dma_start(spare[:, :], a["spare"]).then_inc(tables_in, 16)
                act.dma_start(res[:, :, :], res_d.rearrange("t p c -> p t c")).then_inc(res_in, 16)
                act.wait_ge(gap_ready, 1)
                nc.scalar.activation(share[1][:, :], gap[:, :], ACT.Exp).then_inc(share_exp, 1)

                def gates(n, s):
                    for m in range(MF):
                        act.wait_ge(gu_done, n * MF + (m + 1))
                        nc.scalar.activation(act_g[s % 2][:, m, :], third(m, 0), ACT.Silu)\
                            .then_inc(g_ready, 1)

                def take_y(n, s, turn, first=False):
                    act.wait_ge(y_done, n + 1)
                    if not first:
                        act.wait_ge(y_out[s], turn * 16)
                    o = 512 * (s % 2)
                    nc.scalar.copy(y_t[s][:, :], region[3][:, o:o + C]).then_inc(y_ready, 1)

                gates(0, 0)
                for s in range(RX):
                    gates(s + 1, s + 1)
                    take_y(s, s, 0, first=True)
                with act.Fori(1, LAST) as it:
                    for s in range(RX):
                        gates(it * RX + (1 + s), s + 1)
                        take_y(it * RX + s, s, it)
                for s in range(RX):
                    if s < RX - 1:
                        gates(NST - RX + s + 1, s + 1)
                    take_y(NST - RX + s, s, LAST)

            @block.vector
            def _(dve):
                link = chain(dve, dve_self)
                dve.wait_ge(logit_in, 16)
                for t in range(NT):
                    link(nc.vector.max(top[:, t, :], logit[:, t, :]), wait=t == NT - 1)
                for t in range(NT):
                    link(nc.vector.max_index(top_i[:, t, :], top[:, t, :], logit[:, t, :]), wait=t == NT - 1)
                nc.vector.tensor_tensor(gap[:, :], top[:, :, 1], top[:, :, 0], ALU.subtract).then_inc(gap_ready, 1)
                link(nc.vector.tensor_copy(top_f[:, :, :], top_i[:, :, 0:TOPK]))
                dve.wait_ge(tables_in, 64)
                link(nc.vector.tensor_copy(before[:, :], before32[:, :]), wait=False)
                link(nc.vector.memset(ones[:, :], 1.0), wait=False)
                for k in range(TOPK):
                    link(nc.vector.tensor_tensor(hot[k][:, :, :], number.unsqueeze(1).broadcast_to([P, NT, E]),
                                                 top_f[:, :, k:k + 1].broadcast_to([P, NT, E]), ALU.is_equal))
                nc.vector.tensor_tensor(hot_sum[:, :, :], hot[0][:, :, :], hot[1][:, :, :], ALU.add)\
                    .then_inc(hot_ready, 1)
                dve.wait_ge(share_exp, 1)
                link(nc.vector.tensor_scalar(gap[:, :], share[1][:, :], 1.0, None, ALU.add))
                link(nc.vector.reciprocal(share[0][:, :], gap[:, :]))
                link(nc.vector.tensor_tensor(share[1][:, :], share[1][:, :], share[0][:, :], ALU.mult))
                dve.wait_ge(prefix_ready, 1)
                by_tile = lambda r: r[0:P, 0:NT * E].rearrange("p (t e) -> p t e", e=E)
                link(nc.vector.tensor_copy(total[:, :, :].rearrange("p e t -> p t e"), by_tile(region[1])))
                link(nc.vector.tensor_tensor_scan(upto[:, :, :].rearrange("p e t -> p (e t)"), restart,
                                                  total[:, :, :].rearrange("p e t -> p (e t)"), 0.0, ALU.mult, ALU.add))
                link(nc.vector.tensor_tensor(over[:, :, :], upto[:, :, NT - 1:NT].broadcast_to([P, E, WMAX]),
                                             thresholds.unsqueeze(1).broadcast_to([P, E, WMAX]), ALU.is_gt))
                link(nc.vector.tensor_reduce(n_tiles[:, :], over[:, :, :], AX.X, ALU.add))
                link(nc.vector.tensor_tensor_scan(end[:, :], no_restart, n_tiles[:, :], 0.0, ALU.mult, ALU.add))
                link(nc.vector.tensor_tensor(base[:, :], end[:, :], n_tiles[:, :], ALU.subtract))
                link(nc.vector.tensor_scalar(base[:, :], base[:, :], float(ST), None, ALU.mult))
                link(nc.vector.tensor_tensor(passed[:, :, :], tile_no[0:1, :].unsqueeze(2).broadcast_to([1, NST, E]),
                                             end[0:1, :].unsqueeze(1).broadcast_to([1, NST, E]), ALU.is_ge))
                link(nc.vector.tensor_reduce(who[:, :], passed[:, :, :], AX.X, ALU.add))
                link(nc.vector.tensor_scalar(who[:, :], who[:, :], float(E - 1), None, ALU.min))
                nc.vector.tensor_copy(who_i[:, :], who[:, :]).then_inc(who_ready, 1)
                link(nc.vector.tensor_tensor(upto[:, :, :], upto[:, :, :], total[:, :, :], ALU.subtract))
                link(nc.vector.tensor_tensor(pos[:, :, :], by_tile(region[0]),
                                             upto[:, :, :].rearrange("p e t -> p t e"), ALU.add))
                link(nc.vector.tensor_tensor(pos[:, :, :], pos[:, :, :],
                                             base[:, :].unsqueeze(1).broadcast_to([P, NT, E]), ALU.add))
                nc.vector.engine_nop().then_inc(prefix_read, 1)
                for k in range(TOPK):
                    link(nc.vector.tensor_tensor(picked[:, :, :], hot[k][:, :, :], pos[:, :, :], ALU.mult))
                    link(nc.vector.tensor_reduce(slot[:, :], picked[:, :, :], AX.X, ALU.add))
                    link(nc.vector.tensor_copy(slot_i[:, :], slot[:, :]))
                    link(nc.vector.tensor_scalar(lane_i[:, :], slot_i[:, :], ST - 1, None, ALU.bitwise_and))
                    link(nc.vector.tensor_copy(lane_of[:, :], lane_i[:, :]))
                    link(nc.vector.tensor_tensor(row_of[:, :], slot[:, :], lane_of[:, :], ALU.subtract))
                    link(nc.vector.tensor_scalar(row_of[:, :], row_of[:, :], 1.0 / ST, None, ALU.mult))
                    link(nc.vector.tensor_tensor(in_lane[k][:, :, :], lanes.unsqueeze(1).broadcast_to([P, NT, ST]),
                                                 lane_of[:, :].unsqueeze(2).broadcast_to([P, NT, ST]), ALU.is_equal),
                         wait=False)
                    link(nc.vector.tensor_tensor(in_row[:, :, :], tile_no.unsqueeze(1).broadcast_to([P, NT, NST]),
                                                 row_of[:, :].unsqueeze(2).broadcast_to([P, NT, NST]), ALU.is_equal))
                    nc.vector.tensor_tensor(pair_in_row[k][:, :, :, :],
                                            in_row[:, :, :].unsqueeze(2).broadcast_to([P, NT, 2, NST]),
                                            pair_no[:, k, :, :].unsqueeze(3).broadcast_to([P, NT, 2, NST]), ALU.mult)\
                        .then_inc(marks_ready, 1)
                    dve.wait_ge(marks_ready, k + 1)
                dve.wait_ge(pairs_found, 1)
                link(nc.vector.tensor_copy(digits[:, :, :], region[2][:, 0:2 * NST].rearrange("p (d n) -> p d n", d=2)))
                link(nc.vector.scalar_tensor_tensor(out=taken_by[:, :], in0=digits[:, 0, :], scalar=64.0,
                                                    in1=digits[:, 1, :], op0=ALU.mult, op1=ALU.add))
                for out_row, own in ((to_row, spare[:, 0:NST]), (from_row, spare[:, NST:].broadcast_to([ST, NST]))):
                    link(nc.vector.scalar_tensor_tensor(out=unused[:, :], in0=taken_by[:, :], scalar=0.0, in1=own,
                                                        op0=ALU.is_equal, op1=ALU.mult))
                    link(nc.vector.scalar_tensor_tensor(out=out_row[:, :], in0=taken_by[:, :], scalar=-1.0,
                                                        in1=unused[:, :], op0=ALU.add, op1=ALU.add))
                link(nc.vector.tensor_scalar(second[:, :], taken_by[:, :], float(NTOK), -float(NTOK),
                                             ALU.is_gt, ALU.mult))
                link(nc.vector.tensor_tensor(from_row[:, :], from_row[:, :], second[:, :], ALU.add))
                nc.vector.tensor_copy(from_row_i[:, :], from_row[:, :]).then_inc(rows_known, 1)
                nc.vector.tensor_copy(to_row_i[:, :], to_row[:, :]).then_inc(rows_known, 1)

                def take_x(n, s):
                    dve.wait_ge(x_turned, n + 1)
                    o = 512 * (s % 2)
                    nc.vector.tensor_copy(xT[s % 2][:, :, :], region[0][0:KC, o:o + NK * ST]
                                          .rearrange("p (k n) -> p k n", k=NK)).then_inc(xT_ready, 1)

                def products(n, s):
                    for m in range(MF):
                        dve.wait_ge(g_ready, n * MF + (m + 1))
                        nc.vector.tensor_tensor(hidden[s % 2][:, m, :], third(m, 1), act_g[s % 2][:, m, :],
                                                ALU.mult).then_inc(h_ready, 1)

                take_x(0, 0)
                take_x(1, 1)
                products(0, 0)
                with dve.Fori(0, LAST) as it:
                    for s in range(RX):
                        take_x(it * RX + (2 + s), s)
                        products(it * RX + (1 + s), s + 1)
                for s in range(RX - 1):
                    if s < RX - 2:
                        take_x(NST - RX + 2 + s, s)
                    products(NST - RX + 1 + s, s + 1)
                dve.wait_ge(res_in, 16)
                for b in range(B):
                    dve.wait_ge(y_back[b], 16 * TOPK)
                    for k in range(TOPK):
                        for t in range(b * T, (b + 1) * T):
                            ins = nc.vector.scalar_tensor_tensor(
                                out=res[:, t, :], in0=y_in[:, k, t, :], scalar=share[k][:, t:t + 1],
                                in1=res[:, t, :], op0=ALU.mult, op1=ALU.add)
                            if k == 0:
                                link(ins, wait=t == (b + 1) * T - 1)
                    ins.then_inc(combined, 1)

            @block.tensor
            def _(pe):
                pe.wait_ge(hot_ready, 1)
                pairs_in = hot_sum[:, :, :].rearrange("p t e -> p (t e)")
                nc.tensor.matmul(region[0][0:P, 0:NT * E], before[:, :], pairs_in, start=True, stop=True)
                nc.tensor.matmul(region[1][0:P, 0:NT * E], ones[:, :], pairs_in, start=True, stop=True)\
                    .then_inc(prefix_ready, 1)
                for k in range(TOPK):
                    pe.wait_ge(marks_ready, k + 1)
                    for t in range(NT):
                        ins = nc.tensor.matmul(region[2][:, 0:2 * NST], in_lane[k][:, t, :],
                                               pair_in_row[k][:, t, :, :].rearrange("p d n -> p (d n)"),
                                               start=(k == t == 0), stop=(k == TOPK - 1 and t == NT - 1))
                ins.then_inc(pairs_found, 1)
                pe.wait_ge(prefix_read, 1)
                pe.wait_ge(rows_known, 1)

                def turn_x(n, s, turn):
                    pe.wait_ge(x_in[s], turn * 16 + 16)
                    for k in range(NK):
                        o = 512 * (s % 2) + k * ST
                        ins = nc.tensor.transpose(region[0][0:KC, o:o + ST],
                                                  x_t[s][:, k * KC:(k + 1) * KC], ident[:, :])
                    ins.then_inc(x_turned, 1)

                def gate_up(n, s, turn, first=False):
                    pe.wait_ge(xT_ready, n + 1)
                    pe.wait_ge(gu_in[s], turn * 16 + 16)
                    for m in range(MF):
                        if not first:
                            pe.wait_ge(h_ready, n * MF + (m + 1 - MF))
                        for up, o in enumerate((0, FF)):
                            for k in range(NK):
                                ins = nc.tensor.matmul(third(m, up),
                                                       w_gu[s][:, k, o + m * ST:o + (m + 1) * ST], xT[s % 2][:, k, :],
                                                       start=(k == 0), stop=(k == NK - 1))
                        ins.then_inc(gu_done, 1)

                def down(n, s, turn, first=False):
                    pe.wait_ge(dn_in[s], turn * 16 + 16)
                    pe.wait_ge(h_ready, n * MF + MF)
                    if not first:
                        pe.wait_ge(y_ready, n - 1)
                    o = 512 * (s % 2)
                    for m in range(MF):
                        ins = nc.tensor.matmul(region[3][:, o:o + C], hidden[s % 2][:, m, :], w_dn[s][:, m, :],
                                               start=(m == 0), stop=(m == MF - 1))
                    ins.then_inc(y_done, 1)

                def tile_step(it, s, first=False, last=False):
                    n, after = it * RX + s, lambda d: (s + d) % RX
                    wrap = lambda d: it + (s + d) // RX
                    if not (last and s + 2 >= RX):
                        turn_x(n + 2, after(2), wrap(2))
                    if not (last and s + 1 >= RX):
                        gate_up(n + 1, after(1), wrap(1))
                    down(n, s, it, first=first and s < 2)

                turn_x(0, 0, 0)
                turn_x(1, 1, 0)
                gate_up(0, 0, 0, first=True)
                for s in range(RX):
                    tile_step(0, s, first=True)
                with pe.Fori(1, LAST) as it:
                    for s in range(RX):
                        tile_step(it, s)
                for s in range(RX):
                    tile_step(LAST, s, last=True)

            @block.gpsimd
            def _(pool):
                pool.wait_ge(rows_known, 2)
                for n in range(NST + OUT_LAG):
                    s = n % RX
                    if n < NST:
                        if n >= RX:
                            pool.wait_ge(x_turned, n - RX + 1)
                        nc.gpsimd.indirect_dma_start(
                            x_t[s][:, :], None, moe_in_d,
                            bass.IndirectOffsetOnAxis(ap=from_row_i[:, n:n + 1], axis=0)).then_inc(x_in[s], 16)
                    if n >= OUT_LAG:
                        m = n - OUT_LAG
                        pool.wait_ge(y_ready, m + 1)
                        nc.gpsimd.indirect_dma_start(
                            pair_y_d, bass.IndirectOffsetOnAxis(ap=to_row_i[:, m:m + 1], axis=0),
                            y_t[m % RX][:, :], None).then_inc(y_out[m % RX], 16)


def lay_out(x, L0_tok_w, L0_tok_b, L0_attn_w_qkv, L0_attn_b_qkv, L0_attn_w_proj, L0_attn_b_proj, L0_ffn_norm1_w,
            L0_ffn_w_qkv, L0_ffn_w_out, L0_ffn_norm2_w, L0_ffn_w_router, L0_ffn_w_gate_up, L0_ffn_w_down):
    r = {"x": x, "tok_w": L0_tok_w.reshape(1, C), "tok_b": L0_tok_b.reshape(1, 1)}
    r["w_qkv1"] = L0_attn_w_qkv.T
    r["b_qk1"] = L0_attn_b_qkv[:2 * C].reshape(2 * NK, KC).T
    r["b_v1"] = L0_attn_b_qkv[2 * C:].reshape(1, C)
    r["w_proj1"] = L0_attn_w_proj.T
    r["b_proj1"] = L0_attn_b_proj.reshape(1, C)
    r["norm1"] = L0_ffn_norm1_w.reshape(NK, KC).T
    r["norm2_row"] = L0_ffn_norm2_w.reshape(1, C)
    w = L0_ffn_w_qkv
    nq, nk = H2 * D2, HKV * D2
    q = w[:, :nq].reshape(C, NPAIR, 2, HALF, 2).transpose(0, 1, 4, 2, 3).reshape(C, nq)
    k = w[:, nq:nq + nk].reshape(C, HKV, HALF, 2).transpose(0, 1, 3, 2).reshape(C, HKV, 2, 1, HALF)
    k = np.broadcast_to(k, (C, HKV, 2, 2, HALF)).reshape(C, 2 * nk)
    r["w_qkv2"] = np.concatenate([q, k, w[:, nq + nk:]], axis=1)
    r["w_out2"] = L0_ffn_w_out
    r["w_router"] = L0_ffn_w_router
    r["w_gate_up"] = L0_ffn_w_gate_up
    r["w_down"] = L0_ffn_w_down
    r.update(constants())
    return {n: np.ascontiguousarray(v) for n, v in r.items()}


def kernel(**inputs):
    import concourse.bacc as bacc
    from concourse.bass_utils import run_bass_kernel_spmd

    nc = bacc.Bacc("TRN2", target_bir_lowering=False, num_devices=1)
    arrays, aps = {}, {}
    for name, v in lay_out(**{n: np.asarray(v) for n, v in inputs.items()}).items():
        arrays[f"in_{name}"] = v
        aps[name] = nc.dram_tensor(f"in_{name}", v.shape, mybir.dt.from_np(v.dtype), kind="ExternalInput").ap()
    out = nc.dram_tensor("out", [B, KEEP, C], F32, kind="ExternalOutput").ap()
    audio_tower(nc, aps, out)
    r = run_bass_kernel_spmd(nc, [arrays], core_ids=[0])
    return r.results[0]["out"]
```
